# Optimizing a Trainium2 kernel written in Bass

```python
import numpy as np
import jax
import jax.numpy as jnp

def _softmax(x, axis=-1):
    return jax.nn.softmax(x, axis=axis)

def _gelu(x):
    return jax.nn.gelu(x, approximate=True)

def _silu(x):
    return jax.nn.silu(x)

def _sigmoid(x):
    return jax.nn.sigmoid(x)

def _layernorm(x, axis=-1, eps=1e-05):
    m = jnp.mean(x, axis=axis, keepdims=True)
    v = jnp.var(x, axis=axis, keepdims=True)
    return (x - m) / jnp.sqrt(v + eps)

def _scatter_add(tgt, idx, src, axis=0):
    return tgt.at[idx].add(src)

def _segment_sum(src, seg, n):
    return jax.ops.segment_sum(src, seg, n)
kernel_name = 'mk_adaln_d2_jaxref_r4_72da56'

def setup_inputs(seed: int=0):
    np.random.seed(seed)
    _w = jnp.asarray

    def _L0_attn_setup():
        import jax, jax.numpy as jnp
        import numpy as np
        import math
        DIM = 256
        HEADS = 8
        DIM_HEAD = 64
        SEQ = 2048
        BATCH = 2
        WINDOW = 64
        NQ = 256
        NKV = 256
        FETCH_K_RATIO = 9.0 / 8.0
        N_ITERS = 20
        EPS = 0.03
        EPS_INIT = 4.0
        EPS_DECAY = 0.7
        HDIM = HEADS * DIM_HEAD

        def _layernorm(x, g, b, eps=1e-05):
            mu = x.mean(-1, keepdims=True)
            var = ((x - mu) ** 2).mean(-1, keepdims=True)
            return (x - mu) * jax.lax.rsqrt(var + eps) * g + b

        def _rmsnorm(x, gamma):
            normed = x / jnp.maximum(jnp.linalg.norm(x, axis=-1, keepdims=True), 1e-12)
            return normed * x.shape[-1] ** 0.5 * gamma

        def _rotate_half(x):
            x1, x2 = jnp.split(x, 2, axis=-1)
            return jnp.concatenate([-x2, x1], axis=-1)

        def _apply_rope(pos, t):
            return t * jnp.cos(pos) + _rotate_half(t) * jnp.sin(pos)

        def _coor_descent(s, k):
            logk = math.log(max(k, 1e-20))
            b = -s
            a = jnp.zeros_like(s[..., :1])
            cur = max(EPS_INIT, EPS)
            for _ in range(N_ITERS):
                sb = (s + b) / cur
                a = cur * (logk - jax.nn.logsumexp(sb, axis=-1, keepdims=True))
                b = -jax.nn.relu(s + a)
                cur = max(cur * EPS_DECAY, EPS)
            return jnp.exp((s + a + b) / cur)

        def _route(x, tok, num_tokens):
            s = jnp.einsum('bnd,d->bn', x, tok)
            eff_k = min(num_tokens * FETCH_K_RATIO, x.shape[1])
            scores = _coor_descent(s, eff_k)
            sel_scores, sel_idx = jax.lax.top_k(scores, num_tokens)
            sel_scores = sel_scores + jax.lax.stop_gradient(1.0 - sel_scores)
            routed = jnp.take_along_axis(x, sel_idx[..., None], axis=1)
            return (sel_idx, sel_scores, routed)

        def _light_attn(x, ln_g, ln_b, qkv_w, out_w):
            b, n, d = x.shape
            h, dh, w = (HEADS, DIM_HEAD, WINDOW)
            nw = n // w
            xn = _layernorm(x, ln_g, ln_b)
            q, k, v = jnp.split(xn @ qkv_w, 3, axis=-1)
            to_heads = lambda t: t.reshape(b, n, h, dh).transpose(0, 2, 1, 3)
            q, k, v = (to_heads(q), to_heads(k), to_heads(v))
            bq = q.reshape(b, h, nw, w, dh) * dh ** (-0.5)

            def look_around(t):
                tp = jnp.pad(t.reshape(b, h, nw, w, dh), ((0, 0), (0, 0), (1, 1), (0, 0), (0, 0)))
                return jnp.concatenate([tp[:, :, i:nw + i] for i in range(3)], axis=3)
            bk, bv = (look_around(k), look_around(v))
            sim = jnp.einsum('bhwid,bhwjd->bhwij', bq, bk)
            t_q = jnp.arange(n).reshape(nw, w)
            tpad = jnp.pad(t_q, ((1, 1), (0, 0)), constant_values=-1)
            t_k = jnp.concatenate([tpad[i:nw + i] for i in range(3)], axis=-1)
            valid = (t_k >= 0)[:, None, :] & (jnp.abs(t_q[:, :, None] - t_k[:, None, :]) <= w)
            sim = jnp.where(valid[None, None], sim, -jnp.finfo(sim.dtype).max)
            attn = jax.nn.softmax(sim, axis=-1)
            out = jnp.einsum('bhwij,bhwjd->bhwid', attn, bv)
            out = out.reshape(b, h, n, dh).transpose(0, 2, 1, 3).reshape(b, n, h * dh)
            return out @ out_w

        def _heavy_attn(xq, ctx, scores_kv, gamma, q_w, kv_w, null_kv, out_w, rope_q, rope_k):
            b = xq.shape[0]
            h, dh = (HEADS, DIM_HEAD)
            xq = _rmsnorm(xq, gamma)
            ctx = _rmsnorm(ctx, gamma)
            q = (xq @ q_w).reshape(b, -1, h, dh).transpose(0, 2, 1, 3)
            kv = jnp.einsum('hdi,bni->bhnd', kv_w, ctx)
            k, v = (kv[..., :dh], kv[..., dh:])
            v = v * scores_kv[:, None, :, None]
            q = _apply_rope(rope_q[:, None], q)
            k = _apply_rope(rope_k[:, None], k)
            nk = jnp.broadcast_to(null_kv[0][None, :, None, :], (b, h, 1, dh))
            nv = jnp.broadcast_to(null_kv[1][None, :, None, :], (b, h, 1, dh))
            k = jnp.concatenate([nk, k], axis=2)
            v = jnp.concatenate([nv, v], axis=2)
            sim = jnp.einsum('bhid,bhjd->bhij', q, k) * dh ** (-0.5)
            attn = jax.nn.softmax(sim, axis=-1)
            out = jnp.einsum('bhij,bhjd->bhid', attn, v)
            out = out.transpose(0, 2, 1, 3).reshape(b, -1, h * dh)
            return out @ out_w

        def _forward(x, ln_gamma, ln_beta, light_qkv_w, light_out_w, q_route_tok, kv_route_tok, heavy_gamma, heavy_q_w, heavy_kv_w, heavy_null_kv, heavy_out_w, null_q_token):
            b, n, d = x.shape
            light_out = _light_attn(x, ln_gamma, ln_beta, light_qkv_w, light_out_w)
            idx_q, sc_q, rt_q = _route(x, q_route_tok, NQ)
            idx_kv, sc_kv, rt_kv = _route(x, kv_route_tok, NKV)
            inv_freq = 1.0 / 10000.0 ** (jnp.arange(0, DIM_HEAD, 2, dtype=jnp.float32) / DIM_HEAD)
            freqs = jnp.arange(n, dtype=jnp.float32)[:, None] * inv_freq[None]
            pos = jnp.concatenate([freqs, freqs], axis=-1)
            rope_q = pos[idx_q]
            rope_k = pos[idx_kv]
            heavy_out = _heavy_attn(rt_q, rt_kv, sc_kv, heavy_gamma, heavy_q_w, heavy_kv_w, heavy_null_kv, heavy_out_w, rope_q, rope_k)
            heavy_out = heavy_out * sc_q[..., None]
            out = jnp.broadcast_to(null_q_token, x.shape)
            out = out.at[jnp.arange(b)[:, None], idx_q].set(heavy_out)
            return light_out + out
        ks = jax.random.split(jax.random.key(seed), 10)
        d = DIM
        return {'x': jax.random.normal(ks[0], (BATCH, SEQ, d), jnp.float32), 'ln_gamma': jnp.ones((d,), jnp.float32), 'ln_beta': jnp.zeros((d,), jnp.float32), 'light_qkv_w': jax.random.normal(ks[1], (d, 3 * HDIM), jnp.float32) * 0.02, 'light_out_w': jax.random.normal(ks[2], (HDIM, d), jnp.float32) * 0.02, 'q_route_tok': jax.random.normal(ks[3], (d,), jnp.float32), 'kv_route_tok': jax.random.normal(ks[4], (d,), jnp.float32), 'heavy_gamma': jnp.ones((d,), jnp.float32), 'heavy_q_w': jax.random.normal(ks[5], (d, HDIM), jnp.float32) * 0.02, 'heavy_kv_w': jax.random.normal(ks[6], (HEADS, 2 * DIM_HEAD, d), jnp.float32) * 0.02, 'heavy_null_kv': jax.random.normal(ks[7], (2, HEADS, DIM_HEAD), jnp.float32), 'heavy_out_w': jax.random.normal(ks[8], (HDIM, d), jnp.float32) * 0.02, 'null_q_token': jax.random.normal(ks[9], (d,), jnp.float32)}
    _L0_attn_in = _L0_attn_setup()

    def _L0_ffn_setup():
        import jax, jax.numpy as jnp
        import numpy as np
        D_MODEL = 256
        M = 64
        INNER = 16
        key = jax.random.key(seed)
        ks = jax.random.split(key, 9)

        def init(k, shape, fan_in):
            bound = 1.0 / np.sqrt(fan_in)
            return jax.random.uniform(k, shape, jnp.float32, -bound, bound)
        x = jax.random.normal(ks[0], (16, 1024, D_MODEL), dtype=jnp.float32)
        Win = init(ks[1], (D_MODEL, M), D_MODEL)
        bin_ = init(ks[2], (M,), D_MODEL)
        W1 = init(ks[3], (M, INNER), 1)
        b1 = init(ks[4], (M, INNER), 1)
        W2 = init(ks[5], (M, INNER), INNER)
        b2 = init(ks[6], (M,), INNER)
        Wout = init(ks[7], (M, D_MODEL), M)
        bout = init(ks[8], (D_MODEL,), M)
        return {'x': x, 'Win': Win, 'bin_': bin_, 'W1': W1, 'b1': b1, 'W2': W2, 'b2': b2, 'Wout': Wout, 'bout': bout}
    _L0_ffn_in = _L0_ffn_setup()
    _L0_c = _w((lambda *s: np.random.randn(*s).astype(np.float32) * 0.05)(8, 256))
    _L0_wmod = _w((lambda *s: np.random.randn(*s).astype(np.float32) * 0.05)(256, 6 * 256) * 256 ** (-0.5))

    def _L1_attn_setup():
        import math
        import jax, jax.numpy as jnp
        import numpy as np
        DIM = 256
        N_HEADS = 16
        HEAD_DIM = DIM // N_HEADS
        SEQ_LEN = 512
        BASE = 10000.0
        EPS = 1e-05

        def rope_cache(seq_len, dim):
            pos = jnp.arange(seq_len, dtype=jnp.float32)[:, None]
            di = jnp.arange(0, dim, 2, dtype=jnp.float32) / dim
            theta = pos * jnp.exp(-di * math.log(BASE))
            cos = jnp.repeat(jnp.cos(theta), 2, axis=1)
            sin = jnp.repeat(jnp.sin(theta), 2, axis=1)
            return (cos, sin)

        def rotate_half(x):
            x1 = x[..., ::2]
            x2 = x[..., 1::2]
            return jnp.concatenate((-x2, x1), axis=-1)

        def layernorm(x, gamma, beta):
            mu = jnp.mean(x, axis=-1, keepdims=True)
            var = jnp.var(x, axis=-1, keepdims=True)
            return (x - mu) * jax.lax.rsqrt(var + EPS) * gamma + beta
        key = jax.random.key(seed)
        ks = jax.random.split(key, 7)
        s = 1.0 / math.sqrt(DIM)
        return {'x': jax.random.normal(ks[0], (2, SEQ_LEN, DIM), dtype=jnp.float32), 'Wq': jax.random.normal(ks[1], (DIM, DIM), dtype=jnp.float32) * s, 'Wk': jax.random.normal(ks[2], (DIM, DIM), dtype=jnp.float32) * s, 'Wv': jax.random.normal(ks[3], (DIM, DIM), dtype=jnp.float32) * s, 'q_gamma': jnp.ones((HEAD_DIM,), jnp.float32), 'q_beta': jnp.zeros((HEAD_DIM,), jnp.float32), 'k_gamma': jnp.ones((HEAD_DIM,), jnp.float32), 'k_beta': jnp.zeros((HEAD_DIM,), jnp.float32), 'Wo': jax.random.normal(ks[4], (DIM, DIM), dtype=jnp.float32) * s, 'bo': jnp.zeros((DIM,), jnp.float32)}
    _L1_attn_in = _L1_attn_setup()

    def _L1_ffn_setup():
        import jax, jax.numpy as jnp
        import numpy as np

        def _binarize(w):
            alpha = jax.lax.stop_gradient(jnp.mean(jnp.abs(w), axis=1, keepdims=True))
            bw = alpha * jnp.sign(w)
            return w + jax.lax.stop_gradient(bw - w)
        key = jax.random.key(seed)
        k1, k2, k3, k4, k5 = jax.random.split(key, 5)
        D, H = (256, 1024)
        x = jax.random.normal(k1, (64, 196, D), dtype=jnp.float32)
        w1 = jax.random.normal(k2, (H, D), dtype=jnp.float32) * 0.02
        b1 = jax.random.normal(k3, (H,), dtype=jnp.float32) * 0.02
        w2 = jax.random.normal(k4, (D, H), dtype=jnp.float32) * 0.02
        b2 = jax.random.normal(k5, (D,), dtype=jnp.float32) * 0.02
        return {'x': x, 'w1': w1, 'b1': b1, 'w2': w2, 'b2': b2}
    _L1_ffn_in = _L1_ffn_setup()
    _L1_c = _w((lambda *s: np.random.randn(*s).astype(np.float32) * 0.05)(8, 256))
    _L1_wmod = _w((lambda *s: np.random.randn(*s).astype(np.float32) * 0.05)(256, 6 * 256) * 256 ** (-0.5))
    _d = {'L0_attn_x': _L0_attn_in['x'], 'L0_attn_ln_gamma': _L0_attn_in['ln_gamma'], 'L0_attn_ln_beta': _L0_attn_in['ln_beta'], 'L0_attn_light_qkv_w': _L0_attn_in['light_qkv_w'], 'L0_attn_light_out_w': _L0_attn_in['light_out_w'], 'L0_attn_q_route_tok': _L0_attn_in['q_route_tok'], 'L0_attn_kv_route_tok': _L0_attn_in['kv_route_tok'], 'L0_attn_heavy_gamma': _L0_attn_in['heavy_gamma'], 'L0_attn_heavy_q_w': _L0_attn_in['heavy_q_w'], 'L0_attn_heavy_kv_w': _L0_attn_in['heavy_kv_w'], 'L0_attn_heavy_null_kv': _L0_attn_in['heavy_null_kv'], 'L0_attn_heavy_out_w': _L0_attn_in['heavy_out_w'], 'L0_attn_null_q_token': _L0_attn_in['null_q_token'], 'L0_ffn_Win': _L0_ffn_in['Win'], 'L0_ffn_bin_': _L0_ffn_in['bin_'], 'L0_ffn_W1': _L0_ffn_in['W1'], 'L0_ffn_b1': _L0_ffn_in['b1'], 'L0_ffn_W2': _L0_ffn_in['W2'], 'L0_ffn_b2': _L0_ffn_in['b2'], 'L0_ffn_Wout': _L0_ffn_in['Wout'], 'L0_ffn_bout': _L0_ffn_in['bout'], 'L0_c': _L0_c, 'L0_wmod': _L0_wmod, 'L1_attn_Wq': _L1_attn_in['Wq'], 'L1_attn_Wk': _L1_attn_in['Wk'], 'L1_attn_Wv': _L1_attn_in['Wv'], 'L1_attn_q_gamma': _L1_attn_in['q_gamma'], 'L1_attn_q_beta': _L1_attn_in['q_beta'], 'L1_attn_k_gamma': _L1_attn_in['k_gamma'], 'L1_attn_k_beta': _L1_attn_in['k_beta'], 'L1_attn_Wo': _L1_attn_in['Wo'], 'L1_attn_bo': _L1_attn_in['bo'], 'L1_ffn_w1': _L1_ffn_in['w1'], 'L1_ffn_b1': _L1_ffn_in['b1'], 'L1_ffn_w2': _L1_ffn_in['w2'], 'L1_ffn_b2': _L1_ffn_in['b2'], 'L1_c': _L1_c, 'L1_wmod': _L1_wmod}
    _x0 = _d['L0_attn_x']
    _d['L0_attn_x'] = jax.random.normal(jax.random.fold_in(jax.random.key(seed), 1), (8, 1024, 256), dtype=_x0.dtype)
    del _x0
    return _d

def reference(L0_attn_x, L0_attn_ln_gamma, L0_attn_ln_beta, L0_attn_light_qkv_w, L0_attn_light_out_w, L0_attn_q_route_tok, L0_attn_kv_route_tok, L0_attn_heavy_gamma, L0_attn_heavy_q_w, L0_attn_heavy_kv_w, L0_attn_heavy_null_kv, L0_attn_heavy_out_w, L0_attn_null_q_token, L0_ffn_Win, L0_ffn_bin_, L0_ffn_W1, L0_ffn_b1, L0_ffn_W2, L0_ffn_b2, L0_ffn_Wout, L0_ffn_bout, L0_c, L0_wmod, L1_attn_Wq, L1_attn_Wk, L1_attn_Wv, L1_attn_q_gamma, L1_attn_q_beta, L1_attn_k_gamma, L1_attn_k_beta, L1_attn_Wo, L1_attn_bo, L1_ffn_w1, L1_ffn_b1, L1_ffn_w2, L1_ffn_b2, L1_c, L1_wmod):

    def _L0_attn_ref(x, ln_gamma, ln_beta, light_qkv_w, light_out_w, q_route_tok, kv_route_tok, heavy_gamma, heavy_q_w, heavy_kv_w, heavy_null_kv, heavy_out_w, null_q_token):
        import jax, jax.numpy as jnp
        import numpy as np
        import math
        DIM = 256
        HEADS = 8
        DIM_HEAD = 64
        SEQ = 2048
        BATCH = 2
        WINDOW = 64
        NQ = 256
        NKV = 256
        FETCH_K_RATIO = 9.0 / 8.0
        N_ITERS = 20
        EPS = 0.03
        EPS_INIT = 4.0
        EPS_DECAY = 0.7
        HDIM = HEADS * DIM_HEAD

        def _layernorm(x, g, b, eps=1e-05):
            mu = x.mean(-1, keepdims=True)
            var = ((x - mu) ** 2).mean(-1, keepdims=True)
            return (x - mu) * jax.lax.rsqrt(var + eps) * g + b

        def _rmsnorm(x, gamma):
            normed = x / jnp.maximum(jnp.linalg.norm(x, axis=-1, keepdims=True), 1e-12)
            return normed * x.shape[-1] ** 0.5 * gamma

        def _rotate_half(x):
            x1, x2 = jnp.split(x, 2, axis=-1)
            return jnp.concatenate([-x2, x1], axis=-1)

        def _apply_rope(pos, t):
            return t * jnp.cos(pos) + _rotate_half(t) * jnp.sin(pos)

        def _coor_descent(s, k):
            logk = math.log(max(k, 1e-20))
            b = -s
            a = jnp.zeros_like(s[..., :1])
            cur = max(EPS_INIT, EPS)
            for _ in range(N_ITERS):
                sb = (s + b) / cur
                a = cur * (logk - jax.nn.logsumexp(sb, axis=-1, keepdims=True))
                b = -jax.nn.relu(s + a)
                cur = max(cur * EPS_DECAY, EPS)
            return jnp.exp((s + a + b) / cur)

        def _route(x, tok, num_tokens):
            s = jnp.einsum('bnd,d->bn', x, tok)
            eff_k = min(num_tokens * FETCH_K_RATIO, x.shape[1])
            scores = _coor_descent(s, eff_k)
            sel_scores, sel_idx = jax.lax.top_k(scores, num_tokens)
            sel_scores = sel_scores + jax.lax.stop_gradient(1.0 - sel_scores)
            routed = jnp.take_along_axis(x, sel_idx[..., None], axis=1)
            return (sel_idx, sel_scores, routed)

        def _light_attn(x, ln_g, ln_b, qkv_w, out_w):
            b, n, d = x.shape
            h, dh, w = (HEADS, DIM_HEAD, WINDOW)
            nw = n // w
            xn = _layernorm(x, ln_g, ln_b)
            q, k, v = jnp.split(xn @ qkv_w, 3, axis=-1)
            to_heads = lambda t: t.reshape(b, n, h, dh).transpose(0, 2, 1, 3)
            q, k, v = (to_heads(q), to_heads(k), to_heads(v))
            bq = q.reshape(b, h, nw, w, dh) * dh ** (-0.5)

            def look_around(t):
                tp = jnp.pad(t.reshape(b, h, nw, w, dh), ((0, 0), (0, 0), (1, 1), (0, 0), (0, 0)))
                return jnp.concatenate([tp[:, :, i:nw + i] for i in range(3)], axis=3)
            bk, bv = (look_around(k), look_around(v))
            sim = jnp.einsum('bhwid,bhwjd->bhwij', bq, bk)
            t_q = jnp.arange(n).reshape(nw, w)
            tpad = jnp.pad(t_q, ((1, 1), (0, 0)), constant_values=-1)
            t_k = jnp.concatenate([tpad[i:nw + i] for i in range(3)], axis=-1)
            valid = (t_k >= 0)[:, None, :] & (jnp.abs(t_q[:, :, None] - t_k[:, None, :]) <= w)
            sim = jnp.where(valid[None, None], sim, -jnp.finfo(sim.dtype).max)
            attn = jax.nn.softmax(sim, axis=-1)
            out = jnp.einsum('bhwij,bhwjd->bhwid', attn, bv)
            out = out.reshape(b, h, n, dh).transpose(0, 2, 1, 3).reshape(b, n, h * dh)
            return out @ out_w

        def _heavy_attn(xq, ctx, scores_kv, gamma, q_w, kv_w, null_kv, out_w, rope_q, rope_k):
            b = xq.shape[0]
            h, dh = (HEADS, DIM_HEAD)
            xq = _rmsnorm(xq, gamma)
            ctx = _rmsnorm(ctx, gamma)
            q = (xq @ q_w).reshape(b, -1, h, dh).transpose(0, 2, 1, 3)
            kv = jnp.einsum('hdi,bni->bhnd', kv_w, ctx)
            k, v = (kv[..., :dh], kv[..., dh:])
            v = v * scores_kv[:, None, :, None]
            q = _apply_rope(rope_q[:, None], q)
            k = _apply_rope(rope_k[:, None], k)
            nk = jnp.broadcast_to(null_kv[0][None, :, None, :], (b, h, 1, dh))
            nv = jnp.broadcast_to(null_kv[1][None, :, None, :], (b, h, 1, dh))
            k = jnp.concatenate([nk, k], axis=2)
            v = jnp.concatenate([nv, v], axis=2)
            sim = jnp.einsum('bhid,bhjd->bhij', q, k) * dh ** (-0.5)
            attn = jax.nn.softmax(sim, axis=-1)
            out = jnp.einsum('bhij,bhjd->bhid', attn, v)
            out = out.transpose(0, 2, 1, 3).reshape(b, -1, h * dh)
            return out @ out_w

        def _forward(x, ln_gamma, ln_beta, light_qkv_w, light_out_w, q_route_tok, kv_route_tok, heavy_gamma, heavy_q_w, heavy_kv_w, heavy_null_kv, heavy_out_w, null_q_token):
            b, n, d = x.shape
            light_out = _light_attn(x, ln_gamma, ln_beta, light_qkv_w, light_out_w)
            idx_q, sc_q, rt_q = _route(x, q_route_tok, NQ)
            idx_kv, sc_kv, rt_kv = _route(x, kv_route_tok, NKV)
            inv_freq = 1.0 / 10000.0 ** (jnp.arange(0, DIM_HEAD, 2, dtype=jnp.float32) / DIM_HEAD)
            freqs = jnp.arange(n, dtype=jnp.float32)[:, None] * inv_freq[None]
            pos = jnp.concatenate([freqs, freqs], axis=-1)
            rope_q = pos[idx_q]
            rope_k = pos[idx_kv]
            heavy_out = _heavy_attn(rt_q, rt_kv, sc_kv, heavy_gamma, heavy_q_w, heavy_kv_w, heavy_null_kv, heavy_out_w, rope_q, rope_k)
            heavy_out = heavy_out * sc_q[..., None]
            out = jnp.broadcast_to(null_q_token, x.shape)
            out = out.at[jnp.arange(b)[:, None], idx_q].set(heavy_out)
            return light_out + out
        return _forward(x, ln_gamma, ln_beta, light_qkv_w, light_out_w, q_route_tok, kv_route_tok, heavy_gamma, heavy_q_w, heavy_kv_w, heavy_null_kv, heavy_out_w, null_q_token)

    def _L0_ffn_ref(x, Win, bin_, W1, b1, W2, b2, Wout, bout):
        import jax, jax.numpy as jnp
        import numpy as np
        D_MODEL = 256
        M = 64
        INNER = 16
        s = jnp.einsum('btd,dm->btm', x, Win) + bin_
        h = jax.nn.relu(s[..., None] * W1 + b1)
        g = jnp.einsum('btmh,mh->btm', h, W2) + b2
        out = jnp.einsum('btm,md->btd', g, Wout) + bout
        return out

    def _L1_attn_ref(x, Wq, Wk, Wv, q_gamma, q_beta, k_gamma, k_beta, Wo, bo):
        import math
        import jax, jax.numpy as jnp
        import numpy as np
        DIM = 256
        N_HEADS = 16
        HEAD_DIM = DIM // N_HEADS
        SEQ_LEN = 512
        BASE = 10000.0
        EPS = 1e-05

        def rope_cache(seq_len, dim):
            pos = jnp.arange(seq_len, dtype=jnp.float32)[:, None]
            di = jnp.arange(0, dim, 2, dtype=jnp.float32) / dim
            theta = pos * jnp.exp(-di * math.log(BASE))
            cos = jnp.repeat(jnp.cos(theta), 2, axis=1)
            sin = jnp.repeat(jnp.sin(theta), 2, axis=1)
            return (cos, sin)

        def rotate_half(x):
            x1 = x[..., ::2]
            x2 = x[..., 1::2]
            return jnp.concatenate((-x2, x1), axis=-1)

        def layernorm(x, gamma, beta):
            mu = jnp.mean(x, axis=-1, keepdims=True)
            var = jnp.var(x, axis=-1, keepdims=True)
            return (x - mu) * jax.lax.rsqrt(var + EPS) * gamma + beta
        B, S, D = x.shape
        H, hd = (N_HEADS, HEAD_DIM)
        q = (x @ Wq.T).reshape(B, S, H, hd).transpose(0, 2, 1, 3)
        k = (x @ Wk.T).reshape(B, S, H, hd).transpose(0, 2, 1, 3)
        v = (x @ Wv.T).reshape(B, S, H, hd).transpose(0, 2, 1, 3)
        q = layernorm(q, q_gamma, q_beta)
        k = layernorm(k, k_gamma, k_beta)
        cos, sin = rope_cache(S, hd)
        cos = cos[None, None]
        sin = sin[None, None]
        q = q * cos + rotate_half(q) * sin
        k = k * cos + rotate_half(k) * sin
        scale = 1.0 / math.sqrt(hd)
        scores = scale * jnp.einsum('bhqd,bhkd->bhqk', q, k)
        mask = jnp.tril(jnp.ones((S, S), dtype=bool))
        scores = jnp.where(mask, scores, -jnp.inf)
        attn = jax.nn.softmax(scores, axis=-1)
        out = jnp.einsum('bhqk,bhkd->bhqd', attn, v)
        out = out.transpose(0, 2, 1, 3).reshape(B, S, D)
        return out @ Wo.T + bo

    def _L1_ffn_ref(x, w1, b1, w2, b2):
        import jax, jax.numpy as jnp
        import numpy as np

        def _binarize(w):
            alpha = jax.lax.stop_gradient(jnp.mean(jnp.abs(w), axis=1, keepdims=True))
            bw = alpha * jnp.sign(w)
            return w + jax.lax.stop_gradient(bw - w)
        bw1 = _binarize(w1)
        h = jnp.einsum('bsd,hd->bsh', x, bw1) + b1
        h = jax.nn.gelu(h, approximate=False)
        bw2 = _binarize(w2)
        out = jnp.einsum('bsh,dh->bsd', h, bw2) + b2
        return out
    x = L0_attn_x
    mod = (_silu(L0_c) @ L0_wmod).reshape(L0_c.shape[0], 6, 1, -1)
    sa, ca, ga, sb, cb, gb = (mod[:, 0], mod[:, 1], mod[:, 2], mod[:, 3], mod[:, 4], mod[:, 5])
    ga = (2 * (ga >= 0) - 1) * jnp.maximum(jnp.abs(ga), 0.25)
    gb = (2 * (gb >= 0) - 1) * jnp.maximum(jnp.abs(gb), 0.25)
    h = _layernorm(x, axis=-1) * (1 + ca) + sa
    x = x + ga * _L0_attn_ref(h, L0_attn_ln_gamma, L0_attn_ln_beta, L0_attn_light_qkv_w, L0_attn_light_out_w, L0_attn_q_route_tok, L0_attn_kv_route_tok, L0_attn_heavy_gamma, L0_attn_heavy_q_w, L0_attn_heavy_kv_w, L0_attn_heavy_null_kv, L0_attn_heavy_out_w, L0_attn_null_q_token)
    h = _layernorm(x, axis=-1) * (1 + cb) + sb
    x = x + gb * _L0_ffn_ref(h, L0_ffn_Win, L0_ffn_bin_, L0_ffn_W1, L0_ffn_b1, L0_ffn_W2, L0_ffn_b2, L0_ffn_Wout, L0_ffn_bout)
    mod = (_silu(L1_c) @ L1_wmod).reshape(L1_c.shape[0], 6, 1, -1)
    sa, ca, ga, sb, cb, gb = (mod[:, 0], mod[:, 1], mod[:, 2], mod[:, 3], mod[:, 4], mod[:, 5])
    ga = (2 * (ga >= 0) - 1) * jnp.maximum(jnp.abs(ga), 0.25)
    gb = (2 * (gb >= 0) - 1) * jnp.maximum(jnp.abs(gb), 0.25)
    h = _layernorm(x, axis=-1) * (1 + ca) + sa
    x = x + ga * _L1_attn_ref(h, L1_attn_Wq, L1_attn_Wk, L1_attn_Wv, L1_attn_q_gamma, L1_attn_q_beta, L1_attn_k_gamma, L1_attn_k_beta, L1_attn_Wo, L1_attn_bo)
    h = _layernorm(x, axis=-1) * (1 + cb) + sb
    x = x + gb * _L1_ffn_ref(h, L1_ffn_w1, L1_ffn_b1, L1_ffn_w2, L1_ffn_b2)
    return x

_drawn_inputs = setup_inputs


def setup_inputs(seed=0):
    import zlib

    import numpy as np

    out = dict(_drawn_inputs(seed))
    spreads = {'L0_attn_ln_gamma': (1.0, 0.6),
     'L0_attn_ln_beta': (0.0, 0.8),
     'L0_attn_heavy_gamma': (1.0, 0.6),
     'L1_attn_q_gamma': (1.0, 0.6),
     'L1_attn_q_beta': (0.0, 2.0),
     'L1_attn_k_gamma': (1.0, 0.6),
     'L1_attn_k_beta': (0.0, 2.0),
     'L1_attn_bo': (0.0, 1.355)}
    factors = {'L0_attn_light_qkv_w': 8.0,
     'L0_attn_light_out_w': 8.0,
     'L0_attn_kv_route_tok': 8.0,
     'L0_attn_heavy_q_w': 8.0,
     'L0_attn_heavy_kv_w': 8.0,
     'L0_attn_heavy_null_kv': 8.0,
     'L0_attn_heavy_out_w': 8.0,
     'L0_ffn_Win': 3.465,
     'L0_ffn_bin_': 56.31,
     'L0_ffn_W1': 3.41,
     'L0_ffn_bout': 13.138,
     'L1_ffn_w1': 3.393,
     'L1_ffn_b1': 41.637,
     'L1_ffn_w2': 3.288,
     'L1_ffn_b2': 47.689,
     'L0_ffn_b1': 6.967,
     'L0_ffn_b2': 8.0,
     'L1_attn_Wq': 3.894,
     'L1_attn_Wk': 3.724}
    for name, (base, spread) in spreads.items():
        noise = np.random.default_rng([zlib.crc32(name.encode()), seed]).standard_normal(out[name].shape)
        drawn = base * np.exp(spread * noise) if base else spread * noise
        out[name] = jnp.asarray(drawn.astype(out[name].dtype))
    for name, factor in factors.items():
        out[name] = (out[name] * factor).astype(out[name].dtype)
    return out
```

```python
from contextlib import ExitStack
import math

import numpy as np

import concourse.bass as bass
from concourse import mybir

F32 = mybir.dt.float32
BF16 = mybir.dt.bfloat16
I32 = mybir.dt.int32
U32 = mybir.dt.uint32
ALU = mybir.AluOpType
ACT = mybir.ActivationFunctionType
AX_X = mybir.AxisListType.X

P = 128
B, N, D = 8, 1024, 256
T = N // P
KD = D // P
H0, DH = 8, 64
HD = H0 * DH
WIN = 64
NPAD = N + 2 * WIN
NQ = 256
NITER, EPS, EPS0, DECAY = 20, 0.03, 4.0, 0.7
EFF_K = min(NQ * 9.0 / 8.0, N)
H1, HD1 = 16, 16
G1 = 4
NG = H1 // G1
KS = 6 * HD1
KA = KS + 2
F1 = 1024
FT = F1 // P
MU, INNER = 64, 16
NEG = -1e30
LOG_K = math.log(max(EFF_K, 1e-20))
FLOOR_EXP = 87.4

C_LNG, C_LNB, C_HG, C_BIN, C_W1, C_B1, C_W2, C_B2, C_FB1 = 0, 2, 4, 6, 7, 15, 23, 31, 32
NCOLS = 40
R_TQ, R_TK, R_NULL, R_BOUT, R_BO, R_B2 = (i * D for i in range(6))
R_GB = 6 * D
NROWS = R_GB + 4 * HD1


class Plan:

    ENGINES = ("tensor", "vector", "scalar", "gpsimd", "sync")

    def __init__(self, sems, dma_sems):
        self.sems, self.dma_sems = sems, dma_sems
        self.queue = {e: [] for e in self.ENGINES}
        self.pool_dmas = set()
        self.count, self.seen, self.used = {}, {e: {} for e in self.ENGINES}, {}

    def _waits(self, engine, waits):
        need = {}
        for w in waits:
            for sem, value in (w if isinstance(w, list) else [w]) if w is not None else []:
                if self.seen[engine].get(sem, 0) < value:
                    need[sem] = max(need.get(sem, 0), value)
        self.seen[engine].update(need)
        return list(need.items())

    def do(self, engine, fn, *waits, sig=True):
        need = self._waits(engine, waits)
        token = None
        if sig:
            self.count[engine] = self.count.get(engine, 0) + 1
            token = (engine, self.count[engine])
        self.queue[engine].append((fn, need, self.sems[engine] if sig else None, 1))
        return token

    def dma(self, engine, name, fn, *waits):
        need = self._waits(engine, waits)
        if name not in self.used:
            self.used[name] = self.dma_sems[len(self.used)]
        if engine == "gpsimd":
            self.pool_dmas.add(name)
        self.count[name] = self.count.get(name, 0) + 16
        self.queue[engine].append((fn, need, self.used[name], 16))
        return (name, self.count[name])

    def emit(self, nc):
        last = [(n, self.count[n]) for n in self.used]
        self.queue["sync"].append((None, self._waits("sync", last), None, 0))
        pool_last = [(n, self.count[n]) for n in sorted(self.pool_dmas)]
        self.queue["gpsimd"].append((None, self._waits("gpsimd", pool_last), None, 0))
        with nc.Block() as block:
            for name in self.ENGINES:
                def program(eng, name=name):
                    for fn, need, sem, by in self.queue[name]:
                        for s, v in need:
                            eng.wait_ge(self.sems[s] if s in self.sems else self.used[s], v)
                        if fn is not None:
                            ins = fn(eng)
                            if sem is not None:
                                ins.then_inc(sem, by)
                block_on = {"tensor": block.tensor, "vector": block.vector, "scalar": block.scalar,
                            "gpsimd": block.gpsimd, "sync": block.sync}[name]
                block_on(program)
        every = [*self.sems.values(), *self.dma_sems]
        used = range(min(s.num for s in every), max(s.num for s in every) + 1)
        if self.pool_dmas:
            nc.gpsimd.dma_reset(used)
        nc.gpsimd.sem_clear(used)
        nc.all_engine_barrier()


def adaln_kernel(nc, a, out):
    ctx = ExitStack()
    with ctx:
        def sb(name, shape, dt=F32):
            return ctx.enter_context(nc.sbuf_tensor(name, shape, dt))

        def dram(name, shape, dt=F32):
            return nc.dram_tensor(name, shape, dt, kind="Internal").ap()

        sems = {e: ctx.enter_context(nc.semaphore(f"done_{e}")) for e in Plan.ENGINES}
        dma_sems = [ctx.enter_context(nc.semaphore(f"landed_{i}")) for i in range(40)]

        mod_d = dram("mod_d", (B, 12 * D))
        h_d = dram("h_d", (B * N, D))
        heavy_d = dram("heavy_d", (N, D))
        split_d = dram("split_d", (3, 2 * D, N), BF16)
        max_d = dram("max_d", (2, NG, G1 * T, P), BF16)

        ident = sb("ident", [P, P])
        identb = sb("identb", [P, P], BF16)
        wmask = sb("wmask", [P, 3, 2 * P])
        cmask = sb("cmask", [P, P], BF16)
        cols = sb("cols", [P, NCOLS])
        rows = sb("rows", [P, NROWS])
        modc = sb("modc", [P, 6 * KD, B])
        wqkv = sb("wqkv", [P, KD, 3 * HD])
        wlo = sb("wlo", [P, HD // P, D])
        whq = sb("whq", [P, KD, HD])
        whk = sb("whk", [P, KD, HD])
        whv = sb("whv", [P, KD, HD])
        who = sb("who", [P, HD // P, D])
        nullk = sb("nullk", [P, H0 // 2])
        nullv = sb("nullv", [1, H0, DH + 1])
        win = sb("win", [P, KD, P])
        wfo = sb("wfo", [P, D])
        wqk1 = sb("wqk1", [P, KD, 2 * D])
        wv1 = sb("wv1", [P, KD, D])
        wo1 = sb("wo1", [P, KD, D])
        w1T = sb("w1T", [P, KD, F1])
        w2T = sb("w2T", [P, FT, D])
        tabA = sb("tabA", [P, 2, T, HD1])
        tabB = sb("tabB", [P, 2, T, HD1])
        tabC = sb("tabC", [P, 2, T, HD1])
        idx_all = sb("idx_all", [P, 2, 4 * B], U32)
        sc_all = sb("sc_all", [P, 4 * B])

        xt = sb("xt", [P, T, D])
        xn = sb("xn", [P, T, D])
        hT = sb("hT", [P, KD, NPAD])
        hvb = sb("hvb", [P, T, D])
        gates = sb("gates", [P, 4, D])
        wsc = sb("wsc", [P, FT, D])
        small = sb("small", [P, 640])
        work = sb("work", [P, 4096])
        arena = sb("arena", [P, 17536])

        def at(base, start, shape, dt=F32):
            n = int(np.prod(shape))
            words = n if dt != BF16 else n // 2
            v = base[:, start:start + words]
            if dt != F32:
                v = v.bitcast(dt)
            names = " ".join(f"x{i}" for i in range(len(shape)))
            return v.rearrange(f"p ({names}) -> p {names}", **{f"x{i}": s for i, s in enumerate(shape)})

        pb2 = [ctx.enter_context(nc.psum_tensor(f"pb{i}", [P, 2, 512], F32)) for i in range(4)]
        bank = [pb2[i // 2][:, i % 2, :] for i in range(8)]

        pl = Plan(sems, dma_sems)
        do, dma = pl.do, pl.dma
        free = [None] * 8

        for dst, src in ((ident[:, :], a["ident"]), (wmask[:, :, :], a["wmask"]), (cols[:, :], a["cols"]),
                         (rows[:, :], a["rows"].partition_broadcast(P))):
            ld_c = dma("sync", "consts", lambda e, dst=dst, src=src: e.dma_start(dst, src))
        cmf = at(work, 0, [P])
        ld_c = dma("sync", "consts", lambda e: e.dma_start(cmf, a["cmask"]))
        rope1 = at(work, 128, [2, T, HD1])
        ld_c = dma("sync", "consts", lambda e: e.dma_start(rope1, a["rope1"]))
        cT = at(work, 512, [2, KD, B])
        ld_c = dma("sync", "consts", lambda e: e.dma_start(cT, a["cT"]))
        wmod = at(arena, 0, [2, KD, 6 * D])
        for i in range(2):
            ld_m = dma("sync", "wmod", lambda e, i=i: e.dma_start(
                wmod[:, i], a[f"wmod{i}"].rearrange("(k p) m -> p k m", p=P)))
        w1r = at(arena, 6144, [FT, D])
        w2r = at(arena, 8192, [KD, F1])
        ld_w = dma("scalar", "mlp_w", lambda e: e.dma_start(w1r, a["w1"].rearrange("(k p) m -> p k m", p=P)))
        ld_w = dma("scalar", "mlp_w", lambda e: e.dma_start(w2r, a["w2"].rearrange("(k p) m -> p k m", p=P)))
        ld_q = dma("scalar", "qk_w", lambda e: e.dma_start(wqk1[:, :, :], a["wqk1"].rearrange("(k p) m -> p k m", p=P)))
        for dst, name in ((wqkv, "wqkv"), (wlo, "wlo"), (whq, "whq"), (whk, "whk"), (whv, "whv"), (who, "who"),
                          (win, "win"), (wv1, "wv1"), (wo1, "wo1")):
            dma("scalar", "rest_w", lambda e, dst=dst, name=name: e.dma_start(
                dst[:, :, :], a[name].rearrange("(k p) m -> p k m", p=P)))
        dma("scalar", "rest_w", lambda e: e.dma_start(wfo[:, :], a["wfo"]))
        dma("scalar", "rest_w", lambda e: e.dma_start(nullk[:, :], a["nullk"]))
        do("vector", lambda e: e.memset(nullv[:, :, DH:DH + 1], 1.0))
        ld_n = dma("sync", "null_v", lambda e: e.dma_start(nullv[:, :, 0:DH], a["null_v"]))

        do("vector", lambda e: e.memset(hT[:, :, 0:WIN], 0.0))
        do("vector", lambda e: e.memset(hT[:, :, WIN + N:NPAD], 0.0))
        do("vector", lambda e: e.tensor_copy(identb[:, :], ident[:, :]), ld_c)
        t_cm = do("vector", lambda e: e.tensor_copy(cmask[:, :], cmf), ld_c)

        sg = at(work, 576, [2, KD, B])
        sc = at(work, 640, [2, KD, B])
        t = do("scalar", lambda e: e.activation(sg, cT, ACT.Exp, scale=-1.0), ld_c)
        t = do("vector", lambda e: e.tensor_scalar(sg, sg, 1.0, None, ALU.add), t)
        t = do("vector", lambda e: e.reciprocal(sg, sg), t)
        t_sc = do("vector", lambda e: e.tensor_tensor(sc, cT, sg, ALU.mult), t)

        for j, (blk, part) in enumerate(((0, 3), (0, 4), (1, 0), (1, 1), (1, 3), (1, 4))):
            for kk in range(KD):
                c0 = (j * KD + kk) * B
                for k in range(KD):
                    t = do("tensor", lambda e, k=k, blk=blk, part=part, kk=kk, c0=c0: e.matmul(
                        bank[0][:, c0:c0 + B], wmod[:, blk, k, part * D + kk * P:part * D + (kk + 1) * P],
                        sc[:, blk, k, :], start=k == 0, stop=k == KD - 1), t_sc, ld_m, sig=k == KD - 1)
        t = do("vector", lambda e: e.tensor_copy(modc[:, :, :].rearrange("p j b -> p (j b)"), bank[0][:, 0:6 * KD * B]), t)
        for j in (1, 3, 5):
            do("vector", lambda e, j=j: e.tensor_scalar(modc[:, j * KD:(j + 1) * KD, :], modc[:, j * KD:(j + 1) * KD, :],
                                                        1.0, None, ALU.add), t)
        free[0] = t
        modr = at(arena, 10240, [12 * D])
        for q in range(6):
            bk = q % 6 + 1
            for k in range(KD):
                t = do("tensor", lambda e, k=k, q=q, bk=bk: e.matmul(
                    bank[bk][0:B, :], sc[:, q // 3, k, :], wmod[:, q // 3, k, (q % 3) * 512:(q % 3 + 1) * 512],
                    start=k == 0, stop=k == KD - 1), sig=k == KD - 1)
            t_mr = do("vector", lambda e, q=q, bk=bk: e.tensor_copy(modr[0:B, q * 512:(q + 1) * 512], bank[bk][0:B, :]), t)
            free[bk] = t_mr
        for j in (1, 4, 7, 10):
            v = modr[0:B, j * D:(j + 1) * D]
            do("vector", lambda e, v=v: e.tensor_scalar(v, v, 1.0, None, ALU.add), t_mr)
        for j in (2, 5, 8, 11):
            v = modr[0:B, j * D:(j + 1) * D]
            s = small[0:B, 0:D]
            t = do("vector", lambda e, v=v, s=s: e.tensor_scalar(s, v, 0.0, None, ALU.is_ge), t_mr)
            t = do("vector", lambda e, s=s: e.tensor_scalar(s, s, 2.0, -1.0, ALU.mult, ALU.add), t)
            t = do("vector", lambda e, v=v, s=s: e.tensor_tensor(v, v, s, ALU.mult), t)
            t = do("vector", lambda e, v=v: e.tensor_scalar(v, v, 0.25, None, ALU.max), t)
            t_mr = do("vector", lambda e, v=v, s=s: e.tensor_tensor(v, v, s, ALU.mult), t)
        dma("sync", "mod_out", lambda e: e.dma_start(mod_d, modr[0:B, :]), t_mr)

        wm = at(small, 256, [KD, 2 * H1])
        v4 = wqk1[:, :, :].rearrange("p k (h d) -> p k h d", d=HD1)
        t = do("vector", lambda e: e.tensor_reduce(wm, v4, AX_X, ALU.add), ld_q)
        t = do("vector", lambda e: e.tensor_scalar(wm, wm, 1.0 / HD1, None, ALU.mult), t)
        for k in range(KD):
            do("vector", lambda e, k=k: e.tensor_tensor(
                v4[:, k], v4[:, k], wm[:, k].unsqueeze(2).broadcast_to([P, 2 * H1, HD1]), ALU.subtract), t)

        cosr, sinr = rope1[:, 0], rope1[:, 1]
        half = HD1 // 2
        tmp = at(small, 384, [T, HD1])
        for i in range(2):
            g = rows[:, R_GB + 2 * i * HD1:R_GB + (2 * i + 1) * HD1]
            bt = rows[:, R_GB + (2 * i + 1) * HD1:R_GB + (2 * i + 2) * HD1]
            bc = lambda v, n: v.unsqueeze(1).broadcast_to([P, T, n])
            do("vector", lambda e, i=i, g=g: e.tensor_tensor(tabA[:, i], cosr, bc(g, HD1), ALU.mult), ld_c)
            do("vector", lambda e, i=i, g=g: e.tensor_tensor(tabB[:, i, :, 0:half], sinr[:, :, 0:half], bc(g[:, 1:HD1:2], half), ALU.mult))
            do("vector", lambda e, i=i, g=g: e.tensor_tensor(tabB[:, i, :, half:HD1], sinr[:, :, half:HD1], bc(g[:, 0:HD1:2], half), ALU.mult))
            do("vector", lambda e, i=i, bt=bt: e.tensor_tensor(tabC[:, i], cosr, bc(bt, HD1), ALU.mult))
            do("vector", lambda e, i=i, bt=bt: e.tensor_tensor(tmp[:, :, 0:half], sinr[:, :, 0:half], bc(bt[:, 1:HD1:2], half), ALU.mult),
               pl_last(pl, "vector"))
            t = do("vector", lambda e, i=i, bt=bt: e.tensor_tensor(tmp[:, :, half:HD1], sinr[:, :, half:HD1], bc(bt[:, 0:HD1:2], half), ALU.mult))
            t = do("vector", lambda e, i=i: e.tensor_tensor(tabC[:, i], tabC[:, i], tmp, ALU.add), t)
            if i == 0:
                for tb in (tabA, tabB, tabC):
                    do("vector", lambda e, tb=tb: e.tensor_scalar(tb[:, 0], tb[:, 0], HD1 ** -0.5, None, ALU.mult), t)

        al = small[:, 512:512 + FT + KD]
        sgn = at(arena, 13312, [F1])
        nb = 0
        for which, raw, nt, width in ((0, w1r, FT, D), (1, w2r, KD, F1)):
            for i in range(nt):
                w, ac, sv = raw[:, i, :], al[:, which * FT + i:which * FT + i + 1], sgn[:, 0:width]
                t = do("vector", lambda e, w=w, ac=ac: e.tensor_reduce(ac, w, AX_X, ALU.add, apply_absolute_value=True), ld_w)
                t = do("vector", lambda e, ac=ac, width=width: e.tensor_scalar(ac, ac, 1.0 / width, None, ALU.mult), t)
                t2 = do("scalar", lambda e, w=w, sv=sv: e.activation(sv, w, ACT.Sign), t, ld_w)
                t = do("vector", lambda e, w=w, ac=ac, sv=sv: e.scalar_tensor_tensor(
                    out=sv, in0=sv, scalar=ac, in1=w, op0=ALU.mult, op1=ALU.subtract), t, t2)
                t = do("vector", lambda e, w=w, sv=sv: e.tensor_tensor(w, w, sv, ALU.add), t)
                for c0 in range(0, width // P, 4):
                    n = min(4, width // P - c0)
                    bk = nb % 7 + 1
                    nb += 1
                    for c in range(n):
                        tt = do("tensor", lambda e, raw=raw, i=i, c=c, c0=c0, bk=bk: e.transpose(
                            bank[bk][:, c * P:(c + 1) * P], raw[:, i, (c0 + c) * P:(c0 + c + 1) * P], ident[:, :]),
                            t, free[bk], sig=c == n - 1)
                    dst = w1T[:, 0:KD, i * P:(i + 1) * P] if which == 0 else w2T[:, c0:c0 + 4, i * P:(i + 1) * P]
                    free[bk] = do("scalar", lambda e, dst=dst, bk=bk, n=n: e.activation(
                        dst, bank[bk][:, 0:n * P].rearrange("p (c q) -> p c q", q=P), ACT.Copy), tt)
        pl.emit(nc)

        s_all = at(arena, 16384, [B, 2, T])
        with nc.Fori(0, B) as b:
            pl = Plan(sems, dma_sems)
            do, dma = pl.do, pl.dma
            mods = at(arena, 0, [2, D])
            s_b = at(small, 0, [2, T])
            ld_x = dma("sync", "x", lambda e: e.dma_start(xt[:, :, :], a["x"][b].rearrange("(t p) d -> p t d", p=P)))
            ld_r = dma("scalar", "mod", lambda e: e.dma_start(
                mods, mod_d[bass.ds(b, 1), 0:2 * D].partition_broadcast(P)))
            t_n = layer_norm(pl, xt, xn, small, 64, ld_x)
            hb = at(arena, 2048, [T, D])
            scratch = at(arena, 4096, [D])
            for i in range(T):
                t = do("gpsimd", lambda e, i=i: e.tensor_tensor(hb[:, i], xn[:, i], mods[:, 1], ALU.mult), t_n[i], ld_r)
                t_h = do("gpsimd", lambda e, i=i: e.tensor_tensor(hb[:, i], hb[:, i], mods[:, 0], ALU.add), t)
                for r, c in ((0, R_TQ), (1, R_TK)):
                    t = do("vector", lambda e, i=i, r=r, c=c: e.tensor_tensor_reduce(
                        out=scratch, in0=hb[:, i], in1=rows[:, c:c + D], scale=1.0, scalar=0.0, op0=ALU.mult,
                        op1=ALU.add, accum_out=s_b[:, r, i:i + 1]), t_h, pl_last(pl, "vector"))
            dma("sync", "h", lambda e: e.dma_start(
                h_d[bass.ds(b * N, N), :].rearrange("(t p) d -> p t d", p=P), hb), t_h)
            do("vector", lambda e: e.tensor_copy(s_all[:, bass.ds(b, 1), :, :].rearrange("p o r t -> p (o r t)"), s_b.rearrange("p r t -> p (r t)")), t)
            pl.emit(nc)

        pl = Plan(sems, dma_sems)
        do, dma = pl.do, pl.dma
        V = lambda fn, *w: do("vector", fn, *w, pl_last(pl, "vector"))
        group, lower = at(arena, 0, [P]), at(arena, 128, [P])
        iota = at(arena, 256, [NQ])
        tokv = at(arena, 512, [T])
        ld = dma("sync", "consts", lambda e: e.dma_start(group, a["group"]))
        ld = dma("sync", "consts", lambda e: e.dma_start(lower, a["lower"]))
        ld = dma("sync", "consts", lambda e: e.dma_start(iota, a["iota"].partition_broadcast(P)))
        ld = dma("sync", "consts", lambda e: e.dma_start(tokv, a["tokv"]))
        s, u, ex, w_, m1, m2, r1, posm = (at(arena, 1024 + 128 * i, [P]) for i in range(8))
        c_ = lambda i: small[:, i:i + 1]
        pmax, smax, na, m, mt, part, lns, cnt, ndef, flag = (c_(i) for i in range(10))
        sall2 = s_all.rearrange("p b r t -> p (b r t)")
        t = do("tensor", lambda e: e.transpose(bank[0][:, 0:P], sall2, ident[:, :]))
        t = V(lambda e: e.tensor_copy(s, bank[0][:, 0:P]), t)
        t = V(lambda e: e.tensor_reduce(pmax, s, AX_X, ALU.max))
        row, row8 = at(arena, 2048, [P])[0:1, :], at(arena, 2176, [2 * B])[0:1, :]
        t = do("tensor", lambda e: e.transpose(bank[1][0:1, 0:P], pmax, ident[:, :]), t)
        t = V(lambda e: e.tensor_reduce(row8, bank[1][0:1, 0:P].rearrange("o (g t) -> o g t", t=T), AX_X, ALU.max), t)
        t = V(lambda e: e.tensor_copy(row.rearrange("o (g t) -> o g t", t=T), row8.unsqueeze(2).broadcast_to([1, 2 * B, T])))
        t = do("tensor", lambda e: e.matmul(bank[2][:, 0:1], row, ident[0:1, 0:1], start=True, stop=True), t)
        V(lambda e: e.tensor_copy(smax, bank[2][:, 0:1]), t)

        cur = max(EPS0, EPS)
        V(lambda e, v=-cur * (LOG_K - math.log(N)): e.memset(na, v))
        for it in range(1, NITER):
            cur = max(cur * DECAY, EPS)
            V(lambda e: e.tensor_scalar(m, smax, na, None, ALU.min))
            t = V(lambda e: e.tensor_scalar(u, s, na, m, ALU.min, ALU.subtract))
            V(lambda e, v=-cur * LOG_K: e.tensor_scalar(mt, m, v, None, ALU.add))
            t = do("scalar", lambda e, v=1.0 / cur: e.activation(ex, u, ACT.Exp, scale=v, accum_out=part), t)
            t = do("tensor", lambda e: e.matmul(bank[3][:, 0:1], group, part, start=True, stop=True), t, ld)
            t = do("scalar", lambda e: e.activation(lns, bank[3][:, 0:1], ACT.Ln), t)
            V(lambda e, v=cur: e.tensor_scalar(na, lns, v, mt, ALU.mult, ALU.add), t)
        cur = max(cur * DECAY, EPS)
        V(lambda e: e.tensor_scalar(u, s, na, -1.0, ALU.subtract, ALU.mult))
        V(lambda e: e.tensor_scalar(w_, u, 0.0, 1.0 / cur, ALU.max, ALU.mult))
        t_w = V(lambda e: e.tensor_scalar(w_, w_, FLOOR_EXP, None, ALU.min))
        t = do("scalar", lambda e: e.activation(ex, w_, ACT.Exp, scale=-1.0), t_w)
        V(lambda e: e.tensor_scalar(u, ex, -1.0, 1.0, ALU.mult, ALU.add), t)
        t_sc = V(lambda e: e.tensor_tensor(u, u, ex, ALU.add))

        thr, cand, acc = (small[:, 16 + i:17 + i] for i in range(3))
        thri, candi, acci = thr.bitcast(I32), cand.bitcast(I32), acc.bitcast(I32)
        V(lambda e: e.memset(thr, 0.0))
        for bit in range(30, -1, -1):
            V(lambda e, bit=bit: e.tensor_scalar(candi, thri, 1 << bit, None, ALU.bitwise_or))
            t = V(lambda e: e.tensor_scalar(m1, w_, cand, None, ALU.is_lt, ALU.add, accum_out=cnt))
            t = do("tensor", lambda e: e.matmul(bank[4][:, 0:1], group, cnt, start=True, stop=True), t)
            V(lambda e: e.tensor_scalar(acci, bank[4][:, 0:1], float(NQ), None, ALU.is_lt), t)
            V(lambda e, bit=bit: e.scalar_tensor_tensor(out=thri, in0=acci, scalar=bit, in1=thri,
                                                        op0=ALU.logical_shift_left, op1=ALU.bitwise_or))
        V(lambda e: e.tensor_scalar(m1, w_, thr, None, ALU.is_lt, ALU.add, accum_out=cnt))
        t = V(lambda e: e.tensor_scalar(m2, w_, thr, None, ALU.is_equal, ALU.add, accum_out=flag))
        t = do("tensor", lambda e: e.matmul(bank[4][:, 0:1], group, cnt, start=True, stop=True), t)
        t = do("tensor", lambda e: e.matmul(bank[5][:, 0:1], lower, flag, start=True, stop=True))
        V(lambda e: e.tensor_scalar(ndef, bank[4][:, 0:1], -1.0, float(NQ), ALU.mult, ALU.add), t)
        V(lambda e: e.tensor_scalar(ndef, ndef, bank[5][:, 0:1], None, ALU.subtract))
        zero = at(arena, 2304, [P])
        V(lambda e: e.memset(zero, 0.0))
        V(lambda e: e.tensor_tensor_scan(r1, m2, zero, 0.0, ALU.add, ALU.add))
        V(lambda e: e.tensor_scalar(r1, r1, ndef, None, ALU.is_le))
        V(lambda e: e.tensor_tensor(m2, m2, r1, ALU.mult))
        V(lambda e: e.tensor_tensor(m1, m1, m2, ALU.add))
        V(lambda e: e.tensor_tensor_scan(r1, m1, zero, 0.0, ALU.add, ALU.add))
        t = V(lambda e: e.tensor_copy(cnt, r1[:, P - 1:P]))
        t = do("tensor", lambda e: e.matmul(bank[4][:, 0:1], lower, cnt, start=True, stop=True), t)
        V(lambda e: e.tensor_scalar(r1, r1, bank[4][:, 0:1], None, ALU.add), t)
        V(lambda e: e.tensor_tensor(r1, r1, m1, ALU.mult))
        t = V(lambda e: e.tensor_scalar(posm, r1, -1.0, None, ALU.add))
        t = do("tensor", lambda e: e.transpose(bank[0][:, 0:P], posm, ident[:, :]), t)
        t2 = do("tensor", lambda e: e.transpose(bank[1][:, 0:P], u, ident[:, :]), t_sc)
        posT = at(arena, 2432, [2 * B, T])
        val = at(arena, 2560, [2 * B * T, 2])
        V(lambda e: e.tensor_copy(posT.rearrange("p g t -> p (g t)"), bank[0][:, 0:P]), t)
        V(lambda e: e.tensor_copy(val[:, :, 1], bank[1][:, 0:P]), t2)
        t_v = V(lambda e: e.tensor_copy(val[:, :, 0].rearrange("p (g t) -> p g t", t=T),
                                        tokv.unsqueeze(1).broadcast_to([P, 2 * B, T])), ld)
        used = [None] * 2
        res = bank[6].rearrange("p (g two) -> p g two", two=2)
        for g in range(2 * B):
            hots = []
            for t_ in range(T):
                hot = at(arena, 3072 + NQ * (t_ + T * (g % 2)), [NQ])
                t = do("vector", lambda e, hot=hot, g=g, t_=t_: e.tensor_scalar(
                    hot, iota, posT[:, g, t_:t_ + 1], None, ALU.is_equal), t_v, used[g % 2])
                hots.append((hot, t))
            for h in range(2):
                for t_, (hot, tk) in enumerate(hots):
                    t = do("tensor", lambda e, hot=hot, g=g, h=h, t_=t_: e.matmul(
                        res[:, 2 * g + h, :], hot[:, h * P:(h + 1) * P], val[:, g * T + t_, :],
                        start=t_ == 0, stop=t_ == T - 1), tk, t_v, sig=t_ == T - 1)
            used[g % 2] = t
        V(lambda e: e.tensor_copy(sc_all[:, :], res[:, 0:4 * B, 1]), t)
        V(lambda e: e.tensor_copy(idx_all[:, 1, :], res[:, 0:4 * B, 0]))
        off = at(arena, 2816, [4 * B])
        ld = dma("sync", "rowoff", lambda e: e.dma_start(off, a["rowoff"].partition_broadcast(P)))
        V(lambda e: e.tensor_tensor(off, off, res[:, 0:4 * B, 0], ALU.add), ld)
        V(lambda e: e.tensor_copy(idx_all[:, 0, :], off))
        pl.emit(nc)

        idxb = sb("idxb", [P, 2, 4], U32)
        scb = sb("scb", [P, 4])
        modcb = sb("modcb", [P, 6 * KD])
        with nc.Fori(0, B) as b:
            pl = Plan(sems, dma_sems)
            do, dma = pl.do, pl.dma
            free = [None] * 8
            last = lambda e: pl_last(pl, e)

            ld_x = dma("sync", "x", lambda e: e.dma_start(xt[:, :, :], a["x"][b].rearrange("(t p) d -> p t d", p=P)))
            ld_h = dma("sync", "h", lambda e: e.dma_start(
                hvb[:, :, :], h_d[bass.ds(b * N, N), :].rearrange("(t p) d -> p t d", p=P)))
            ld_g = dma("scalar", "gates", lambda e: e.dma_start(
                gates[:, :, :], mod_d[bass.ds(b, 1), :].rearrange("o (j d) -> o j d", d=D)[:, 2:12:3, :].partition_broadcast(P)))
            fill = dma("scalar", "fill", lambda e: e.dma_start(
                heavy_d.rearrange("(t p) d -> p t d", p=P), rows[:, R_NULL:R_NULL + D].unsqueeze(1).broadcast_to([P, T, D])))
            t_ix = do("vector", lambda e: e.tensor_copy(idxb[:, :, :], idx_all[:, :, bass.ds(b * 4, 4)]))
            do("vector", lambda e: e.tensor_copy(scb[:, :], sc_all[:, bass.ds(b * 4, 4)]))
            t_mc = do("vector", lambda e: e.tensor_copy(modcb[:, :], modc[:, :, bass.ds(b, 1)].rearrange("p j o -> p (j o)")))

            rg = at(arena, 0, [4, D])
            ropeg = at(arena, 1024, [4, 2 * DH])
            nT = at(arena, 1536, [2, KD, NQ])
            qk = at(arena, 2560, [4, HD])
            rt1 = at(arena, 4608, [HD])
            rt2 = at(arena, 5120, [HD])
            qz = at(arena, 5632, [H0 // 2, 2, NQ])
            kh = at(arena, 7680, [H0 // 2, NQ + 1])
            vh = at(arena, 8712, [2, H0, DH + 1])
            ph = [at(arena, 9752 + 260 * i, [NQ + 1]) for i in range(2)]
            pth = [at(arena, 10272 + 384 * i, [3, P]) for i in range(2)]
            ot_h = at(arena, 11040, [HD])
            otT = at(arena, 11552, [HD // P, P])
            hout = at(arena, 12064, [2, D])
            ssum, rn, mxh = small[:, 0:4], small[:, 4:8], small[:, 8:8 + 16]
            exq, rcph = small[:, 24:28], small[:, 28:36]
            junk = at(arena, 12576, [D])
            gat, rop = [], []
            for j in range(4):
                gat.append(dma("gpsimd", f"gather{j}", lambda e, j=j: e.indirect_dma_start(
                    out=rg[:, j], out_offset=None, in_=h_d, in_offset=bass.IndirectOffsetOnAxis(ap=idxb[:, 0, j:j + 1], axis=0)), t_ix))
            for j in range(4):
                rop.append(dma("gpsimd", f"rope{j}", lambda e, j=j: e.indirect_dma_start(
                    out=ropeg[:, j], out_offset=None, in_=a["rope0"], in_offset=bass.IndirectOffsetOnAxis(ap=idxb[:, 1, j:j + 1], axis=0)), t_ix))
            do("vector", lambda e: e.memset(qz[0:DH, :, 1], 0.0))
            do("vector", lambda e: e.memset(qz[DH:P, :, 0], 0.0))
            do("vector", lambda e: e.memset(vh[:, :, :, DH:DH + 1], 1.0))
            t_nk = do("vector", lambda e: e.tensor_copy(kh[:, :, 0], nullk[:, :]))
            t = do("gpsimd", lambda e: e.memset(exq, -0.5))
            for j in range(4):
                t1 = do("vector", lambda e, j=j: e.tensor_tensor_reduce(
                    out=junk, in0=rg[:, j], in1=rg[:, j], scale=1.0, scalar=0.0, op0=ALU.mult, op1=ALU.add,
                    accum_out=ssum[:, j:j + 1]), gat[j], last("vector"))
            t1 = do("vector", lambda e: e.tensor_scalar(rn, ssum, 1e-24, None, ALU.max), t1)
            t1 = do("gpsimd", lambda e: e.tensor_tensor(rn, rn, exq, ALU.pow), t, t1)
            t1 = do("vector", lambda e: e.tensor_scalar(rn, rn, float(D) ** 0.5, None, ALU.mult), t1)
            for j in range(4):
                tn = do("vector", lambda e, j=j: e.tensor_scalar(rg[:, j], rg[:, j], rn[:, j:j + 1], None, ALU.mult), t1)
                for k in range(KD):
                    t = do("tensor", lambda e, j=j, k=k: e.transpose(
                        bank[j // 2][:, k * NQ + (j % 2) * P:k * NQ + (j % 2 + 1) * P], rg[:, j, k * P:(k + 1) * P], ident[:, :]),
                        tn, sig=k == KD - 1)
                if j % 2:
                    for k in range(KD):
                        t_nT = do("scalar", lambda e, j=j, k=k: e.activation(
                            nT[:, j // 2, k], bank[j // 2][:, k * NQ:(k + 1) * NQ], ACT.Copy,
                            scale=cols[:, C_HG + k:C_HG + k + 1]), t)
                    free[j // 2] = t_nT
            t_v = []
            for j in range(6):
                w = (whq, whq, whk, whk, whv, whv)[j]
                src, half_ = (0, 0, 1, 1, 1, 1)[j], j % 2
                bk = 2 + j
                for k in range(KD):
                    t = do("tensor", lambda e, w=w, src=src, half_=half_, k=k, bk=bk: e.matmul(
                        bank[bk], nT[:, src, k, half_ * P:(half_ + 1) * P], w[:, k, :], start=k == 0, stop=k == KD - 1),
                        t_nT, free[bk], sig=k == KD - 1)
                if j < 4:
                    free[bk] = t_e = do("scalar", lambda e, j=j, bk=bk: e.activation(
                        qk[:, j], bank[bk], ACT.Copy, scale=DH ** -0.5 if j < 2 else 1.0), t)
                    x4 = qk[:, j].rearrange("p (h d) -> p h d", d=DH)
                    r1_, r2_ = (v.rearrange("p (h d) -> p h d", d=DH) for v in (rt1, rt2))
                    hd = DH // 2
                    cs = lambda lo, hi, j=j: ropeg[:, j, lo:hi].unsqueeze(1).broadcast_to([P, H0, hi - lo])
                    do("vector", lambda e, x4=x4, r=r1_, c=cs(0, DH): e.tensor_tensor(r, x4, c, ALU.mult), t_e, rop[j], last("vector"))
                    do("vector", lambda e, x4=x4, r=r2_, c=cs(DH, DH + hd): e.tensor_tensor(r[:, :, 0:hd], x4[:, :, hd:DH], c, ALU.mult))
                    t = do("vector", lambda e, x4=x4, r=r2_, c=cs(DH + hd, 2 * DH): e.tensor_tensor(r[:, :, hd:DH], x4[:, :, 0:hd], c, ALU.mult))
                    t = do("vector", lambda e, j=j: e.tensor_tensor(qk[:, j], rt1, rt2, ALU.add), t)
                    tb = j % 2
                    for p_ in range(H0 // 2):
                        t2 = do("tensor", lambda e, j=j, p_=p_, tb=tb: e.transpose(
                            bank[tb][:, p_ * P:(p_ + 1) * P], qk[:, j, p_ * P:(p_ + 1) * P], ident[:, :]), t, free[tb],
                            sig=p_ == H0 // 2 - 1)
                    bv = bank[tb].rearrange("p (c q) -> p c q", q=P)
                    if j < 2:
                        do("scalar", lambda e, j=j, bv=bv: e.activation(
                            qz[0:DH, :, 0, j * P:(j + 1) * P], bv[0:DH], ACT.Copy), t2)
                        free[tb] = do("scalar", lambda e, j=j, bv=bv: e.activation(
                            qz[DH:P, :, 1, j * P:(j + 1) * P], bv[DH:P], ACT.Copy), t2)
                    else:
                        free[tb] = do("scalar", lambda e, half_=half_, bv=bv: e.activation(
                            kh[:, :, 1 + half_ * P:1 + (half_ + 1) * P], bv, ACT.Copy), t2)
                    t_qk = free[tb]
                else:
                    t_v.append(do("vector", lambda e, half_=half_, bk=bk: e.tensor_scalar(
                        vh[:, half_, :, 0:DH], bank[bk].rearrange("p (h d) -> p h d", d=DH), scb[:, 2 + half_:3 + half_],
                        None, ALU.mult), t))
                    free[bk] = t_v[-1]
            t_qz0 = t_nk
            n = 0
            for half_ in range(2):
                for h in range(H0):
                    pr, sl = h // 2, n % 2
                    t = do("tensor", lambda e, pr=pr, h=h, half_=half_, sl=sl: e.matmul(
                        bank[sl][:, 0:NQ + 1], qz[:, pr, h % 2, half_ * P:(half_ + 1) * P], kh[:, pr, :], start=True, stop=True),
                        t_qk, t_qz0, free[sl])
                    t = do("vector", lambda e, sl=sl, n=n: e.tensor_reduce(
                        mxh[:, n:n + 1], bank[sl][:, 0:NQ + 1], AX_X, ALU.max, negate=True), t)
                    t = free[sl] = do("scalar", lambda e, sl=sl, n=n: e.activation(
                        ph[sl], bank[sl][:, 0:NQ + 1], ACT.Exp, bias=mxh[:, n:n + 1]), t, last("tensor"), last("scalar"))
                    for c, (lo, wd) in enumerate(((1, P), (1 + P, P), (0, 1))):
                        t2 = do("tensor", lambda e, sl=sl, c=c, lo=lo, wd=wd: e.transpose(
                            bank[2 + sl][0:wd, c * P:(c + 1) * P], ph[sl][:, lo:lo + wd], ident[:, :]), t, free[2 + sl], sig=c == 2)
                    do("vector", lambda e, sl=sl: e.tensor_copy(
                        pth[sl][:, 0:2], bank[2 + sl][:, 0:2 * P].rearrange("p (c q) -> p c q", q=P)), t2)
                    t = free[2 + sl] = do("vector", lambda e, sl=sl: e.tensor_copy(pth[sl][0:1, 2], bank[2 + sl][0:1, 2 * P:3 * P]))
                    ob = bank[4 + h // 4][:, (h % 4) * (DH + 1):(h % 4 + 1) * (DH + 1)]
                    for c in range(2):
                        do("tensor", lambda e, ob=ob, sl=sl, c=c, h=h: e.matmul(
                            ob, pth[sl][:, c], vh[:, c, h, :], start=c == 0, stop=False), t, t_v[-1], free[4 + h // 4], sig=False)
                    t_o = do("tensor", lambda e, ob=ob, sl=sl, h=h: e.matmul(
                        ob, pth[sl][0:1, 2], nullv[0:1, h, :], start=False, stop=True))
                    n += 1
                for c in range(2):
                    ov = bank[4 + c][:, 0:4 * (DH + 1)].rearrange("p (h d) -> p h d", d=DH + 1)
                    t = do("vector", lambda e, ov=ov, c=c: e.reciprocal(rcph[:, 4 * c:4 * c + 4], ov[:, :, DH]), t_o, last("vector"))
                    t = free[4 + c] = do("vector", lambda e, ov=ov, c=c: e.tensor_tensor(
                        ot_h.rearrange("p (h d) -> p h d", d=DH)[:, 4 * c:4 * c + 4], ov[:, :, 0:DH],
                        rcph[:, 4 * c:4 * c + 4].unsqueeze(2).broadcast_to([P, 4, DH]), ALU.mult), t, last("tensor"))
                for c in range(4):
                    t2 = do("tensor", lambda e, c=c: e.transpose(bank[6][:, c * P:(c + 1) * P], ot_h[:, c * P:(c + 1) * P], ident[:, :]),
                            t, free[6], sig=c == 3)
                t = free[6] = do("scalar", lambda e: e.activation(otT.rearrange("p c q -> p (c q)"), bank[6], ACT.Copy), t2)
                for c in range(4):
                    t2 = do("tensor", lambda e, c=c: e.matmul(bank[7][:, 0:D], otT[:, c], who[:, c, :], start=c == 0, stop=c == 3),
                            t, free[7], sig=c == 3)
                t = free[7] = do("vector", lambda e, half_=half_: e.tensor_scalar(
                    hout[:, half_], bank[7][:, 0:D], scb[:, half_:half_ + 1], None, ALU.mult), t2)
                t_sct = dma("gpsimd", f"scatter{half_}", lambda e, half_=half_: e.indirect_dma_start(
                    out=heavy_d, out_offset=bass.IndirectOffsetOnAxis(ap=idxb[:, 1, half_:half_ + 1], axis=0),
                    in_=hout[:, half_], in_offset=None), t, fill)
                if half_ == 0:
                    t_sct0 = t_sct

            t_n = layer_norm(pl, hvb, xn, small, 64, ld_h)
            ld_hv = dma("sync", "heavy", lambda e: e.dma_start(
                hvb[:, :, :], heavy_d.rearrange("(t p) d -> p t d", p=P)), t_sct, t_sct0, t_n[-1])
            t_hT = to_columns(pl, xn, t_n, hT, bank, ident, free, [0, 1, 2, 3], lambda k: cols[:, C_LNG + k:C_LNG + k + 1],
                              lambda k: cols[:, C_LNB + k:C_LNB + k + 1])
            t_ws = do("gpsimd", lambda e: e.tensor_tensor(
                wsc[:, 0:4], wlo[:, :, :], gates[:, 0].unsqueeze(1).broadcast_to([P, 4, D]), ALU.mult), ld_g)
            t = do("gpsimd", lambda e: e.tensor_tensor(
                hvb[:, :, :], hvb[:, :, :], gates[:, 0].unsqueeze(1).broadcast_to([P, T, D]), ALU.mult), ld_hv, ld_g)
            t_xh = do("gpsimd", lambda e: e.tensor_tensor(xt[:, :, :], xt[:, :, :], hvb[:, :, :], ALU.add), t, ld_x)

            qt = at(arena, 0, [H0 // 2, 2, N])
            kt = at(arena, 8192, [H0 // 2, NPAD])
            vt = at(arena, 8192 + 4 * NPAD, [T + 1, H0, DH + 1])
            t0 = last("tensor"), last("gpsimd"), last("scalar"), t_sct, t_sct0
            do("gpsimd", lambda e: e.memset(qt[0:DH, :, 1], 0.0), *t0)
            do("gpsimd", lambda e: e.memset(qt[DH:P, :, 0], 0.0), last("gpsimd"))
            t_z = do("gpsimd", lambda e: e.memset(vt[:, :, :, DH:DH + 1], 1.0), last("gpsimd"))
            kpad = do("vector", lambda e: e.memset(kt[:, :, 0:WIN], 0.0), *t0)
            kpad = do("vector", lambda e: e.memset(kt[:, :, WIN + N:NPAD], 0.0), *t0)
            nb = 0
            for m_ in range(8):
                for c in range(2):
                    bk = nb % 8
                    nb += 1
                    for k in range(KD):
                        t = do("tensor", lambda e, m_=m_, c=c, k=k, bk=bk: e.matmul(
                            bank[bk], wqkv[:, k, m_ * P:(m_ + 1) * P], hT[:, k, WIN + c * 512:WIN + (c + 1) * 512],
                            start=k == 0, stop=k == KD - 1), t_hT, free[bk], sig=k == KD - 1)
                    if m_ < 4:
                        do("scalar", lambda e, m_=m_, c=c, bk=bk: e.activation(
                            qt[0:DH, m_, 0, c * 512:(c + 1) * 512], bank[bk][0:DH], ACT.Copy, scale=DH ** -0.5), t, t0[4])
                        t = do("vector", lambda e, m_=m_, c=c, bk=bk: e.tensor_scalar(
                            qt[DH:P, m_, 1, c * 512:(c + 1) * 512], bank[bk][DH:P], DH ** -0.5, None, ALU.mult), t, t0[4])
                        free[bk] = [t, last("scalar")]
                        t_q = free[bk]
                    else:
                        eng = "scalar" if nb % 2 else "vector"
                        dst = kt[:, m_ - 4, WIN + c * 512:WIN + (c + 1) * 512]
                        free[bk] = do(eng, lambda e, dst=dst, bk=bk, eng=eng: copy(e, eng, dst, bank[bk]), t, *t0)
            for j in range(T + 1):
                bk = nb % 8
                nb += 1
                for k in range(KD):
                    t = do("tensor", lambda e, j=j, k=k, bk=bk: e.matmul(
                        bank[bk], hT[:, k, j * P:(j + 1) * P], wqkv[:, k, 2 * HD:3 * HD], start=k == 0, stop=k == KD - 1),
                        free[bk], sig=k == KD - 1)
                eng = "scalar" if nb % 2 else "vector"
                free[bk] = do(eng, lambda e, j=j, bk=bk, eng=eng: copy(
                    e, eng, vt[:, j, :, 0:DH], bank[bk].rearrange("p (h d) -> p h d", d=DH)), t, *t0)
            t_qkv = (last("scalar"), last("vector"), t_z)

            sm = [at(work, 256 * i, [2 * P]) for i in range(4)]
            pm = [at(work, 1024 + 256 * i, [2 * P]) for i in range(4)]
            pt = [at(work, 2048 + 256 * i, [2, P]) for i in range(4)]
            on = at(work, 3072, [HD])
            onT = at(work, 3584, [HD // P, P])
            nmx = small[:, 0:4]
            rcp = small[:, 8:16]
            st = {}

            def scores(s_):
                i, h = divmod(s_, H0)
                bk = s_ % 2
                t = do("tensor", lambda e: e.matmul(
                    bank[bk][:, 0:2 * P], qt[:, h // 2, h % 2, i * P:(i + 1) * P], kt[:, h // 2, i * P:i * P + 2 * P],
                    start=True, stop=True), free[bk], *t_qkv)
                mk = wmask[:, 0 if i == 0 else 2 if i == T - 1 else 1]
                t = free[bk] = do("vector", lambda e: e.tensor_tensor_reduce(
                    out=sm[s_ % 4], in0=bank[bk][:, 0:2 * P], in1=mk, scale=-1.0, scalar=3e38, op0=ALU.add, op1=ALU.min,
                    accum_out=nmx[:, s_ % 4:s_ % 4 + 1]), t, st.get(("exp", s_ - 4)))
                st["exp", s_] = do("scalar", lambda e: e.activation(
                    pm[s_ % 4], sm[s_ % 4], ACT.Exp, bias=nmx[:, s_ % 4:s_ % 4 + 1], scale=-1.0), t, st.get(("tr", s_ - 4)))

            def turn(s_):
                bk = 2 + s_ % 2
                for c in range(2):
                    t = do("tensor", lambda e, c=c: e.transpose(
                        bank[bk][:, c * P:(c + 1) * P], pm[s_ % 4][:, c * P:(c + 1) * P], ident[:, :]),
                        st["exp", s_], free[bk], sig=c == 1)
                st["tr", s_] = t
                eng = "scalar" if s_ % 2 else "vector"
                st["pt", s_] = free[bk] = do(eng, lambda e: copy(
                    e, eng, pt[s_ % 4].rearrange("p c q -> p (c q)"), bank[bk][:, 0:2 * P]), t, st.get(("pv", s_ - 4)))

            def weigh(s_):
                i, h = divmod(s_, H0)
                bk = 4 + h // 4
                for c in range(2):
                    t = do("tensor", lambda e, c=c: e.matmul(
                        bank[bk][:, (h % 4) * (DH + 1):(h % 4 + 1) * (DH + 1)], pt[s_ % 4][:, c], vt[:, i + c, h, :],
                        start=c == 0, stop=c == 1), st["pt", s_], free[bk], sig=c == 1)
                st["pv", s_] = t
                if h % 4 == 3:
                    c = h // 4
                    ov = bank[bk][:, 0:4 * (DH + 1)].rearrange("p (h d) -> p h d", d=DH + 1)
                    t = do("vector", lambda e: e.reciprocal(rcp[:, 4 * c:4 * c + 4], ov[:, :, DH]), t, st.get("on" + str(c)))
                    t = free[bk] = st["on" + str(c)] = do("vector", lambda e: e.tensor_tensor(
                        on.rearrange("p (h d) -> p h d", d=DH)[:, 4 * c:4 * c + 4], ov[:, :, 0:DH],
                        rcp[:, 4 * c:4 * c + 4].unsqueeze(2).broadcast_to([P, 4, DH]), ALU.mult), t, st.get("onT"))

            def project(i):
                for c in range(4):
                    t = do("tensor", lambda e, c=c: e.transpose(
                        bank[6][:, c * P:(c + 1) * P], on[:, c * P:(c + 1) * P], ident[:, :]),
                        st["on0"], st["on1"], free[6], sig=c == 3)
                st["onT"] = t
                t = free[6] = do("scalar", lambda e: e.activation(onT.rearrange("p c q -> p (c q)"), bank[6], ACT.Copy), t, st.get("out"))
                for c in range(4):
                    t = do("tensor", lambda e, c=c: e.matmul(
                        bank[7][:, 0:D], onT[:, c], wsc[:, c, :], start=c == 0, stop=c == 3), t, free[7], t_ws, sig=c == 3)
                st["out"] = t
                st["x", i] = free[7] = do("vector", lambda e: e.tensor_tensor(xt[:, i], xt[:, i], bank[7][:, 0:D], ALU.add), t, t_xh)

            total = T * H0
            for s_ in range(total + 5):
                if s_ < total:
                    scores(s_)
                if 0 <= s_ - 2 < total:
                    turn(s_ - 2)
                if 0 <= s_ - 3 < total:
                    weigh(s_ - 3)
                if s_ >= 12 and (s_ - 12) % H0 == 0:
                    project((s_ - 12) // H0)

            t_x = [st["x", i] for i in range(T)]
            t_n = layer_norm(pl, xt, xn, small, 64, dict(enumerate(t_x)))
            t_hT = to_columns(pl, xn, t_n, hT, bank, ident, free, [0, 1, 2, 3], lambda k: modcb[:, KD + k:KD + k + 1],
                              lambda k: modcb[:, k:k + 1], t_mc)
            t_ws = do("gpsimd", lambda e: e.tensor_tensor(wsc[:, 0], wfo[:, :], gates[:, 1], ALU.mult), last("tensor"))
            t_xb = add_bias(pl, xt, xn, wsc[:, 7], rows[:, R_BOUT:R_BOUT + D], gates[:, 1], t_n[-1])
            sT, rl, gT = at(arena, 0, [N]), [at(arena, 1024 + 1024 * i, [N]) for i in range(2)], at(arena, 3072, [N])
            t0 = last("tensor")
            for c in range(2):
                for k in range(KD):
                    t = do("tensor", lambda e, c=c, k=k: e.matmul(
                        bank[4 + c], win[:, k, :], hT[:, k, WIN + c * 512:WIN + (c + 1) * 512], start=k == 0, stop=k == KD - 1),
                        t_hT, free[4 + c], sig=k == KD - 1)
                t_s = free[4 + c] = do("scalar", lambda e, c=c: e.activation(
                    sT[:, c * 512:(c + 1) * 512], bank[4 + c], ACT.Identity, bias=cols[:, C_BIN:C_BIN + 1]), t, t0)
            t_g = do("vector", lambda e: e.tensor_copy(gT, cols[:, C_B2:C_B2 + 1].broadcast_to([P, N])), t0)
            rd = {}
            for j in range(INNER // 2):
                t = do("scalar", lambda e, j=j: e.activation(
                    rl[j % 2], sT, ACT.Relu, scale=cols[:, C_W1 + j:C_W1 + j + 1], bias=cols[:, C_B1 + j:C_B1 + j + 1]),
                    t_s, rd.get(j - 2))
                t_g = rd[j] = do("vector", lambda e, j=j: e.scalar_tensor_tensor(
                    out=gT, in0=rl[j % 2], scalar=cols[:, C_W2 + j:C_W2 + j + 1], in1=gT, op0=ALU.mult, op1=ALU.add), t, t_g)
            t_x = []
            for i in range(T):
                bk = i % 4
                t = do("tensor", lambda e, i=i, bk=bk: e.matmul(
                    bank[bk][:, 0:D], gT[:, i * P:(i + 1) * P], wsc[:, 0], start=True, stop=True), t_g, t_ws, free[bk])
                t = free[bk] = do("vector", lambda e, i=i, bk=bk: e.tensor_tensor(xt[:, i], xt[:, i], bank[bk][:, 0:D], ALU.add), t, t_xb)
                t_x.append(t)

            t_n = layer_norm(pl, xt, xn, small, 64, dict(enumerate(t_x)))
            t_hT = to_columns(pl, xn, t_n, hT, bank, ident, free, [0, 1, 2, 3], lambda k: modcb[:, 3 * KD + k:3 * KD + k + 1],
                              lambda k: modcb[:, 2 * KD + k:2 * KD + k + 1])
            t_ws = do("gpsimd", lambda e: e.tensor_tensor(
                wsc[:, 0:KD], wo1[:, :, :], gates[:, 2].unsqueeze(1).broadcast_to([P, KD, D]), ALU.mult), last("tensor"))
            t_xb = add_bias(pl, xt, xn, wsc[:, 7], rows[:, R_BO:R_BO + D], gates[:, 2], t_n[-1])
            QC, T1, T2 = at(arena, 0, [T, 2 * D]), at(arena, 4096, [T, 2 * D]), at(arena, 8192, [T, 2 * D])
            v1 = at(arena, 12288, [T, H1, 2 * HD1])
            t0 = last("tensor"), last("vector"), last("scalar")
            t_vz = do("gpsimd", lambda e: e.memset(v1[:, :, :, HD1:2 * HD1], 0.0), *t0)
            t_vo = do("gpsimd", lambda e: e.memset(v1[:, :, :, HD1:HD1 + 1], 1.0), t_vz)
            nb = 4
            for i in range(T):
                bk = nb % 8
                nb += 1
                for k in range(KD):
                    t = do("tensor", lambda e, i=i, k=k, bk=bk: e.matmul(
                        bank[bk], hT[:, k, WIN + i * P:WIN + (i + 1) * P], wqk1[:, k, :], start=k == 0, stop=k == KD - 1),
                        t_hT, free[bk], sig=k == KD - 1)
                do("scalar", lambda e, i=i, bk=bk: e.activation(T1[:, i], bank[bk], ACT.Square), t, *t0)
                free[bk] = t_qc = do("scalar", lambda e, i=i, bk=bk: e.activation(QC[:, i], bank[bk], ACT.Copy), t, *t0)
                bk = nb % 8
                nb += 1
                for k in range(KD):
                    t = do("tensor", lambda e, i=i, k=k, bk=bk: e.matmul(
                        bank[bk][:, 0:D], hT[:, k, WIN + i * P:WIN + (i + 1) * P], wv1[:, k, :], start=k == 0, stop=k == KD - 1),
                        free[bk], sig=k == KD - 1)
                free[bk] = t_v = do("vector", lambda e, i=i, bk=bk: e.tensor_copy(
                    v1[:, i, :, 0:HD1], bank[bk][:, 0:D].rearrange("p (h d) -> p h d", d=HD1)), t, *t0)
            hs = at(small, 256, [T * 2 * H1])
            t = do("vector", lambda e: e.tensor_reduce(hs, T1.rearrange("p t (h d) -> p (t h) d", d=HD1), AX_X, ALU.add), t_qc)
            t = do("vector", lambda e: e.tensor_scalar(hs, hs, 1.0 / HD1, 1e-5, ALU.mult, ALU.add), t)
            t = do("scalar", lambda e: e.activation(hs, hs, ACT.Sqrt), t)
            t_rs = do("vector", lambda e: e.reciprocal(hs, hs), t)
            for i in range(2):
                x4, a4, b4 = (v[:, :, i * D:(i + 1) * D].rearrange("p t (h d) -> p t h d", d=HD1) for v in (QC, T1, T2))
                tb = lambda v, lo, hi, i=i: v[:, i, :, lo:hi].unsqueeze(2).broadcast_to([P, T, H1, hi - lo])
                do("vector", lambda e, x4=x4, a4=a4, c=tb(tabA, 0, HD1): e.tensor_tensor(a4, x4, c, ALU.mult), t_rs)
                do("gpsimd", lambda e, x4=x4, b4=b4, c=tb(tabB, 0, half): e.tensor_tensor(
                    b4[:, :, :, 0:half], x4[:, :, :, 1:HD1:2], c, ALU.mult), t_qc)
                t_b = do("gpsimd", lambda e, x4=x4, b4=b4, c=tb(tabB, half, HD1): e.tensor_tensor(
                    b4[:, :, :, half:HD1], x4[:, :, :, 0:HD1:2], c, ALU.mult), t_qc)
            t = last("vector")
            t = do("vector", lambda e: e.tensor_tensor(T1, T1, T2, ALU.add), t, t_b)
            t = do("vector", lambda e: e.tensor_tensor(
                T1.rearrange("p t (h d) -> p (t h) d", d=HD1), T1.rearrange("p t (h d) -> p (t h) d", d=HD1),
                hs.unsqueeze(2).broadcast_to([P, T * 2 * H1, HD1]), ALU.mult), t)
            for i in range(2):
                q4, a4 = (v[:, :, i * D:(i + 1) * D].rearrange("p t (h d) -> p t h d", d=HD1) for v in (QC, T1))
                t_r = do("vector", lambda e, q4=q4, a4=a4, c=tabC[:, i].unsqueeze(2).broadcast_to([P, T, H1, HD1]):
                         e.tensor_tensor(q4, a4, c, ALU.add), t)
            parts = [at(arena, 8192, [4, N], BF16), at(arena, 10240, [4, N], BF16),
                     at(hvb[:, :, :].rearrange("p t d -> p (t d)"), 0, [4, N], BF16)]
            t_pt = [None] * 3
            for c in range(4):
                for hf in range(2):
                    bk = nb % 8
                    nb += 1
                    for i in range(4):
                        t = do("tensor", lambda e, c=c, hf=hf, i=i, bk=bk: e.transpose(
                            bank[bk][:, i * P:(i + 1) * P], QC[:, 4 * hf + i, c * P:(c + 1) * P], ident[:, :]),
                            t_r, free[bk], sig=i == 3)
                    hi, mi, lo = (v[:, c, hf * 512:(hf + 1) * 512] for v in parts)
                    rr = T1.rearrange("p t d -> p (t d)")[:, (2 * c + hf) * 512:(2 * c + hf + 1) * 512]
                    t1 = do("scalar", lambda e, hi=hi, bk=bk: e.activation(hi, bank[bk], ACT.Copy), t, t_r)
                    t2 = free[bk] = do("vector", lambda e, hi=hi, bk=bk, rr=rr: e.tensor_tensor(rr, bank[bk], hi, ALU.subtract), t1, t)
                    t3 = do("scalar", lambda e, mi=mi, rr=rr: e.activation(mi, rr, ACT.Copy), t2)
                    t4 = do("vector", lambda e, mi=mi, lo=lo, rr=rr: e.tensor_tensor(lo, rr, mi, ALU.subtract), t3)
            t_sp = [t1, t3, t4]
            st_p = []
            for i in range(3):
                st_p.append(dma("sync", f"split{i}", lambda e, i=i: e.dma_start(
                    split_d[i].rearrange("(c p) n -> p c n", p=P), parts[i]), t_sp[i]))
            QROWS, KROWS = (0, 1, 0, 1, 0, 2), (0, 0, 1, 1, 2, 0)
            qa = at(arena, 0, [2, G1, N], BF16)
            ka = at(arena, 4096, [2, G1, N], BF16)
            t_one = do("vector", lambda e: e.memset(ka[KS:KA], 1.0), last("tensor"), last("scalar"), last("vector"))
            t_all = last("tensor"), last("scalar"), last("vector")
            t_grp, t_max, t_p2 = {}, {}, {}

            def load_group(g):
                for r in range(6):
                    for dst, off_, pr in ((qa, 0, QROWS[r]), (ka, D, KROWS[r])):
                        t_grp[g] = dma("sync", f"group{g % 2}", lambda e, g=g, r=r, dst=dst, off_=off_, pr=pr: e.dma_start(
                            dst[r * HD1:(r + 1) * HD1, g % 2],
                            split_d[pr, off_ + g * G1 * HD1:off_ + (g + 1) * G1 * HD1, :].rearrange("(h d) n -> d h n", d=HD1)),
                            *st_p, *t_all, t_p2.get(g - 2), t_p2.get(("m", g - 2)))

            nm = [at(small, 256 + 64 * i, [G1, T, 2]) for i in range(2)]
            nmf = [at(small, 384 + 32 * i, [G1 * T]) for i in range(2)]
            mhi = [at(small, 448 + 64 * i, [P], BF16) for i in range(1)]
            mmi = [at(small, 512 + 64 * i, [P], BF16) for i in range(1)]

            def max_units(g):
                first = [None]

                def unit(h, i, c):
                    w_ = min(512, (i + 1) * P - c * 512)
                    diag = c * 512 + w_ == (i + 1) * P
                    bk = 6 + st.setdefault("mb", 0) % 2
                    st["mb"] += 1
                    if diag:
                        do("tensor", lambda e: e.matmul(
                            bank[bk][:, w_ - P:w_], identb[:, :], cmask[:, :], start=True, stop=True), t_grp[g], free[bk], sig=False)
                    t = do("tensor", lambda e: e.matmul(
                        bank[bk][:, 0:w_], qa[0:KS, g % 2, h, i * P:(i + 1) * P], ka[0:KS, g % 2, h, c * 512:c * 512 + w_],
                        start=not diag, stop=True, skip_group_check=True), t_grp[g], free[bk])
                    free[bk] = do("vector", lambda e: e.tensor_reduce(
                        nm[g % 2][:, h, i, c:c + 1], bank[bk][:, 0:w_], AX_X, ALU.max, negate=True), t, first[0])

                def begin():
                    first[0] = do("vector", lambda e: e.memset(nm[g % 2], 3e38), t_max.get(("n", g - 2)), t_p2.get("hs"))

                def end():
                    t = do("vector", lambda e: e.tensor_tensor(
                        nmf[g % 2].rearrange("p (h t) -> p h t", t=T), nm[g % 2][:, :, :, 0], nm[g % 2][:, :, :, 1], ALU.min),
                        last("vector"), t_max.get(("n", g - 2)))
                    t = t_max["n", g] = do("tensor", lambda e: e.transpose(bank[5][0:G1 * T, 0:P], nmf[g % 2], ident[:, :]), t, free[5])
                    t1 = do("scalar", lambda e: e.activation(mhi[0][0:G1 * T], bank[5][0:G1 * T, 0:P], ACT.Copy), t, t_max.get(("st", g - 1)))
                    t2 = free[5] = do("vector", lambda e: e.tensor_tensor(
                        mmi[0][0:G1 * T], bank[5][0:G1 * T, 0:P], mhi[0][0:G1 * T], ALU.subtract), t1, t_max.get(("st", g - 1)))
                    ta = dma("sync", f"max_out{g}", lambda e: e.dma_start(max_d[0, g], mhi[0][0:G1 * T]), t1)
                    ta = t_max["st", g] = dma("sync", f"max_out{g}", lambda e: e.dma_start(max_d[1, g], mmi[0][0:G1 * T]), t2)
                    for r in range(2):
                        t_max[g] = dma("sync", f"max_in{g}", lambda e, r=r: e.dma_start(
                            qa[KS + r:KS + r + 1, g % 2].rearrange("o h n -> o (h n)"),
                            max_d[r, g:g + 1].rearrange("o q n -> o (q n)")), ta, t_grp[g], t_p2.get(g - 2))

                units = [lambda h=h, i=i, c=c: unit(h, i, c) for h in range(G1) for i in range(T) for c in range(2) if c * 4 <= i]
                return begin, units, end

            pp = [at(work, 1024 * i, [2, 512]) for i in range(4)]
            og = [at(wsc[:, :, :].rearrange("p a b -> p (a b)"), 512 + 512 * i, [512]) for i in range(2)]
            oc = at(xn[:, :, :].rearrange("p a b -> p (a b)"), 0, [T, D])
            npp = [0]

            def attend(g, c, kt_):
                q0 = max(kt_ * P, c * 512)
                w_ = (c + 1) * 512 - q0
                tp = []
                for pr in range(2):
                    sl = npp[0] % 4
                    db = npp[0] % 2
                    npp[0] += 1
                    for j in range(2):
                        h = 2 * pr + j
                        t = do("tensor", lambda e, h=h, j=j, db=db: e.matmul(
                            pb2[db][:, j, 0:w_], ka[0:KA, g % 2, h, kt_ * P:(kt_ + 1) * P], qa[0:KA, g % 2, h, q0:q0 + w_],
                            start=True, stop=True), t_max[g], t_one, free[2 * db], sig=j == 1)
                    t = free[2 * db] = free[2 * db + 1] = do("scalar", lambda e, sl=sl, db=db: e.activation(
                        pp[sl][:, :, 0:w_], pb2[db][:, :, 0:w_], ACT.Exp), t, st.get(("pp", sl)))
                    if q0 == kt_ * P:
                        t = do("gpsimd", lambda e, sl=sl: e.affine_select(
                            out=pp[sl][:, :, 0:P], in_=pp[sl][:, :, 0:P], pattern=[[0, 2], [1, P]], compare_op=ALU.is_ge,
                            fill=0.0, base=0, channel_multiplier=-1), t)
                    tp.append((sl, t))
                last_kt = kt_ == 4 * c + 3
                return lambda: weigh1(g, c, kt_, q0, w_, tp, last_kt)

            def weigh1(g, c, kt_, q0, w_, tp, last_kt):
                for pr, (sl, t) in enumerate(tp):
                    for j in range(2):
                        h = 2 * pr + j
                        t2 = do("tensor", lambda e, h=h, j=j, sl=sl: e.matmul(
                            bank[4][32 * h:32 * h + 32, q0 - c * 512:512], v1[:, kt_, G1 * g + h, :], pp[sl][:, j, 0:w_],
                            start=kt_ == 0, stop=kt_ >= 4 * c, skip_group_check=True), t, free[4], t_vo, sig=j == 1)
                    st["pp", sl] = t2
                if last_kt:
                    sl = c
                    t = free[4] = do("scalar", lambda e: e.activation(og[sl], bank[4], ACT.Copy), t2, st.get(("og", sl)))
                    for i in range(4):
                        t2 = do("tensor", lambda e, i=i: e.transpose(bank[5][:, i * P:(i + 1) * P], og[sl][:, i * P:(i + 1) * P], ident[:, :]),
                                t, free[5], sig=i == 3)
                    st["og", sl] = t2
                    ov = bank[5].rearrange("p (t h d) -> p t h d", h=G1, d=2 * HD1)
                    rc = small[:, 16 * c:16 * c + 16].rearrange("p (t h) -> p t h", h=G1)
                    t = do("vector", lambda e: e.reciprocal(rc, ov[:, :, :, HD1]), t2, st.get(("rc", c)))
                    t = free[5] = st["rc", c] = do("vector", lambda e: e.tensor_tensor(
                        oc[:, 4 * c:4 * c + 4, g * G1 * HD1:(g + 1) * G1 * HD1].rearrange("p t (h d) -> p t h d", d=HD1),
                        ov[:, :, :, 0:HD1], rc.unsqueeze(3).broadcast_to([P, 4, G1, HD1]), ALU.mult), t)
                    st["oc"] = t
                    if c == 1:
                        t_p2[g] = last("tensor")

            load_group(0)
            load_group(1)
            begin, units, end = max_units(0)
            begin()
            for u_ in units:
                u_()
            end()
            for g in range(NG):
                nxt = []
                if g + 1 < NG:
                    begin, nxt, end = max_units(g + 1)
                    begin()
                t_p2["m", g] = last("tensor")
                behind = None
                for n, (c, kt_) in enumerate([(c, k_) for c in range(2) for k_ in range(4 * c + 4)]):
                    w_now = attend(g, c, kt_)
                    for u_ in nxt[4 * n:4 * n + 4]:
                        u_()
                    if behind:
                        behind()
                    behind = w_now
                behind()
                if nxt:
                    end()
                if g + 2 < NG:
                    load_group(g + 2)
            ocT = at(arena, 8192, [KD, N])
            t_x = []
            for c in range(2):
                for k in range(KD):
                    bk = 2 * c + k
                    for i in range(4):
                        t = do("tensor", lambda e, c=c, k=k, i=i, bk=bk: e.transpose(
                            bank[bk][:, i * P:(i + 1) * P], oc[:, 4 * c + i, k * P:(k + 1) * P], ident[:, :]),
                            st["oc"], free[bk], sig=i == 3)
                    t_oc = free[bk] = do("scalar", lambda e, c=c, k=k, bk=bk: e.activation(
                        ocT[:, k, c * 512:(c + 1) * 512], bank[bk], ACT.Copy), t, *st_p)
            for i in range(T):
                bk = 4 + i % 4
                for k in range(KD):
                    t = do("tensor", lambda e, i=i, k=k, bk=bk: e.matmul(
                        bank[bk][:, 0:D], ocT[:, k, i * P:(i + 1) * P], wsc[:, k], start=k == 0, stop=k == KD - 1),
                        t_oc, t_ws, free[bk], sig=k == KD - 1)
                t_x.append(do("vector", lambda e, i=i, bk=bk: e.tensor_tensor(xt[:, i], xt[:, i], bank[bk][:, 0:D], ALU.add), t, t_xb))
                free[bk] = t_x[-1]

            t_n = layer_norm(pl, xt, xn, small, 64, dict(enumerate(t_x)))
            t_hT = to_columns(pl, xn, t_n, hT, bank, ident, free, [0, 1, 2, 3], lambda k: modcb[:, 5 * KD + k:5 * KD + k + 1],
                              lambda k: modcb[:, 4 * KD + k:4 * KD + k + 1])
            t_ws = do("gpsimd", lambda e: e.tensor_tensor(
                wsc[:, :, :], w2T[:, :, :], gates[:, 3].unsqueeze(1).broadcast_to([P, FT, D]), ALU.mult), last("tensor"))
            t_xb = add_bias(pl, xt, xn, small[:, 256:512], rows[:, R_B2:R_B2 + D], gates[:, 3], t_n[-1], last("tensor"))
            g1 = at(arena, 0, [FT, N])
            t0 = last("tensor")
            for m_ in range(FT):
                for c in range(2):
                    bk = (2 * m_ + c) % 4 + 4
                    for k in range(KD):
                        t = do("tensor", lambda e, m_=m_, c=c, k=k, bk=bk: e.matmul(
                            bank[bk], w1T[:, k, m_ * P:(m_ + 1) * P], hT[:, k, WIN + c * 512:WIN + (c + 1) * 512],
                            start=k == 0, stop=k == KD - 1), t_hT, free[bk], sig=k == KD - 1)
                    t_g = free[bk] = do("scalar", lambda e, m_=m_, c=c, bk=bk: e.activation(
                        g1[:, m_, c * 512:(c + 1) * 512], bank[bk], ACT.Gelu, bias=cols[:, C_FB1 + m_:C_FB1 + m_ + 1]), t, t0)
            for i in range(T):
                bk = i % 4
                for k in range(FT):
                    t = do("tensor", lambda e, i=i, k=k, bk=bk: e.matmul(
                        bank[bk][:, 0:D], g1[:, k, i * P:(i + 1) * P], wsc[:, k], start=k == 0, stop=k == FT - 1),
                        t_g, t_ws, free[bk], sig=k == FT - 1)
                t = free[bk] = do("vector", lambda e, i=i, bk=bk: e.tensor_tensor(xt[:, i], xt[:, i], bank[bk][:, 0:D], ALU.add), t, t_xb)
            dma("sync", "out", lambda e: e.dma_start(out[b].rearrange("(t p) d -> p t d", p=P), xt[:, :, :]), t)
            pl.emit(nc)


def copy(e, engine, dst, src):
    return e.activation(dst, src, ACT.Copy) if engine == "scalar" else e.tensor_copy(dst, src)


def to_columns(pl, xn, t_n, hT, bank, ident, free, banks, scale, bias, *ready):
    out = []
    for c in range(2):
        for k in range(KD):
            bk = banks[2 * c + k]
            for i in range(4):
                t = pl.do("tensor", lambda e, c=c, k=k, i=i, bk=bk: e.transpose(
                    bank[bk][:, i * P:(i + 1) * P], xn[:, 4 * c + i, k * P:(k + 1) * P], ident[:, :]),
                    t_n[4 * c + i], free[bk], sig=i == 3)
            dst = hT[:, k, WIN + c * 512:WIN + (c + 1) * 512]
            if (2 * c + k) % 2:
                free[bk] = pl.do("vector", lambda e, k=k, bk=bk, dst=dst: e.tensor_scalar(
                    dst, bank[bk], scale(k), bias(k), ALU.mult, ALU.add), t, *ready)
            else:
                free[bk] = pl.do("scalar", lambda e, k=k, bk=bk, dst=dst: e.activation(
                    dst, bank[bk], ACT.Identity, scale=scale(k), bias=bias(k)), t, *ready)
            out.append(free[bk])
    return out


def add_bias(pl, xt, xn, tmp, bias, gate, *after):
    t = pl.do("gpsimd", lambda e: e.tensor_tensor(tmp, bias, gate, ALU.mult), *after)
    return pl.do("gpsimd", lambda e: e.tensor_tensor(xt[:, :, :], xt[:, :, :], tmp.unsqueeze(1).broadcast_to([P, T, D]), ALU.add), t, *after)


def pl_last(pl, engine):
    n = pl.count.get(engine, 0)
    return (engine, n) if n else None


def layer_norm(pl, src, dst, small, c0, *ready, rows=D, tiles=T):
    do = pl.do
    st = small[:, c0:c0 + 6 * tiles].rearrange("p (t s) -> p t s", s=6)
    mv = small[:, c0 + 6 * tiles:c0 + 8 * tiles].rearrange("p (t s) -> p t s", s=2)
    rs = small[:, c0 + 8 * tiles:c0 + 9 * tiles]
    ex = small[:, c0 + 9 * tiles:c0 + 10 * tiles]
    t_e = do("gpsimd", lambda e: e.memset(ex, -0.5), pl_last(pl, "gpsimd"))
    for i in range(tiles):
        t = do("vector", lambda e, i=i: e.bn_stats(st[:, i], src[:, i]),
               *[r[i] if isinstance(r, dict) else r for r in ready])
        t_a = do("vector", lambda e, i=i: e.bn_aggr(mv[:, i], st[:, i]), t)
    t = do("vector", lambda e: e.tensor_scalar(rs, mv[:, :, 1], 1e-5, None, ALU.add), t_a)
    t = do("gpsimd", lambda e: e.tensor_tensor(rs, rs, ex, ALU.pow), t, t_e)
    return [do("vector", lambda e, i=i: e.tensor_scalar(dst[:, i], src[:, i], mv[:, i, 0:1], rs[:, i:i + 1],
                                                        ALU.subtract, ALU.mult), t) for i in range(tiles)]



def kernel(**inputs):
    import concourse.bacc as bacc
    from concourse.bass_utils import run_bass_kernel_spmd

    x = {k: np.asarray(v) for k, v in inputs.items()}
    p = lambda n: x["L0_attn_" + n]
    f, q, m = (lambda n: x["L0_ffn_" + n]), (lambda n: x["L1_attn_" + n]), (lambda n: x["L1_ffn_" + n])
    f32 = np.float32
    two = lambda v: v.reshape(2, P).T
    pair = lambda w: w.reshape(MU, INNER // 2, 2).transpose(2, 0, 1).reshape(P, INNER // 2)
    arrays = {
        "x": x["L0_attn_x"],
        "cT": np.stack([x[n].T.reshape(KD, P, B).transpose(1, 0, 2) for n in ("L0_c", "L1_c")], 1),
        "wmod0": x["L0_wmod"], "wmod1": x["L1_wmod"],
        "wqkv": p("light_qkv_w"), "wlo": p("light_out_w"), "whq": p("heavy_q_w"),
        "whk": p("heavy_kv_w")[:, :DH].transpose(2, 0, 1).reshape(D, HD),
        "whv": p("heavy_kv_w")[:, DH:].transpose(2, 0, 1).reshape(D, HD),
        "who": p("heavy_out_w"),
        "nullk": p("heavy_null_kv")[0].reshape(H0 // 2, P).T,
        "null_v": p("heavy_null_kv")[1].reshape(1, H0, DH),
        "win": np.concatenate([f("Win"), f("Win")], 1),
        "wfo": np.concatenate([f("Wout"), f("Wout")], 0),
        "wqk1": np.concatenate([q("Wq").T, q("Wk").T], 1), "wv1": q("Wv").T, "wo1": q("Wo").T,
        "w1": m("w1"), "w2": m("w2"),
        "cols": np.concatenate([two(p("ln_gamma")), two(p("ln_beta")), two(p("heavy_gamma")),
                                np.tile(f("bin_"), 2)[:, None], pair(f("W1")), pair(f("b1")), pair(f("W2")),
                                np.concatenate([f("b2"), np.zeros(MU, f32)])[:, None], m("b1").reshape(FT, P).T], 1),
        "rows": np.concatenate([p("q_route_tok"), p("kv_route_tok"), p("null_q_token"), f("bout"), q("bo"), m("b2"),
                                q("q_gamma"), q("q_beta"), q("k_gamma"), q("k_beta")])[None],
    }
    i = np.arange(P)
    c = np.arange(2 * P)
    band = (c[None] >= i[:, None]) & (c[None] - i[:, None] <= 2 * WIN)
    first, last = band & (c[None] >= WIN), band & (c[None] < 3 * WIN)
    pos = np.arange(N, dtype=f32)[:, None]
    th = pos * np.exp(-(np.arange(0, HD1, 2, dtype=f32) / f32(HD1)) * f32(math.log(10000.0))).astype(f32)
    sign1 = np.where(np.arange(HD1) < HD1 // 2, -1, 1).astype(f32)
    r1 = np.stack([np.repeat(np.cos(th), 2, 1), np.repeat(np.sin(th), 2, 1) * sign1])
    fr = pos * (f32(1.0) / f32(10000.0) ** (np.arange(0, DH, 2, dtype=f32) / f32(DH))).astype(f32)
    fr = np.concatenate([fr, fr], 1)
    sign0 = np.where(np.arange(DH) < DH // 2, -1, 1).astype(f32)
    arrays |= {
        "ident": np.eye(P, dtype=f32),
        "wmask": np.where(np.stack([first, band, last], 1), 0, NEG).astype(f32),
        "cmask": np.where(i[None] > i[:, None], NEG, 0).astype(f32),
        "rope1": r1.reshape(2, T, P, HD1).transpose(2, 0, 1, 3).astype(f32),
        "rope0": np.concatenate([np.cos(fr), np.sin(fr) * sign0], 1).astype(f32),
        "group": (i[:, None] // T == i[None] // T).astype(f32),
        "lower": ((i[:, None] // T == i[None] // T) & (i[:, None] < i[None])).astype(f32),
        "iota": np.arange(NQ, dtype=f32)[None],
        "tokv": (np.arange(T)[None] * P + i[:, None]).astype(f32),
        "rowoff": (np.arange(4 * B) // 4 * N).astype(f32)[None],
    }
    arrays = {n: np.ascontiguousarray(v) for n, v in arrays.items()}
    nc = bacc.Bacc("TRN2", target_bir_lowering=False, num_devices=1)
    aps = {n: nc.dram_tensor("in_" + n, v.shape, mybir.dt.from_np(v.dtype), kind="ExternalInput").ap() for n, v in arrays.items()}
    out = nc.dram_tensor("y", (B, N, D), F32, kind="ExternalOutput").ap()
    adaln_kernel(nc, aps, out)
    r = run_bass_kernel_spmd(nc, [{"in_" + n: v for n, v in arrays.items()}], core_ids=[0])
    return r.results[0]["y"]
```

```python
from contextlib import ExitStack
import math

import numpy as np

import concourse.bass as bass
from concourse import mybir

F32 = mybir.dt.float32
BF16 = mybir.dt.bfloat16
I32 = mybir.dt.int32
U32 = mybir.dt.uint32
ALU = mybir.AluOpType
ACT = mybir.ActivationFunctionType
AX_X = mybir.AxisListType.X

P = 128
B, N, D = 8, 1024, 256
T = N // P
KD = D // P
H0, DH = 8, 64
HD = H0 * DH
WIN = 64
NPAD = N + 2 * WIN
NQ = 256
NITER, EPS, EPS0, DECAY = 20, 0.03, 4.0, 0.7
EFF_K = min(NQ * 9.0 / 8.0, N)
H1, HD1 = 16, 16
G1 = 4
NG = H1 // G1
KS = 6 * HD1
KA = KS + 2
F1 = 1024
FT = F1 // P
NH, TH = N // 2, T // 2
ZONE_B = 13648
ARENA = 22864
PACE = ((1.0, 1.1, 0.9, 2.0), (0.95, 0.7, 0.9, 2.2))
WAIT_HV = 6
MU, INNER = 64, 16
NEG = -1e30
LOG_K = math.log(max(EFF_K, 1e-20))
FLOOR_EXP = 87.4

C_LNG, C_LNB, C_HG, C_BIN, C_W1, C_B1, C_W2, C_B2, C_FB1 = 0, 2, 4, 6, 7, 15, 23, 31, 32
NCOLS = 40
R_NULL, R_BOUT, R_BO, R_B2 = (i * D for i in range(4))
R_GB = 4 * D
NROWS = R_GB + 4 * HD1


class Plan:

    ENGINES = ("tensor", "vector", "scalar", "gpsimd", "sync")

    def __init__(self, sems, dma_sems):
        self.sems, self.dma_sems = sems, dma_sems
        self.queue = {e: [] for e in self.ENGINES}
        self.pool_dmas = set()
        self.kept = {}
        self.pending = {}
        self.partial = None
        self.count, self.seen, self.used = {}, {e: {} for e in self.ENGINES}, {}

    def fence(self, tokens):
        self.pending = {e: self.pending.get(e, []) + tokens for e in self.ENGINES[:4]}

    def _waits(self, engine, waits):
        need = {}
        waits = (*waits, self.pending.pop(engine, None))
        for w in waits:
            for sem, value in (w if isinstance(w, list) else [w]) if w is not None else []:
                if self.seen[engine].get(sem, 0) < value:
                    need[sem] = max(need.get(sem, 0), value)
        self.seen[engine].update(need)
        return list(need.items())

    def do(self, engine, fn, *waits, sig=True):
        if engine == "gpsimd":
            waits, self.partial = (*waits, self.partial), None
        need = self._waits(engine, waits)
        token = None
        if sig:
            self.count[engine] = self.count.get(engine, 0) + 1
            token = (engine, self.count[engine])
        self.queue[engine].append((fn, need, self.sems[engine] if sig else None, 1))
        return token

    def dma(self, engine, name, fn, *waits):
        need = self._waits(engine, waits)
        if name not in self.used:
            self.used[name] = self.dma_sems[len(self.used)]
        if engine == "gpsimd":
            self.pool_dmas.add(name)
        self.count[name] = self.count.get(name, 0) + 16
        self.queue[engine].append((fn, need, self.used[name], 16))
        return (name, self.count[name])

    def emit(self, nc):
        last = [(n, self.count[n]) for n in self.used]
        self.queue["sync"].append((None, self._waits("sync", last), None, 0))
        pool_last = [(n, self.count[n]) for n in sorted(self.pool_dmas)]
        self.queue["gpsimd"].append((None, self._waits("gpsimd", pool_last), None, 0))
        with nc.Block() as block:
            for name in self.ENGINES:
                def program(eng, name=name):
                    for fn, need, sem, by in self.queue[name]:
                        for s, v in need:
                            eng.wait_ge(self.sems[s] if s in self.sems else self.used[s], v)
                        if fn is not None:
                            ins = fn(eng)
                            if sem is not None:
                                ins.then_inc(sem, by)
                block_on = {"tensor": block.tensor, "vector": block.vector, "scalar": block.scalar,
                            "gpsimd": block.gpsimd, "sync": block.sync}[name]
                block_on(program)
        every = [*self.sems.values(), *self.dma_sems]
        used = range(min(s.num for s in every), max(s.num for s in every) + 1)
        if self.pool_dmas:
            nc.gpsimd.dma_reset(used)
        nc.gpsimd.sem_clear(used)
        nc.all_engine_barrier()


def adaln_kernel(nc, a, out):
    ctx = ExitStack()
    with ctx:
        def sb(name, shape, dt=F32):
            return ctx.enter_context(nc.sbuf_tensor(name, shape, dt))

        def dram(name, shape, dt=F32):
            return nc.dram_tensor(name, shape, dt, kind="Internal").ap()

        sems = {e: ctx.enter_context(nc.semaphore(f"done_{e}")) for e in Plan.ENGINES}
        dma_sems = [ctx.enter_context(nc.semaphore(f"landed_{i}")) for i in range(64)]

        mod_d = dram("mod_d", (B, 12 * D))
        h_d = dram("h_d", ((B + 1) * N, D))
        heavy_d = dram("heavy_d", (N, D))
        split_q = dram("split_q", (H1, 6, HD1, N), BF16)
        split_k = dram("split_k", (H1, 3, HD1, N), BF16)

        ident = sb("ident", [P, P])
        identb = sb("identb", [P, P], BF16)
        wmask = sb("wmask", [P, 3, 2 * P])
        cmask = sb("cmask", [P, P], BF16)
        cols = sb("cols", [P, NCOLS])
        rows = sb("rows", [P, NROWS])
        modc = sb("modc", [P, 6 * KD, B])
        wqkv = sb("wqkv", [P, KD, 3 * HD])
        wlo = sb("wlo", [P, HD // P, D])
        whq = sb("whq", [P, KD, HD])
        whk = sb("whk", [P, KD, HD])
        whv = sb("whv", [P, KD, HD])
        who = sb("who", [P, HD // P, D])
        nullk = sb("nullk", [P, H0 // 2])
        nullv = sb("nullv", [1, H0, DH])
        win = sb("win", [P, KD, P])
        wfo = sb("wfo", [P, D])
        wqk1 = sb("wqk1", [P, KD, 2 * D])
        wv1 = sb("wv1", [P, KD, D])
        wo1 = sb("wo1", [P, KD, D])
        w1T = sb("w1T", [P, KD, F1])
        w2T = sb("w2T", [P, FT, D])
        tabA = sb("tabA", [P, 2, T, HD1])
        tabB = sb("tabB", [P, 2, T, HD1])
        tabC = sb("tabC", [P, 2, T, HD1])
        idx_all = sb("idx_all", [P, 2, 4 * B], U32)
        sc_all = sb("sc_all", [P, 4 * B])

        xt = sb("xt", [P, T, D])
        xn = sb("xn", [P, T, D])
        hTf = sb("hTf", [P, KD * NPAD])
        hT = hTf[:, :].rearrange("p (k n) -> p k n", k=KD)
        gates = sb("gates", [P, 4, D])
        v1 = sb("v1", [P, T, H1, HD1 + 1])
        xh = sb("xh", [P, KD * NH + 2 * D])
        small = sb("small", [P, 640])
        arena = sb("arena", [P, ARENA])

        def at(base, start, shape, dt=F32):
            n = int(np.prod(shape))
            words = n if dt != BF16 else n // 2
            v = base[:, start:start + words]
            if dt != F32:
                v = v.bitcast(dt)
            names = " ".join(f"x{i}" for i in range(len(shape)))
            return v.rearrange(f"p ({names}) -> p {names}", **{f"x{i}": s for i, s in enumerate(shape)})

        pb2 = [ctx.enter_context(nc.psum_tensor(f"pb{i}", [P, 2, 512], F32)) for i in range(4)]
        bank = [pb2[i // 2][:, i % 2, :] for i in range(8)]

        pl = Plan(sems, dma_sems)
        do, dma = pl.do, pl.dma
        free = [None] * 8

        for dst, src in ((ident[:, :], a["ident"]), (wmask[:, :, :], a["wmask"]), (cols[:, :], a["cols"]),
                         (rows[:, :], a["rows"].partition_broadcast(P))):
            ld_c = dma("sync", "consts", lambda e, dst=dst, src=src: e.dma_start(dst, src))
        cmf = at(arena, 15000, [P])
        ld_c = dma("sync", "consts", lambda e: e.dma_start(cmf, a["cmask"]))
        rope1 = at(arena, 15200, [2, T, HD1])
        ld_c = dma("sync", "consts", lambda e: e.dma_start(rope1, a["rope1"]))
        toks = at(arena, 16640, [2, D])
        ld_c = dma("sync", "consts", lambda e: e.dma_start(toks.rearrange("p r d -> p (r d)"), a["toks"].partition_broadcast(P)))
        cT = at(arena, 15600, [2, KD, B])
        ld_c = dma("sync", "consts", lambda e: e.dma_start(cT, a["cT"]))
        wmod = at(arena, 0, [2, KD, 6 * D])
        for i in range(2):
            ld_m = dma("sync", "wmod", lambda e, i=i: e.dma_start(
                wmod[:, i], a[f"wmod{i}"].rearrange("(k p) m -> p k m", p=P)))
        w1r = at(arena, 6144, [FT, D])
        w2r = at(arena, 8192, [KD, F1])
        ld_w = dma("scalar", "mlp_w", lambda e: e.dma_start(w1r, a["w1"].rearrange("(k p) m -> p k m", p=P)))
        ld_w = dma("scalar", "mlp_w", lambda e: e.dma_start(w2r, a["w2"].rearrange("(k p) m -> p k m", p=P)))
        ld_q = dma("scalar", "qk_w", lambda e: e.dma_start(wqk1[:, :, :], a["wqk1"].rearrange("(k p) m -> p k m", p=P)))
        for dst, name in ((wqkv, "wqkv"), (wlo, "wlo"), (whq, "whq"), (whk, "whk"), (whv, "whv"), (who, "who"),
                          (win, "win"), (wv1, "wv1"), (wo1, "wo1")):
            dma("scalar", "rest_w", lambda e, dst=dst, name=name: e.dma_start(
                dst[:, :, :], a[name].rearrange("(k p) m -> p k m", p=P)))
        dma("scalar", "rest_w", lambda e: e.dma_start(wfo[:, :], a["wfo"]))
        dma("scalar", "rest_w", lambda e: e.dma_start(nullk[:, :], a["nullk"]))
        ld_n = dma("sync", "null_v", lambda e: e.dma_start(nullv[:, :, :], a["null_v"]))

        do("vector", lambda e: e.tensor_copy(identb[:, :], ident[:, :]), ld_c)
        t_cm = do("vector", lambda e: e.tensor_copy(cmask[:, :], cmf), ld_c)

        sg = at(arena, 15700, [2, KD, B])
        sc = at(arena, 15800, [2, KD, B])
        t = do("scalar", lambda e: e.activation(sg, cT, ACT.Exp, scale=-1.0), ld_c)
        t = do("vector", lambda e: e.tensor_scalar(sg, sg, 1.0, None, ALU.add), t)
        t = do("vector", lambda e: e.reciprocal(sg, sg), t)
        t_sc = do("vector", lambda e: e.tensor_tensor(sc, cT, sg, ALU.mult), t)

        for j, (blk, part) in enumerate(((0, 3), (0, 4), (1, 0), (1, 1), (1, 3), (1, 4))):
            for kk in range(KD):
                c0 = (j * KD + kk) * B
                for k in range(KD):
                    t = do("tensor", lambda e, k=k, blk=blk, part=part, kk=kk, c0=c0: e.matmul(
                        bank[0][:, c0:c0 + B], wmod[:, blk, k, part * D + kk * P:part * D + (kk + 1) * P],
                        sc[:, blk, k, :], start=k == 0, stop=k == KD - 1), t_sc, ld_m, sig=k == KD - 1)
        t = do("vector", lambda e: e.tensor_copy(modc[:, :, :].rearrange("p j b -> p (j b)"), bank[0][:, 0:6 * KD * B]), t)
        for j in (1, 3, 5):
            do("vector", lambda e, j=j: e.tensor_scalar(modc[:, j * KD:(j + 1) * KD, :], modc[:, j * KD:(j + 1) * KD, :],
                                                        1.0, None, ALU.add), t)
        free[0] = t
        modr = at(arena, 10240, [12 * D])
        for q in range(6):
            bk = q % 6 + 1
            for k in range(KD):
                t = do("tensor", lambda e, k=k, q=q, bk=bk: e.matmul(
                    bank[bk][0:B, :], sc[:, q // 3, k, :], wmod[:, q // 3, k, (q % 3) * 512:(q % 3 + 1) * 512],
                    start=k == 0, stop=k == KD - 1), sig=k == KD - 1)
            t_mr = do("vector", lambda e, q=q, bk=bk: e.tensor_copy(modr[0:B, q * 512:(q + 1) * 512], bank[bk][0:B, :]), t)
            free[bk] = t_mr
        for j in (1, 4, 7, 10):
            v = modr[0:B, j * D:(j + 1) * D]
            do("vector", lambda e, v=v: e.tensor_scalar(v, v, 1.0, None, ALU.add), t_mr)
        for j in (2, 5, 8, 11):
            v = modr[0:B, j * D:(j + 1) * D]
            s = small[0:B, 0:D]
            t = do("vector", lambda e, v=v, s=s: e.tensor_scalar(s, v, 0.0, None, ALU.is_ge), t_mr)
            t = do("vector", lambda e, s=s: e.tensor_scalar(s, s, 2.0, -1.0, ALU.mult, ALU.add), t)
            t = do("vector", lambda e, v=v, s=s: e.tensor_tensor(v, v, s, ALU.mult), t)
            t = do("vector", lambda e, v=v: e.tensor_scalar(v, v, 0.25, None, ALU.max), t)
            t_mr = do("vector", lambda e, v=v, s=s: e.tensor_tensor(v, v, s, ALU.mult), t)
        dma("sync", "mod_out", lambda e: e.dma_start(mod_d, modr[0:B, :]), t_mr)

        wm = at(small, 256, [KD, 2 * H1])
        v4 = wqk1[:, :, :].rearrange("p k (h d) -> p k h d", d=HD1)
        t = do("vector", lambda e: e.tensor_reduce(wm, v4, AX_X, ALU.add), ld_q)
        t = do("vector", lambda e: e.tensor_scalar(wm, wm, 1.0 / HD1, None, ALU.mult), t)
        for k in range(KD):
            do("vector", lambda e, k=k: e.tensor_tensor(
                v4[:, k], v4[:, k], wm[:, k].unsqueeze(2).broadcast_to([P, 2 * H1, HD1]), ALU.subtract), t)

        cosr, sinr = rope1[:, 0], rope1[:, 1]
        half = HD1 // 2
        tmp = at(small, 384, [T, HD1])
        for i in range(2):
            g = rows[:, R_GB + 2 * i * HD1:R_GB + (2 * i + 1) * HD1]
            bt = rows[:, R_GB + (2 * i + 1) * HD1:R_GB + (2 * i + 2) * HD1]
            bc = lambda v, n: v.unsqueeze(1).broadcast_to([P, T, n])
            do("vector", lambda e, i=i, g=g: e.tensor_tensor(tabA[:, i], cosr, bc(g, HD1), ALU.mult), ld_c)
            do("vector", lambda e, i=i, g=g: e.tensor_tensor(tabB[:, i, :, 0:half], sinr[:, :, 0:half], bc(g[:, 1:HD1:2], half), ALU.mult))
            do("vector", lambda e, i=i, g=g: e.tensor_tensor(tabB[:, i, :, half:HD1], sinr[:, :, half:HD1], bc(g[:, 0:HD1:2], half), ALU.mult))
            do("vector", lambda e, i=i, bt=bt: e.tensor_tensor(tabC[:, i], cosr, bc(bt, HD1), ALU.mult))
            do("vector", lambda e, i=i, bt=bt: e.tensor_tensor(tmp[:, :, 0:half], sinr[:, :, 0:half], bc(bt[:, 1:HD1:2], half), ALU.mult),
               pl_last(pl, "vector"))
            t = do("vector", lambda e, i=i, bt=bt: e.tensor_tensor(tmp[:, :, half:HD1], sinr[:, :, half:HD1], bc(bt[:, 0:HD1:2], half), ALU.mult))
            t = do("vector", lambda e, i=i: e.tensor_tensor(tabC[:, i], tabC[:, i], tmp, ALU.add), t)
            if i == 0:
                for tb in (tabA, tabB, tabC):
                    do("vector", lambda e, tb=tb: e.tensor_scalar(tb[:, 0], tb[:, 0], HD1 ** -0.5, None, ALU.mult), t)

        al = small[:, 512:512 + FT + KD]
        sgn = at(arena, 13312, [F1])
        nb = 0
        for which, raw, nt, width in ((0, w1r, FT, D), (1, w2r, KD, F1)):
            for i in range(nt):
                w, ac, sv = raw[:, i, :], al[:, which * FT + i:which * FT + i + 1], sgn[:, 0:width]
                t = do("vector", lambda e, w=w, ac=ac: e.tensor_reduce(ac, w, AX_X, ALU.add, apply_absolute_value=True), ld_w)
                t = do("vector", lambda e, ac=ac, width=width: e.tensor_scalar(ac, ac, 1.0 / width, None, ALU.mult), t)
                t2 = do("scalar", lambda e, w=w, sv=sv: e.activation(sv, w, ACT.Sign), t, ld_w)
                t = do("vector", lambda e, w=w, ac=ac, sv=sv: e.scalar_tensor_tensor(
                    out=sv, in0=sv, scalar=ac, in1=w, op0=ALU.mult, op1=ALU.subtract), t, t2)
                t = do("vector", lambda e, w=w, sv=sv: e.tensor_tensor(w, w, sv, ALU.add), t)
                for c0 in range(0, width // P, 4):
                    n = min(4, width // P - c0)
                    bk = nb % 7 + 1
                    nb += 1
                    for c in range(n):
                        tt = do("tensor", lambda e, raw=raw, i=i, c=c, c0=c0, bk=bk: e.transpose(
                            bank[bk][:, c * P:(c + 1) * P], raw[:, i, (c0 + c) * P:(c0 + c + 1) * P], ident[:, :]),
                            t, free[bk], sig=c == n - 1)
                    dst = w1T[:, 0:KD, i * P:(i + 1) * P] if which == 0 else w2T[:, c0:c0 + 4, i * P:(i + 1) * P]
                    free[bk] = do("scalar", lambda e, dst=dst, bk=bk, n=n: e.activation(
                        dst, bank[bk][:, 0:n * P].rearrange("p (c q) -> p c q", q=P), ACT.Copy), tt)
        pl.emit(nc)

        s_all = at(arena, 16384, [B, 2, T])
        UB = 4
        with nc.Fori(0, B // UB) as b4:
            pl = Plan(sems, dma_sems)
            do, dma = pl.do, pl.dma
            mods = at(hTf, 0, [UB, 2, D])
            xin = [at(arena, T * D * u, [T, D]) for u in range(UB)]
            normed = [xt[:, :, :], xn[:, :, :]]
            hb = [at(arena, T * D * (UB + u), [T, D]) for u in range(2)]
            scratch = at(arena, T * D * (UB + 2), [D])
            s_b = at(small, 0, [UB, 2, T])
            ld_r = dma("scalar", "mod", lambda e: e.dma_start(
                mods.rearrange("p u j d -> p u (j d)"), mod_d[bass.ds(b4 * UB, UB), 0:2 * D].partition_broadcast(P)))
            ld_x = [dma("sync", f"x{u}", lambda e, u=u: e.dma_start(
                xin[u], a["x"][bass.ds(b4 * UB + u, 1)].rearrange("o (t p) d -> p (o t) d", p=P))) for u in range(UB)]
            t_n, stored = {}, {}

            def normalize_batch(u):
                t_n[u] = yield from norm_steps(pl, xin[u], normed[u % 2], small, 64 + 96 * (u % 2), 0, T, ld_x[u], stored.get(u - 2))

            def route_products(u):
                for i in range(T + 1):
                    if i < T:
                        t = do("gpsimd", lambda e, i=i: e.tensor_tensor(hb[u % 2][:, i], normed[u % 2][:, i], mods[:, u, 1], ALU.mult),
                               t_n[u][i], ld_r, stored.get(u - 2))
                        t_h = do("gpsimd", lambda e, i=i: e.tensor_tensor(hb[u % 2][:, i], hb[u % 2][:, i], mods[:, u, 0], ALU.add), t)
                    if i > 0:
                        for r_ in range(2):
                            do("vector", lambda e, i=i - 1, r_=r_: e.tensor_tensor_reduce(
                                out=scratch, in0=hb[u % 2][:, i], in1=toks[:, r_], scale=1.0, scalar=0.0, op0=ALU.mult,
                                op1=ALU.add, accum_out=s_b[:, u, r_, i:i + 1]), before, pl_last(pl, "vector"))
                    before = t_h
                    yield
                stored[u] = dma("scalar", f"h{u}", lambda e: e.dma_start(
                    h_d[bass.ds((b4 * UB + u) * N, N), :].rearrange("(t p) d -> p t d", p=P), hb[u % 2]), t_h)

            for _ in normalize_batch(0):
                pass
            for u in range(UB):
                interleave(route_products(u), normalize_batch(u + 1) if u + 1 < UB else chain(), {"first": 1.0})
            do("vector", lambda e: e.tensor_copy(s_all[:, bass.ds(b4 * UB, UB), :, :], s_b), pl_last(pl, "vector"))
            pl.emit(nc)

        pl = Plan(sems, dma_sems)
        do, dma = pl.do, pl.dma
        V = lambda fn, *w: do("vector", fn, *w, pl_last(pl, "vector"))
        group, lower = at(arena, 0, [P]), at(arena, 128, [P])
        iota = at(arena, 256, [NQ])
        tokv = at(arena, 512, [T])
        ld = dma("sync", "consts", lambda e: e.dma_start(group, a["group"]))
        ld = dma("sync", "consts", lambda e: e.dma_start(lower, a["lower"]))
        ld = dma("sync", "consts", lambda e: e.dma_start(iota, a["iota"].partition_broadcast(P)))
        ld = dma("sync", "consts", lambda e: e.dma_start(tokv, a["tokv"]))
        s, u, ex, w_, m1, m2, r1, posm = (at(arena, 1024 + 128 * i, [P]) for i in range(8))
        c_ = lambda i: small[:, i:i + 1]
        pmax, smax, na, m, mt, part, lns, cnt, ndef, flag = (c_(i) for i in range(10))
        sall2 = s_all.rearrange("p b r t -> p (b r t)")
        t = do("tensor", lambda e: e.transpose(bank[0][:, 0:P], sall2, ident[:, :]))
        t = V(lambda e: e.tensor_copy(s, bank[0][:, 0:P]), t)
        t = V(lambda e: e.tensor_reduce(pmax, s, AX_X, ALU.max))
        row, row8 = at(arena, 2048, [P])[0:1, :], at(arena, 2176, [2 * B])[0:1, :]
        t = do("tensor", lambda e: e.transpose(bank[1][0:1, 0:P], pmax, ident[:, :]), t)
        t = V(lambda e: e.tensor_reduce(row8, bank[1][0:1, 0:P].rearrange("o (g t) -> o g t", t=T), AX_X, ALU.max), t)
        t = V(lambda e: e.tensor_copy(row.rearrange("o (g t) -> o g t", t=T), row8.unsqueeze(2).broadcast_to([1, 2 * B, T])))
        t = do("tensor", lambda e: e.matmul(bank[2][:, 0:1], row, ident[0:1, 0:1], start=True, stop=True), t)
        V(lambda e: e.tensor_copy(smax, bank[2][:, 0:1]), t)

        dma("scalar", "h_copy", lambda e: e.dma_start(h_d[B * N:(B + 1) * N, :], h_d[0:N, :]))
        ld_h = dma("sync", "h", lambda e: e.dma_start(xn[:, :, :], h_d[0:N, :].rearrange("(t p) d -> p t d", p=P)))

        cur = max(EPS0, EPS)
        V(lambda e, v=-cur * (LOG_K - math.log(N)): e.memset(na, v))
        for it in range(1, NITER):
            cur = max(cur * DECAY, EPS)
            V(lambda e: e.tensor_scalar(m, smax, na, None, ALU.min))
            t = V(lambda e: e.tensor_scalar(u, s, na, m, ALU.min, ALU.subtract))
            V(lambda e, v=-cur * LOG_K: e.tensor_scalar(mt, m, v, None, ALU.add))
            t = do("scalar", lambda e, v=1.0 / cur: e.activation(ex, u, ACT.Exp, scale=v, accum_out=part), t)
            t = do("tensor", lambda e: e.matmul(bank[3][:, 0:1], group, part, start=True, stop=True), t, ld)
            t = do("scalar", lambda e: e.activation(lns, bank[3][:, 0:1], ACT.Ln), t)
            V(lambda e, v=cur: e.tensor_scalar(na, lns, v, mt, ALU.mult, ALU.add), t)
        for c in range(2):
            layer_norm(pl, xn, xn[:, TH * c:TH * c + TH], small, 64, TH * c, TH, ld_h, pl_last(pl, "vector"))
        cur = max(cur * DECAY, EPS)
        V(lambda e: e.tensor_scalar(u, s, na, -1.0, ALU.subtract, ALU.mult))
        V(lambda e: e.tensor_scalar(w_, u, 0.0, 1.0 / cur, ALU.max, ALU.mult))
        t_w = V(lambda e: e.tensor_scalar(w_, w_, FLOOR_EXP, None, ALU.min))
        t = do("scalar", lambda e: e.activation(ex, w_, ACT.Exp, scale=-1.0), t_w)
        V(lambda e: e.tensor_scalar(u, ex, -1.0, 1.0, ALU.mult, ALU.add), t)
        t_sc = V(lambda e: e.tensor_tensor(u, u, ex, ALU.add))

        thr, cand, acc = (small[:, 16 + i:17 + i] for i in range(3))
        thri, candi, acci = thr.bitcast(I32), cand.bitcast(I32), acc.bitcast(I32)
        V(lambda e: e.memset(thr, 0.0))
        for bit in range(30, -1, -1):
            V(lambda e, bit=bit: e.tensor_scalar(candi, thri, 1 << bit, None, ALU.bitwise_or))
            t = V(lambda e: e.tensor_scalar(m1, w_, cand, None, ALU.is_lt, ALU.add, accum_out=cnt))
            t = do("tensor", lambda e: e.matmul(bank[4][:, 0:1], group, cnt, start=True, stop=True), t)
            V(lambda e: e.tensor_scalar(acci, bank[4][:, 0:1], float(NQ), None, ALU.is_lt), t)
            V(lambda e, bit=bit: e.scalar_tensor_tensor(out=thri, in0=acci, scalar=bit, in1=thri,
                                                        op0=ALU.logical_shift_left, op1=ALU.bitwise_or))
        V(lambda e: e.tensor_scalar(m1, w_, thr, None, ALU.is_lt, ALU.add, accum_out=cnt))
        t = V(lambda e: e.tensor_scalar(m2, w_, thr, None, ALU.is_equal, ALU.add, accum_out=flag))
        t = do("tensor", lambda e: e.matmul(bank[4][:, 0:1], group, cnt, start=True, stop=True), t)
        t = do("tensor", lambda e: e.matmul(bank[5][:, 0:1], lower, flag, start=True, stop=True))
        V(lambda e: e.tensor_scalar(ndef, bank[4][:, 0:1], -1.0, float(NQ), ALU.mult, ALU.add), t)
        V(lambda e: e.tensor_scalar(ndef, ndef, bank[5][:, 0:1], None, ALU.subtract))
        zero = at(arena, 2304, [P])
        V(lambda e: e.memset(zero, 0.0))
        V(lambda e: e.tensor_tensor_scan(r1, m2, zero, 0.0, ALU.add, ALU.add))
        V(lambda e: e.tensor_scalar(r1, r1, ndef, None, ALU.is_le))
        V(lambda e: e.tensor_tensor(m2, m2, r1, ALU.mult))
        V(lambda e: e.tensor_tensor(m1, m1, m2, ALU.add))
        V(lambda e: e.tensor_tensor_scan(r1, m1, zero, 0.0, ALU.add, ALU.add))
        t = V(lambda e: e.tensor_copy(cnt, r1[:, P - 1:P]))
        t = do("tensor", lambda e: e.matmul(bank[4][:, 0:1], lower, cnt, start=True, stop=True), t)
        V(lambda e: e.tensor_scalar(r1, r1, bank[4][:, 0:1], None, ALU.add), t)
        V(lambda e: e.tensor_tensor(r1, r1, m1, ALU.mult))
        t = V(lambda e: e.tensor_scalar(posm, r1, -1.0, None, ALU.add))
        t = do("tensor", lambda e: e.transpose(bank[0][:, 0:P], posm, ident[:, :]), t)
        t2 = do("tensor", lambda e: e.transpose(bank[1][:, 0:P], u, ident[:, :]), t_sc)
        posT = at(arena, 2432, [2 * B, T])
        val = at(arena, 8192, [2 * B * T, 5], BF16)
        scT, rest = at(arena, 8576, [2 * B * T]), at(arena, 8704, [2 * B * T])
        V(lambda e: e.tensor_copy(posT.rearrange("p g t -> p (g t)"), bank[0][:, 0:P]), t)
        V(lambda e: e.tensor_copy(scT, bank[1][:, 0:P]), t2)
        for part_ in (2, 3, 4):
            V(lambda e, c=part_: e.tensor_copy(val[:, :, c], scT))
            V(lambda e, c=part_: e.tensor_tensor(scT, scT, val[:, :, c], ALU.subtract))
        V(lambda e: e.tensor_copy(rest.rearrange("p (g t) -> p g t", t=T), tokv.unsqueeze(1).broadcast_to([P, 2 * B, T])), ld)
        V(lambda e: e.tensor_copy(val[:, :, 0], rest))
        V(lambda e: e.tensor_tensor(val[:, :, 1], rest, val[:, :, 0], ALU.subtract))
        iotab = at(arena, 8832, [NQ], BF16)
        t_v = V(lambda e: e.tensor_copy(iotab, iota), ld)
        used = [None] * 2
        res = bank[6][:, 0:5 * 4 * B].rearrange("p (g c) -> p g c", c=5)
        for g in range(2 * B):
            hots = []
            for t_ in range(T):
                hot = at(arena, 3072 + NQ // 2 * (t_ + T * (g % 2)), [NQ], BF16)
                t = do("vector", lambda e, hot=hot, g=g, t_=t_: e.tensor_scalar(
                    hot, iotab, posT[:, g, t_:t_ + 1], None, ALU.is_equal), t_v, used[g % 2])
                hots.append((hot, t))
            for h in range(2):
                for t_, (hot, tk) in enumerate(hots):
                    t = do("tensor", lambda e, hot=hot, g=g, h=h, t_=t_: e.matmul(
                        res[:, 2 * g + h, :], hot[:, h * P:(h + 1) * P], val[:, g * T + t_, :],
                        start=t_ == 0, stop=t_ == T - 1), tk, t_v, sig=t_ == T - 1)
            used[g % 2] = t
        parts_ = at(arena, 9088, [4 * B, 5])
        off = at(arena, 9312, [4 * B])
        ld = dma("sync", "rowoff", lambda e: e.dma_start(off, a["rowoff"].partition_broadcast(P)))
        V(lambda e: e.tensor_copy(parts_, res), t)
        V(lambda e: e.tensor_tensor(sc_all[:, :], parts_[:, :, 3], parts_[:, :, 4], ALU.add))
        V(lambda e: e.tensor_tensor(sc_all[:, :], sc_all[:, :], parts_[:, :, 2], ALU.add))
        V(lambda e: e.tensor_tensor(parts_[:, :, 0], parts_[:, :, 0], parts_[:, :, 1], ALU.add))
        V(lambda e: e.tensor_copy(idx_all[:, 1, :], parts_[:, :, 0]))
        V(lambda e: e.tensor_tensor(off, off, parts_[:, :, 0], ALU.add), ld)
        V(lambda e: e.tensor_copy(idx_all[:, 0, :], off))
        pl.emit(nc)

        idxb = sb("idxb", [P, 2, 8], U32)
        scb = sb("scb", [P, 8])
        modcb = sb("modcb", [P, 6 * KD, 2])
        with nc.Fori(0, B // 2) as b2:
            pl = Plan(sems, dma_sems)
            do, dma = pl.do, pl.dma
            free = {}
            last = lambda e: pl_last(pl, e)
            engines_now = lambda: [last(e) for e in ("tensor", "vector", "scalar", "gpsimd") if last(e)]
            states = [{}, {}, {}]
            side = {"banks": [7], "n": 0}
            pace = {"first": 1.0}

            def load_h(u, *after):
                states[u]["ld_h"] = dma("sync", "h", lambda e: e.dma_start(
                    xn[:, :, :], h_d[bass.ds((b2 * 2 + u) * N, N), :].rearrange("(t p) d -> p t d", p=P)), *after)

            def load_x(u, c, *after):
                states[u]["ld_x", c] = dma("sync", f"x{c}", lambda e: e.dma_start(
                    xt[:, TH * c:TH * c + TH, :], a["x"][bass.ds(b2 * 2 + u, 1), c * NH:(c + 1) * NH].rearrange("o (t p) d -> p (o t) d", p=P)), *after)

            def load_gates(u, name, lo, hi, *after):
                states[u][name] = dma("sync", name, lambda e: e.dma_start(
                    gates[:, lo:hi, :], mod_d[bass.ds(b2 * 2 + u, 1), :].rearrange("o (j d) -> o j d", d=D)[:, 2 + 3 * lo:3 * hi:3, :].partition_broadcast(P)), *after)

            states[0]["n", 0] = states[0]["n", 1] = [None] * TH
            t_ix = do("vector", lambda e: e.tensor_copy(idxb[:, :, :], idx_all[:, :, bass.ds(b2 * 8, 8)]))
            do("vector", lambda e: e.tensor_copy(scb[:, :], sc_all[:, bass.ds(b2 * 8, 8)]))
            t_mc = do("vector", lambda e: e.tensor_copy(modcb[:, :, :], modc[:, :, bass.ds(b2 * 2, 2)]))

            def zone(base):
                pos_ = [base]

                def view(shape, dt=F32):
                    v = at(arena, pos_[0], shape, dt)
                    pos_[0] += int(np.prod(shape)) // (2 if dt == BF16 else 1)
                    assert pos_[0] <= ARENA
                    return v
                return view

            def streams(u):
                st = states[u]

                def begin():
                    if u == 0:
                        load_x(0, 0)
                        load_x(0, 1)
                        load_gates(0, "gate3", 3, 4)
                    else:
                        pl.fence(engines_now())
                    load_gates(u, "gates", 0, 3, *engines_now())
                    st["fill"] = dma("sync", "fill", lambda e: e.dma_start(
                        heavy_d.rearrange("(t p) d -> p t d", p=P), rows[:, R_NULL:R_NULL + D].unsqueeze(1).broadcast_to([P, T, D])),
                        states[0].get("ld_hv"))
                    yield

                def until(key):
                    for _ in range(1000):
                        if key in st:
                            return
                        yield
                    raise RuntimeError(key)

                def heavy():
                    view = zone(ZONE_B)
                    qz = view([H0 // 2, 2, NQ])
                    kh = view([H0 // 2, NQ + 1])
                    vh = view([2, H0, DH])
                    shared = ZONE_B + 4100
                    view = zone(shared)
                    rg, ropeg, nT = view([4, D]), view([4, 2 * DH]), view([2, KD, NQ])
                    qk = view([4, HD])
                    rt1, rt2 = (rg[:, 2 * i:2 * i + 2].rearrange("p r d -> p (r d)") for i in range(2))
                    junk = qk[:, 0, 0:D]
                    view = zone(shared)
                    ph = [view([NQ + 4])[:, 0:NQ + 1] for _ in range(4)]
                    pth = [view([3, P]) for _ in range(2)]
                    otT, hout = view([H0 // 2, P]), view([2, D])
                    ssum, rn, mxh, exq, smh, rch = (small[:, o:o + n] for o, n in ((0, 4), (4, 4), (8, 16), (24, 4), (56, 4), (60, 4)))
                    yield from until("fill")
                    if u == 1:
                        pl.fence(engines_now())
                        load_gates(1, "gate3", 3, 4, *engines_now())
                    gat, rop = [], []
                    for j in (0, 1, 2, 3):
                        gat.append(dma("gpsimd", f"gather{j}", lambda e, j=j: e.indirect_dma_start(
                            out=rg[:, j], out_offset=None, in_=h_d, in_offset=bass.IndirectOffsetOnAxis(ap=idxb[:, 0, 4 * u + j:4 * u + j + 1], axis=0)), t_ix))
                    for j in range(4):
                        rop.append(dma("gpsimd", f"rope{j}", lambda e, j=j: e.indirect_dma_start(
                            out=ropeg[:, j], out_offset=None, in_=a["rope0"], in_offset=bass.IndirectOffsetOnAxis(ap=idxb[:, 1, 4 * u + j:4 * u + j + 1], axis=0)), t_ix))
                    do("vector", lambda e: e.memset(qz[0:DH, :, 1], 0.0))
                    do("vector", lambda e: e.memset(qz[DH:P, :, 0], 0.0))
                    t_nk = do("vector", lambda e: e.tensor_copy(kh[:, :, 0], nullk[:, :]))
                    t = do("gpsimd", lambda e: e.memset(exq, -0.5))
                    yield
                    for j in range(4):
                        t1 = do("vector", lambda e, j=j: e.tensor_tensor_reduce(
                            out=junk, in0=rg[:, j], in1=rg[:, j], scale=1.0, scalar=0.0, op0=ALU.mult, op1=ALU.add,
                            accum_out=ssum[:, j:j + 1]), gat[j], last("vector"))
                    t1 = do("vector", lambda e: e.tensor_scalar(rn, ssum, 1e-24, None, ALU.max), t1)
                    t1 = do("gpsimd", lambda e: e.tensor_tensor(rn, rn, exq, ALU.pow), t, t1)
                    yield
                    t1 = do("vector", lambda e: e.tensor_scalar(rn, rn, float(D) ** 0.5, None, ALU.mult), t1)
                    for j in range(4):
                        bk = 5 + j // 2
                        tn = do("vector", lambda e, j=j: e.tensor_scalar(rg[:, j], rg[:, j], rn[:, j:j + 1], None, ALU.mult), t1)
                        for k in range(KD):
                            t = do("tensor", lambda e, j=j, k=k, bk=bk: e.transpose(
                                bank[bk][:, k * NQ + (j % 2) * P:k * NQ + (j % 2 + 1) * P], rg[:, j, k * P:(k + 1) * P], ident[:, :]),
                                tn, sig=k == KD - 1)
                        if j % 2:
                            for k in range(KD):
                                t_nT = do("scalar", lambda e, j=j, k=k, bk=bk: e.activation(
                                    nT[:, j // 2, k], bank[bk][:, k * NQ:(k + 1) * NQ], ACT.Copy,
                                    scale=cols[:, C_HG + k:C_HG + k + 1]), t)
                            free[bk] = t_nT
                        yield
                    t_v, t_qk = [], []

                    def turn_qk(j, t):
                        for p_ in range(H0 // 2):
                            t2 = do("tensor", lambda e, p_=p_: e.transpose(
                                bank[6][:, p_ * P:(p_ + 1) * P], qk[:, j, p_ * P:(p_ + 1) * P], ident[:, :]), t, free.get(6),
                                sig=p_ == H0 // 2 - 1)
                        bv = bank[6].rearrange("p (c q) -> p c q", q=P)
                        q0 = (j % 2) * P
                        if j < 2:
                            do("scalar", lambda e: e.activation(qz[0:DH, :, 0, q0:q0 + P], bv[0:DH], ACT.Copy), t2)
                            free[6] = do("scalar", lambda e: e.activation(qz[DH:P, :, 1, q0:q0 + P], bv[DH:P], ACT.Copy), t2)
                        else:
                            free[6] = do("scalar", lambda e: e.activation(kh[:, :, 1 + q0:1 + q0 + P], bv, ACT.Copy), t2)
                        t_qk.append(free[6])

                    behind, t_rot = None, None
                    for j in range(6):
                        w = (whq, whq, whk, whk, whv, whv)[j]
                        src, half_ = (0, 0, 1, 1, 1, 1)[j], j % 2
                        bk = 7 if j % 2 else 5
                        for k in range(KD):
                            t = do("tensor", lambda e, w=w, src=src, half_=half_, k=k, bk=bk: e.matmul(
                                bank[bk], nT[:, src, k, half_ * P:(half_ + 1) * P], w[:, k, :], start=k == 0, stop=k == KD - 1),
                                t_nT, free.get(bk), sig=k == KD - 1)
                        yield
                        if j < 4:
                            free[bk] = t_e = do("scalar", lambda e, j=j, bk=bk: e.activation(
                                qk[:, j], bank[bk], ACT.Copy, scale=DH ** -0.5 if j < 2 else 1.0), t, last("vector"))
                            x4 = qk[:, j].rearrange("p (h d) -> p h d", d=DH)
                            r1_, r2_ = (v.rearrange("p (h d) -> p h d", d=DH) for v in (rt1, rt2))
                            hd = DH // 2
                            cs = lambda lo, hi, j=j: ropeg[:, j, lo:hi].unsqueeze(1).broadcast_to([P, H0, hi - lo])
                            t_c = do("gpsimd", lambda e, x4=x4, r=r1_, c=cs(0, DH): e.tensor_tensor(r, x4, c, ALU.mult), t_e, rop[j], t_rot, t_nT)
                            do("vector", lambda e, x4=x4, r=r2_, c=cs(DH, DH + hd): e.tensor_tensor(r[:, :, 0:hd], x4[:, :, hd:DH], c, ALU.mult), t_e, rop[j], t_rot)
                            t = do("vector", lambda e, x4=x4, r=r2_, c=cs(DH + hd, 2 * DH): e.tensor_tensor(r[:, :, hd:DH], x4[:, :, 0:hd], c, ALU.mult))
                            t_rot = do("vector", lambda e, j=j: e.tensor_tensor(qk[:, j], rt1, rt2, ALU.add), t, t_c)
                            now = lambda j=j, t=t_rot: turn_qk(j, t)
                        else:
                            t_v.append(do("vector", lambda e, half_=half_, bk=bk: e.tensor_scalar(
                                vh[:, half_, :, :], bank[bk].rearrange("p (h d) -> p h d", d=DH), scb[:, 4 * u + 2 + half_:4 * u + 3 + half_],
                                None, ALU.mult), t))
                            free[bk] = t_v[-1]
                            now = None
                        if behind:
                            behind()
                        behind = now
                        yield
                    hs_ = {}

                    def head_scores(n):
                        half_, h = divmod(n, H0)
                        sl = n % 4
                        t = do("tensor", lambda e: e.matmul(
                            bank[5][:, 0:NQ + 1], qz[:, h // 2, h % 2, half_ * P:(half_ + 1) * P], kh[:, h // 2, :], start=True, stop=True),
                            *t_qk, t_nk, free.get(5))
                        t = do("vector", lambda e: e.tensor_reduce(
                            mxh[:, n:n + 1], bank[5][:, 0:NQ + 1], AX_X, ALU.max, negate=True), t)
                        hs_["exp", n] = free[5] = do("scalar", lambda e: e.activation(
                            ph[sl], bank[5][:, 0:NQ + 1], ACT.Exp, bias=mxh[:, n:n + 1], accum_out=smh[:, sl:sl + 1]),
                            t, hs_.get(("tr", n - 4)), hs_.get(("rc", n - 4)), t_rot, t_v[-1])

                    def head_normalize(n):
                        sl = n % 4
                        t = hs_["rc", n] = do("vector", lambda e: e.reciprocal(rch[:, sl:sl + 1], smh[:, sl:sl + 1]), hs_["exp", n], hs_.get(("pn", n - 4)))
                        hs_["pn", n] = do("gpsimd", lambda e: e.tensor_tensor(
                            ph[sl], ph[sl], rch[:, sl:sl + 1].broadcast_to([P, NQ + 1]), ALU.mult), t)

                    def head_turn(n):
                        sl, s2 = n % 4, n % 2
                        for c, (lo, wd) in enumerate(((1, P), (1 + P, P), (0, 1))):
                            t = do("tensor", lambda e, c=c, lo=lo, wd=wd: e.transpose(
                                bank[6][0:wd, c * P:(c + 1) * P], ph[sl][:, lo:lo + wd], ident[:, :]), hs_["pn", n], free.get(6), sig=c == 2)
                        hs_["tr", n] = t
                        do("vector", lambda e: e.tensor_copy(
                            pth[s2][:, 0:2], bank[6][:, 0:2 * P].rearrange("p (c q) -> p c q", q=P)), t, hs_.get(("pv", n - 2)), t_rot)
                        hs_["pt", n] = free[6] = do("vector", lambda e: e.tensor_copy(pth[s2][0:1, 2], bank[6][0:1, 2 * P:3 * P]))

                    def head_weigh(n):
                        half_, h = divmod(n, H0)
                        s2 = n % 2
                        ob = bank[7][(h % 2) * DH:(h % 2 + 1) * DH, (h // 2) * P:(h // 2 + 1) * P]
                        for c in range(2):
                            do("tensor", lambda e, c=c: e.matmul(
                                ob, vh[:, c, h, :], pth[s2][:, c], start=c == 0, stop=False, skip_group_check=True),
                                hs_["pt", n], t_v[-1], free.get(7), sig=False)
                        t = hs_["pv", n] = do("tensor", lambda e: e.matmul(
                            ob, nullv[0:1, h, :], pth[s2][0:1, 2], start=False, stop=True, skip_group_check=True))
                        if h == H0 - 1:
                            hs_["o", half_] = free[7] = do("scalar", lambda e: e.activation(
                                otT.rearrange("p c q -> p (c q)"), bank[7], ACT.Copy), t, hs_.get("out"))

                    def head_project(half_):
                        for c in range(4):
                            t = do("tensor", lambda e, c=c: e.matmul(bank[6][:, 0:D], otT[:, c], who[:, c, :], start=c == 0, stop=c == 3),
                                   hs_["o", half_], free.get(6), sig=c == 3)
                        hs_["out"] = t
                        t = free[6] = do("vector", lambda e: e.tensor_scalar(
                            hout[:, half_], bank[6][:, 0:D], scb[:, 4 * u + half_:4 * u + half_ + 1], None, ALU.mult), t)
                        st["scatter", half_] = dma("gpsimd", f"scatter{half_}", lambda e: e.indirect_dma_start(
                            out=heavy_d, out_offset=bass.IndirectOffsetOnAxis(ap=idxb[:, 1, 4 * u + half_:4 * u + half_ + 1], axis=0),
                            in_=hout[:, half_], in_offset=None), t, st["fill"])

                    for n in range(2 * H0 + 5):
                        if n < 2 * H0:
                            head_scores(n)
                        if 0 <= n - 1 < 2 * H0:
                            head_normalize(n - 1)
                        if 0 <= n - 3 < 2 * H0:
                            head_turn(n - 3)
                        yield
                        if 0 <= n - 4 < 2 * H0:
                            head_weigh(n - 4)
                        if n in (H0 + 4, 2 * H0 + 4):
                            head_project(n // H0 - 1)
                        yield
                    st["ld_hv"] = dma("sync", "heavy", lambda e: e.dma_start(
                        xn[:, :, :], heavy_d.rearrange("(t p) d -> p t d", p=P)), st["scatter", 0], st["scatter", 1], *st["hT", 0], *st["hT", 1])
                    side["banks"] = [5, 6, 7]

                view = zone(0)
                qt = view([H0 // 2, 2, NH])
                kt = view([H0 // 2, NH + 2 * WIN])
                vt = view([TH + 1, H0, DH])
                sm = [view([2, 2 * P]) for _ in range(2)]
                pm = [view([2, 2 * P]) for _ in range(3)]
                pt = [view([4, P]) for _ in range(2)]
                onT = view([H0 // 2, P])
                xadd = [view([D])]
                nmx, sml, rcl = (small[:, o:o + 8] for o in (32, 40, 48))

                def input_norm(u):
                    for c in range(2):
                        states[u]["n", c] = yield from norm_steps(
                            pl, xn, xn[:, TH * c:TH * c + TH], small, 64, TH * c, TH, states[u]["ld_h"], last("vector"))

                def light_start():
                    yield from until(("n", 1))
                    do("gpsimd", lambda e: e.memset(hT[:, :, 0:WIN], 0.0))
                    t_z = do("gpsimd", lambda e: e.memset(hT[:, :, WIN + N:NPAD], 0.0))
                    do("gpsimd", lambda e: e.memset(qt[0:DH, :, 1], 0.0), last("gpsimd"))
                    st["zeros"] = pl.partial = do("gpsimd", lambda e: e.memset(qt[DH:P, :, 0], 0.0), last("gpsimd"))
                    for c in range(2):
                        st["hT", c] = [t_z]
                    turn_norm(0)
                    yield

                def turn_norm(c):
                    for k in range(KD):
                        bk = 2 * c + k
                        for i in range(TH):
                            t = do("tensor", lambda e, k=k, i=i, bk=bk: e.transpose(
                                bank[bk][:, i * P:(i + 1) * P], xn[:, TH * c + i, k * P:(k + 1) * P], ident[:, :]),
                                st["n", c][i], free.get(bk), sig=i == TH - 1)
                        free[bk] = affine(pl, k % 2, hT[:, k, WIN + c * NH:WIN + (c + 1) * NH], bank[bk],
                                          cols[:, C_LNG + k:C_LNG + k + 1], cols[:, C_LNB + k:C_LNB + k + 1], t)
                        st["hT", c].append(free[bk])

                def light(c):
                    pace["first"] = PACE[u][c]
                    prev = [st.get("pv_last"), st.get("q_last")]
                    if c == 1:
                        t_k0 = do("gpsimd", lambda e: e.tensor_copy(kt[:, :, 0:P], kt[:, :, NH:NH + P]), *prev)
                        t_v0 = do("gpsimd", lambda e: e.tensor_copy(vt[:, 0], vt[:, TH]), *prev)
                        prev += [t_k0, t_v0]
                    nb = 0
                    banks = (4, 2, 3)
                    tk, tq, tv = [], [], []
                    for m_ in range(8):
                        if (c, m_) == (0, 4):
                            turn_norm(1)
                        for lo, hi in [(c * NH + WIN, (c + 1) * NH + WIN)] if m_ < 4 else [(c * NH + P, (c + 1) * NH + P)] + [(0, P)] * (c == 0):
                            bk = banks[nb % 3]
                            nb += 1
                            for k in range(KD):
                                t = do("tensor", lambda e, m_=m_, lo=lo, hi=hi, k=k, bk=bk: e.matmul(
                                    bank[bk][:, 0:hi - lo], wqkv[:, k, m_ * P:(m_ + 1) * P], hT[:, k, lo:hi],
                                    start=k == 0, stop=k == KD - 1), *st["hT", 0], *(st["hT", 1] if c or m_ > 3 else []), free.get(bk), sig=k == KD - 1)
                            if m_ < 4:
                                t1 = do("scalar", lambda e, m_=m_, bk=bk: e.activation(
                                    qt[0:DH, m_, 0, :], bank[bk][0:DH], ACT.Copy, scale=DH ** -0.5), t, st["zeros"], *prev)
                                t2 = do("vector", lambda e, m_=m_, bk=bk: e.tensor_scalar(
                                    qt[DH:P, m_, 1, :], bank[bk][DH:P], DH ** -0.5, None, ALU.mult), t, st["zeros"], *prev)
                                free[bk] = [t1, t2]
                                tq += [t1, t2]
                            else:
                                free[bk] = copy(pl, nb % 2, kt[:, m_ - 4, lo - c * NH:hi - c * NH], bank[bk][:, 0:hi - lo], t, *prev)
                                tk.append(free[bk])
                            yield
                    for j in range(c, TH + 1):
                        bk = banks[nb % 3]
                        nb += 1
                        for k in range(KD):
                            t = do("tensor", lambda e, j=j, k=k, bk=bk: e.matmul(
                                bank[bk], hT[:, k, (c * TH + j) * P:(c * TH + j + 1) * P], wqkv[:, k, 2 * HD:3 * HD],
                                start=k == 0, stop=k == KD - 1), free.get(bk), sig=k == KD - 1)
                        free[bk] = copy(pl, nb % 2, vt[:, j, :, 0:DH], bank[bk].rearrange("p (h d) -> p h d", d=DH), t, st["zeros"], *prev)
                        tv.append(free[bk])
                        yield
                    ready = tq + tk + tv + [p for p in prev if p]

                    ls = {}

                    def scores(n):
                        i, p_ = divmod(n, H0 // 2)
                        bk = n % 2
                        for j in range(2):
                            ls["s", n] = do("tensor", lambda e, j=j: e.matmul(
                                bank[bk][:, j * 2 * P:(j + 1) * 2 * P], qt[:, p_, j, i * P:(i + 1) * P], kt[:, p_, i * P:i * P + 2 * P],
                                start=True, stop=True), free.get(bk), *ready, sig=j == 1)

                    def soften(n):
                        i, sl = n // (H0 // 2), n % 4
                        mk = wmask[:, 0 if (c, i) == (0, 0) else 2 if (c, i) == (1, TH - 1) else 1]
                        for j in range(2):
                            t = free[n % 2] = do("vector", lambda e, j=j: e.tensor_tensor_reduce(
                                out=sm[n % 2][:, j], in0=bank[n % 2][:, j * 2 * P:(j + 1) * 2 * P], in1=mk, scale=-1.0, scalar=3e38,
                                op0=ALU.add, op1=ALU.min, accum_out=nmx[:, 2 * sl + j:2 * sl + j + 1]), ls["s", n], ls.get(("exp", n - 2)))
                        for j in range(2):
                            ls["exp", n] = do("scalar", lambda e, j=j: e.activation(
                                pm[n % 3][:, j], sm[n % 2][:, j], ACT.Exp, bias=nmx[:, 2 * sl + j:2 * sl + j + 1], scale=-1.0,
                                accum_out=sml[:, 2 * sl + j:2 * sl + j + 1]), t, ls.get(("tr", n - 3)), ls.get(("rc", n - 4)))

                    def normalize_pair(n):
                        sl = n % 4
                        t = ls["rc", n] = do("vector", lambda e: e.reciprocal(rcl[:, 2 * sl:2 * sl + 2], sml[:, 2 * sl:2 * sl + 2]),
                                             ls["exp", n], ls.get(("pn", n - 4)))
                        ls["pn", n] = do("gpsimd", lambda e: e.tensor_tensor(
                            pm[n % 3], pm[n % 3], rcl[:, 2 * sl:2 * sl + 2].unsqueeze(2).broadcast_to([P, 2, 2 * P]), ALU.mult), t)

                    def turn(n):
                        for j in range(4):
                            ls["tr", n] = do("tensor", lambda e, j=j: e.transpose(
                                bank[2][:, j * P:(j + 1) * P], pm[n % 3][:, j // 2, (j % 2) * P:(j % 2 + 1) * P], ident[:, :]),
                                ls["pn", n], free.get(2), sig=j == 3)

                    def turned(n):
                        ls["pt", n] = free[2] = copy(pl, n % 2, pt[n % 2].rearrange("p c q -> p (c q)"), bank[2], ls["tr", n], ls.get(("pv", n - 2)))

                    def weigh(n):
                        i, p_ = divmod(n, H0 // 2)
                        ob = 3 + i % 2
                        for blk in range(2):
                            for j in range(2):
                                t = do("tensor", lambda e, j=j, blk=blk: e.matmul(
                                    bank[ob][j * DH:(j + 1) * DH, p_ * P:(p_ + 1) * P], vt[:, i + blk, 2 * p_ + j, :], pt[n % 2][:, 2 * j + blk],
                                    start=blk == 0, stop=blk == 1, skip_group_check=True), ls["pt", n], free.get(ob), sig=j + blk == 2)
                        ls["pv", n] = st["pv_last"] = t
                        if p_ == H0 // 2 - 1:
                            ls["o", i] = free[ob] = do("scalar", lambda e: e.activation(
                                onT.rearrange("p c q -> p (c q)"), bank[ob], ACT.Copy), t, st.get("light_out"))

                    def project(i):
                        ob = 3 + i % 2
                        for j in range(4):
                            t = do("tensor", lambda e, j=j: e.matmul(
                                bank[ob][:, 0:D], onT[:, j], wlo[:, j, :], start=j == 0, stop=j == 3), ls["o", i], sig=j == 3)
                        st["light_out"] = t
                        free[ob], st["x", TH * c + i] = add_gated(pl, xt, TH * c + i, bank[ob][:, 0:D], gates[:, 0], xadd, t, st["gates"], st["ld_x", c])

                    units = TH * H0 // 2
                    for n in range(units + 6):
                        if n < units:
                            scores(n)
                        if 0 <= n - 3 < units:
                            turn(n - 3)
                        if n < units:
                            soften(n)
                        if 0 <= n - 3 < units:
                            turned(n - 3)
                        if 0 <= n - 1 < units:
                            normalize_pair(n - 1)
                        yield
                        if 0 <= n - 4 < units:
                            weigh(n - 4)
                        if n >= 8 and n % 4 == 0:
                            project(n // 4 - 2)
                        yield
                    st["q_last"] = last("tensor")
                    st["light", c] = engines_now()

                hT2 = xh[:, 0:KD * NH].rearrange("p (k n) -> p k n", k=KD)
                xadd2 = [xh[:, KD * NH + i * D:KD * NH + (i + 1) * D] for i in range(2)]


                def side_bank():
                    side["n"] += 1
                    return side["banks"][side["n"] % len(side["banks"])]

                def norm_half(c, j, *ready, xn2=None):
                    xn2 = xn[:, TH * c:TH * c + TH] if xn2 is None else xn2
                    t_n = yield from norm_steps(pl, xt, xn2, small, 144, TH * c, TH, *ready, st.get(("n2", c)))
                    st["t_n"] = t_n[-1]
                    yield
                    st["hT2"] = []
                    for k in range(KD):
                        bk = side_bank()
                        for i in range(TH):
                            t = do("tensor", lambda e, k=k, i=i, bk=bk: e.transpose(
                                bank[bk][:, i * P:(i + 1) * P], xn2[:, i, k * P:(k + 1) * P], ident[:, :]),
                                t_n[i], free.get(bk), sig=i == TH - 1)
                        st["n2", c] = t
                        free[bk] = affine(pl, k, hT2[:, k], bank[bk], modcb[:, (j + 1) * KD + k, u:u + 1],
                                         modcb[:, j * KD + k, u:u + 1], t, t_mc)
                        st["hT2"].append(free[bk])
                        yield

                def add_bias(c, bias, gate, *after):
                    t = do("gpsimd", lambda e: e.tensor_tensor(small[:, 256:512], bias, gate, ALU.mult), *after, last("gpsimd"))
                    return do("gpsimd", lambda e: e.tensor_tensor(
                        xt[:, TH * c:TH * c + TH], xt[:, TH * c:TH * c + TH],
                        small[:, 256:512].unsqueeze(1).broadcast_to([P, TH, D]), ALU.add), t)

                def mlp0(c):
                    yield from until(("light", c))
                    z = [*engines_now(), st.get(("split", 0, 0)), st.get(("split", 0, 1))]
                    view = zone(ZONE_B)
                    if c == 0:
                        do("gpsimd", lambda e: e.memset(v1[:, :, :, HD1:HD1 + 1], 1.0), last("gpsimd"))
                        for _ in range(WAIT_HV):
                            yield
                    sT, rl, gT = view([NH]), [view([NH]) for _ in range(2)], view([NH])
                    if c == 0:
                        for j in range(2):
                            st["hv", j] = do("gpsimd", lambda e, j=j: e.tensor_tensor(
                                xn[:, TH * j:TH * j + TH], xn[:, TH * j:TH * j + TH], gates[:, 0].unsqueeze(1).broadcast_to([P, TH, D]), ALU.mult),
                                st["ld_hv"], st["gates"])
                            yield
                    for i in range(TH):
                        t = do("vector", lambda e, i=i: e.tensor_tensor(xt[:, TH * c + i], xt[:, TH * c + i], xn[:, TH * c + i], ALU.add),
                               st["hv", c], st["x", TH * c + i])
                        yield
                    yield from norm_half(c, 0, t)
                    t_b = add_bias(c, rows[:, R_BOUT:R_BOUT + D], gates[:, 1], st["t_n"])
                    b0 = side_bank()
                    for k in range(KD):
                        t = do("tensor", lambda e, k=k: e.matmul(
                            bank[b0], win[:, k, :], hT2[:, k], start=k == 0, stop=k == KD - 1),
                            *st["hT2"], free.get(b0), sig=k == KD - 1)
                    t_s = free[b0] = do("scalar", lambda e: e.activation(
                        sT, bank[b0], ACT.Identity, bias=cols[:, C_BIN:C_BIN + 1]), t, *z)
                    t_g = do("vector", lambda e: e.tensor_copy(gT, cols[:, C_B2:C_B2 + 1].broadcast_to([P, NH])), *z)
                    rd, re = {}, {}
                    for j in range(INNER // 2 + 1):
                        if j < INNER // 2:
                            re[j] = do("scalar", lambda e, j=j: e.activation(
                                rl[j % 2], sT, ACT.Relu, scale=cols[:, C_W1 + j:C_W1 + j + 1], bias=cols[:, C_B1 + j:C_B1 + j + 1]),
                                t_s, rd.get(j - 2), *z)
                        if j > 0:
                            t_g = rd[j - 1] = do("vector", lambda e, j=j - 1: e.scalar_tensor_tensor(
                                out=gT, in0=rl[j % 2], scalar=cols[:, C_W2 + j:C_W2 + j + 1], in1=gT, op0=ALU.mult, op1=ALU.add), re[j - 1], t_g)
                        yield
                    for i in range(0, TH, 2):
                        bk = side_bank()
                        for j in range(2):
                            t = do("tensor", lambda e, i=i, j=j, bk=bk: e.matmul(
                                bank[bk][:, j * D:(j + 1) * D], gT[:, (i + j) * P:(i + j + 1) * P], wfo[:, :], start=True, stop=True),
                                t_g, free.get(bk), sig=j == 1)
                        i0 = TH * c + i
                        xa = xh[:, KD * NH:KD * NH + 2 * D].rearrange("p (t d) -> p t d", d=D)
                        t = free[bk] = do("vector", lambda e, xa=xa, bk=bk: e.tensor_tensor(
                            xa, bank[bk].rearrange("p (t d) -> p t d", d=D), gates[:, 1].unsqueeze(1).broadcast_to([P, 2, D]), ALU.mult),
                            t, st.get("xa"), t_b, last("gpsimd"))
                        st["xa"] = st["x", i0] = st["x", i0 + 1] = do("gpsimd", lambda e, i0=i0, xa=xa: e.tensor_tensor(
                            xt[:, i0:i0 + 2], xt[:, i0:i0 + 2], xa, ALU.add), t)
                        yield

                def project1(c):
                    z = engines_now()
                    view = zone(ZONE_B)
                    QC, T1, T2 = (view([TH, 2 * D]) for _ in range(3))
                    parts = [view([4, NH], BF16) for _ in range(3)]
                    hs = small[:, 512:512 + TH * 2 * H1]
                    yield from norm_half(c, 2, *[st["x", TH * c + i] for i in range(TH)])
                    st["bias1", c] = add_bias(c, rows[:, R_BO:R_BO + D], gates[:, 2], st["t_n"])
                    for i in range(TH):
                        bk = side_bank()
                        for k in range(KD):
                            t = do("tensor", lambda e, i=i, k=k, bk=bk: e.matmul(
                                bank[bk], hT2[:, k, i * P:(i + 1) * P], wqk1[:, k, :], start=k == 0, stop=k == KD - 1),
                                *st["hT2"], free.get(bk), sig=k == KD - 1)
                        free[bk] = t_qc = do("scalar", lambda e, i=i, bk=bk: e.activation(QC[:, i], bank[bk], ACT.Copy), t, *z, last("vector"))
                        t_sq = do("gpsimd", lambda e, i=i: e.tensor_tensor(T1[:, i], QC[:, i], QC[:, i], ALU.mult), t_qc, *z)
                        yield
                        bk = side_bank()
                        for k in range(KD):
                            t = do("tensor", lambda e, i=i, k=k, bk=bk: e.matmul(
                                bank[bk][:, 0:D], hT2[:, k, i * P:(i + 1) * P], wv1[:, k, :], start=k == 0, stop=k == KD - 1),
                                free.get(bk), sig=k == KD - 1)
                        free[bk] = st["v", c] = do("vector", lambda e, i=i, bk=bk: e.tensor_copy(
                            v1[:, TH * c + i, :, 0:HD1], bank[bk][:, 0:D].rearrange("p (h d) -> p h d", d=HD1)), t)
                        yield
                    for i in range(TH):
                        t = do("vector", lambda e, i=i: e.tensor_reduce(
                            hs[:, 2 * H1 * i:2 * H1 * (i + 1)], T1[:, i].rearrange("p (h d) -> p h d", d=HD1), AX_X, ALU.add), t_sq, last("vector"))
                        yield
                    t = do("vector", lambda e: e.tensor_scalar(hs, hs, 1.0 / HD1, 1e-5, ALU.mult, ALU.add), t)
                    t = do("scalar", lambda e: e.activation(hs, hs, ACT.Sqrt), t)
                    yield
                    t_rs = do("vector", lambda e: e.reciprocal(hs, hs), t)
                    turned_, t_r = {}, [None] * 2
                    for u_ in range(5):
                        if u_ < 4:
                            i, i0 = u_ // 2, 2 * (u_ % 2)
                            x4, a4, b4 = (v[:, i0:i0 + 2, i * D:(i + 1) * D].rearrange("p t (h d) -> p t h d", d=HD1) for v in (QC, T1, T2))
                            tb = lambda v, lo, hi: v[:, i, TH * c + i0:TH * c + i0 + 2, lo:hi].unsqueeze(2).broadcast_to([P, 2, H1, hi - lo])
                            t_a = do("vector", lambda e, x4=x4, a4=a4, v=tb(tabA, 0, HD1): e.tensor_tensor(a4, x4, v, ALU.mult), t_rs)
                            do("gpsimd", lambda e, x4=x4, b4=b4, v=tb(tabB, 0, half): e.tensor_tensor(
                                b4[:, :, :, 0:half], x4[:, :, :, 1:HD1:2], v, ALU.mult), t_qc, *z)
                            t_b = do("gpsimd", lambda e, x4=x4, b4=b4, v=tb(tabB, half, HD1): e.tensor_tensor(
                                b4[:, :, :, half:HD1], x4[:, :, :, 0:HD1:2], v, ALU.mult), t_qc)
                            turned_[u_] = (t_a, t_b)
                            yield
                        if u_ > 0:
                            i, i0 = (u_ - 1) // 2, 2 * ((u_ - 1) % 2)
                            a3, b3 = (v[:, i0:i0 + 2, i * D:(i + 1) * D] for v in (T1, T2))
                            q4, a4 = (v[:, i0:i0 + 2, i * D:(i + 1) * D].rearrange("p t (h d) -> p t h d", d=HD1) for v in (QC, T1))
                            rs4 = hs.rearrange("p (t h) -> p t h", t=TH)[:, i0:i0 + 2, i * H1:(i + 1) * H1].unsqueeze(3).broadcast_to([P, 2, H1, HD1])
                            tc4 = tabC[:, i, TH * c + i0:TH * c + i0 + 2].unsqueeze(2).broadcast_to([P, 2, H1, HD1])
                            t = do("vector", lambda e, a3=a3, b3=b3: e.tensor_tensor(a3, a3, b3, ALU.add), *turned_[u_ - 1])
                            t = do("vector", lambda e, a4=a4, rs4=rs4: e.tensor_tensor(a4, a4, rs4, ALU.mult), t)
                            yield
                            t_r[i] = do("vector", lambda e, q4=q4, a4=a4, tc4=tc4: e.tensor_tensor(q4, a4, tc4, ALU.add), t)
                            yield
                    for m_ in (0, 2, 1, 3):
                        bk = side_bank()
                        for i in range(TH):
                            t = do("tensor", lambda e, m_=m_, i=i, bk=bk: e.transpose(
                                bank[bk][:, i * P:(i + 1) * P], QC[:, i, m_ * P:(m_ + 1) * P], ident[:, :]),
                                t_r[m_ // 2], free.get(bk), sig=i == TH - 1)
                        hi, mi, lo = (v[:, m_] for v in parts)
                        rr = T1[:, m_]
                        t1 = do("scalar", lambda e, hi=hi, bk=bk: e.activation(hi, bank[bk], ACT.Copy), t, t_r[1], t_r[0], *z)
                        t2 = free[bk] = do("vector", lambda e, hi=hi, rr=rr, bk=bk: e.tensor_tensor(rr, bank[bk], hi, ALU.subtract), t1, t)
                        t3 = do("scalar", lambda e, mi=mi, rr=rr: e.activation(mi, rr, ACT.Copy), t2, *z)
                        t4 = do("gpsimd", lambda e, mi=mi, lo=lo, rr=rr: e.tensor_tensor(lo, rr, mi, ALU.subtract), t3, *z)
                        heads = slice((m_ % 2) * P // HD1, (m_ % 2 + 1) * P // HD1)
                        for i, row in [(0, 0), (0, 1), (0, 2), (1, 3), (1, 4), (2, 5)] if m_ < 2 else [(0, 0), (1, 1), (2, 2)]:
                            dst = (split_q if m_ < 2 else split_k)[heads, row, :, c * NH:(c + 1) * NH]
                            st["split", c, m_ % 2] = dma("sync", f"split{c}{m_ % 2}", lambda e, i=i, m_=m_, dst=dst: e.dma_start(
                                dst, parts[i][:, m_]), (t1, t3, t4)[i])
                        if m_ >= 2:
                            st["landing", c, m_ - 2] = True
                        yield
                    if c == 1:
                        yield from until(("gdone", 1))
                        load_group(1, 0, st["gdone", 1])
                    st["projected", c] = True
                    if c == 1:
                        load_h(u + 1, st["n2", 0], st["n2", 1], st["hv", 0], st["hv", 1])

                view = zone(0)
                qa = [view([G1, NH], BF16) for _ in range(3)]
                ka = [view([G1, N], BF16) for _ in range(2)] + [at(hTf, 0, [G1, N], BF16)]
                slot = lambda c, g: (NG * c + g) % 3
                pp = [view([2, NH]) for _ in range(4)]
                ocT = view([KD, NH])
                og = [ocT[:, i] for i in range(2)]
                oc = view([TH, D])
                nm = [view([G1, TH, 2]) for _ in range(2)]
                nmf = [view([G1 * TH]) for _ in range(2)]
                nms = [view([G1 * TH, 2], BF16) for _ in range(2)]
                count = {"s": 0, "p": 0, "m": 0, "o": 0}

                def load_group(c, g, *after):
                    heads = slice(g * G1, (g + 1) * G1)
                    dma("sync", f"group{c}{g}", lambda e: e.dma_start(
                        qa[slot(c, g)][0:KS], split_q[heads, :, :, c * NH:(c + 1) * NH].rearrange("h r d n -> (r d) h n")),
                        st["split", c, g // 2], *after)
                    for r0, n in ((0, 3), (3, 2), (5, 1)):
                        st["grp", c, g] = dma("sync", f"group{c}{g}", lambda e, r0=r0, n=n: e.dma_start(
                            ka[slot(c, g)][r0 * HD1:(r0 + n) * HD1, :, 0:(c + 1) * NH],
                            split_k[heads, 0:n, :, 0:(c + 1) * NH].rearrange("h r d n -> (r d) h n")))

                def max_units(c, g):
                    def begin():
                        st["nm", g % 2] = do("vector", lambda e: e.memset(nm[g % 2], 3e38), *st["z_attn"], st.get(("nmf", g % 2)))

                    def unit(h, i, kc):
                        qi = TH * c + i
                        w_ = min(NH, (qi + 1) * P - kc * NH)
                        diag = kc * NH + w_ == (qi + 1) * P
                        bk = 4 + count["m"] % 2
                        count["m"] += 1
                        if diag:
                            do("tensor", lambda e: e.matmul(
                                bank[bk][:, w_ - P:w_], identb[:, :], cmask[:, :], start=True, stop=True), st["grp", c, g], free.get(bk), sig=False)
                        t = do("tensor", lambda e: e.matmul(
                            bank[bk][:, 0:w_], qa[slot(c, g)][0:KS, h, i * P:(i + 1) * P], ka[slot(c, g)][0:KS, h, kc * NH:kc * NH + w_],
                            start=not diag, stop=True, skip_group_check=True), st["grp", c, g], free.get(bk))
                        free[bk] = st["mx"] = do("vector", lambda e: e.tensor_reduce(
                            nm[g % 2][:, h, i, kc:kc + 1], bank[bk][:, 0:w_], AX_X, ALU.max, negate=True), t, st["nm", g % 2])

                    def end():
                        t = do("vector", lambda e: e.tensor_tensor(
                            nmf[g % 2].rearrange("p (h t) -> p h t", t=TH), nm[g % 2][:, :, :, 0], nm[g % 2][:, :, :, 1], ALU.min),
                            st["mx"], st.get(("nmT", g % 2)))
                        st["nmf", g % 2] = t
                        t = do("vector", lambda e: e.tensor_copy(nms[g % 2][:, :, 0], nmf[g % 2]), t, st.get(("nmT", g % 2)))
                        t1 = do("vector", lambda e: e.tensor_tensor(nms[g % 2][:, :, 1], nmf[g % 2], nms[g % 2][:, :, 0], ALU.subtract), t)
                        st["nms", g % 2] = t1

                    def row(h):
                        for i in range(TH):
                            t = do("tensor", lambda e, i=i: e.matmul(
                                bank[6][KS:KA, i * P:(i + 1) * P], nms[g % 2][:, TH * h + i, :], identb[:, :], start=True, stop=True),
                                st["nms", g % 2], free.get(6), sig=i == TH - 1)
                        st["nmT", g % 2] = t
                        st["max", c, g, h] = free[6] = copy(pl, h % 2, qa[slot(c, g)][KS:KA, h], bank[6][KS:KA, :], t, st["grp", c, g])

                    units = [lambda h=h, i=i, kc=kc: unit(h, i, kc) for h in range(G1) for i in range(TH) for kc in range(c + 1)]
                    return begin, units, end, [lambda h=h: row(h) for h in range(G1)]

                def attend(c, g, kt_, maxima, behind):
                    q0 = max(kt_ * P - c * NH, 0)
                    w_ = NH - q0
                    pairs = []
                    for pr in range(2):
                        sl = count["p"] % 4
                        count["p"] += 1
                        for j in range(2):
                            h, bk = 2 * pr + j, count["s"] % 3
                            count["s"] += 1
                            t = do("tensor", lambda e, h=h, bk=bk: e.matmul(
                                bank[bk][:, 0:w_], ka[slot(c, g)][0:KA, h, kt_ * P:(kt_ + 1) * P], qa[slot(c, g)][0:KA, h, q0:NH],
                                start=True, stop=True), st["max", c, g, h], st["one"], free.get(bk))
                            t = free[bk] = do("scalar", lambda e, j=j, sl=sl, bk=bk: e.activation(
                                pp[sl][:, j, 0:w_], bank[bk][:, 0:w_], ACT.Exp), t, st.get(("pp", sl)), *st["z_attn"])
                            for u_ in maxima[h::G1]:
                                u_()
                        if kt_ >= TH * c:
                            t = do("gpsimd", lambda e, sl=sl: e.affine_select(
                                out=pp[sl][:, :, 0:P], in_=pp[sl][:, :, 0:P], pattern=[[0, 2], [1, P]], compare_op=ALU.is_ge,
                                fill=0.0, base=0, channel_multiplier=-1), t)
                        pairs.append((sl, t))
                        if behind and pr == 0:
                            behind()
                    return lambda: times_v(c, g, kt_, q0, w_, pairs)

                def times_v(c, g, kt_, q0, w_, pairs):
                    for h in range(G1):
                        sl, t = pairs[h // 2]
                        st["pp", sl] = t = do("tensor", lambda e, h=h, sl=sl: e.matmul(
                            bank[3][32 * h:32 * h + HD1 + 1, q0:NH], v1[:, kt_, G1 * g + h, :], pp[sl][:, h % 2, 0:w_],
                            start=kt_ == 0, stop=kt_ >= TH * c, skip_group_check=True), t, free.get(3), st["v", c])
                    if kt_ == TH * (c + 1) - 1:
                        st["pvdone", g] = t

                def normalize(c, g):
                    sl = count["o"] % 2
                    count["o"] += 1
                    t = free[3] = do("scalar", lambda e, sl=sl: e.activation(og[sl], bank[3], ACT.Copy), st["pvdone", g], st.get(("og", sl)), st.get("ocTr"), *st["z_attn"])
                    for i in range(TH):
                        t2 = do("tensor", lambda e, i=i, sl=sl: e.transpose(bank[6][:, i * P:(i + 1) * P], og[sl][:, i * P:(i + 1) * P], ident[:, :]),
                                t, free.get(6), sig=i == TH - 1)
                    st["og", sl] = t2
                    ov = bank[6].rearrange("p (t h d) -> p t h d", h=G1, d=2 * HD1)
                    rc = small[:, 16 * sl:16 * sl + 16].rearrange("p (t h) -> p t h", h=G1)
                    t = do("vector", lambda e: e.reciprocal(rc, ov[:, :, :, HD1]), t2, st.get(("rc", sl)))
                    free[6] = st["rc", sl] = st["oc"] = do("vector", lambda e: e.tensor_tensor(
                        oc[:, :, g * G1 * HD1:(g + 1) * G1 * HD1].rearrange("p t (h d) -> p t h d", d=HD1),
                        ov[:, :, :, 0:HD1], rc.unsqueeze(3).broadcast_to([P, TH, G1, HD1]), ALU.mult), t, st.get("ocT"))

                def attention1(c):
                    if c == 0:
                        yield from until(("landing", 0, 0))
                        side["banks"] = [7]
                        st["z_attn"] = z = st["light", 1]
                        pair_of_ones = float(np.array(0x3F803F80, np.uint32).view(np.float32))
                        for ones in (at(arena, 3 * G1 * NH // 2, [G1 * N])[KS:KA], hTf[KS:KA, 0:G1 * N // 2]):
                            st["one"] = pl.partial = do("gpsimd", lambda e, ones=ones: e.memset(ones, pair_of_ones), *z, last("gpsimd"))
                        free[3] = do("vector", lambda e: e.memset(bank[3], 0.0), last("vector"), free.get(3))
                        pace["first"] = PACE[u][2]
                    else:
                        side["banks"] = [7, 0, 1]
                        yield from until(("projected", 1))
                        side["banks"] = [7]
                        pace["first"] = PACE[u][3]
                    for g in range(3):
                        if g == 2:
                            yield from until(("landing", c, 1))
                        if c == 0 or g > 0:
                            load_group(c, g, *st["z_attn"], st.get(("gdone", NG * c + g - 3)))
                    begin, units, end, rows_ = max_units(c, 0)
                    begin()
                    for u_ in units:
                        u_()
                        yield
                    end()
                    for f in rows_:
                        f()
                        yield
                    for g in range(NG):
                        nxt, end, rows_ = [], None, []
                        if g + 1 < NG:
                            begin, nxt, end, rows_ = max_units(c, g + 1)
                            begin()
                        behind = None
                        steps = TH * (c + 1)
                        per = -(-len(nxt) // (steps - 1))
                        for kt_ in range(steps):
                            behind = attend(c, g, kt_, nxt[per * kt_:per * kt_ + per] if kt_ < steps - 1 else rows_, behind)
                            if kt_ == steps - 2 and end:
                                end()
                            yield
                        behind()
                        yield
                        normalize(c, g)
                        st["gdone", NG * c + g] = last("tensor")
                        if g + 3 < NG:
                            load_group(c, g + 3, last("tensor"))
                        yield
                    for k in range(KD):
                        for i in range(TH):
                            t = do("tensor", lambda e, k=k, i=i: e.transpose(
                                bank[6][:, i * P:(i + 1) * P], oc[:, i, k * P:(k + 1) * P], ident[:, :]),
                                st["oc"], free.get(6), sig=i == TH - 1)
                        t_oc = free[6] = do("scalar", lambda e, k=k: e.activation(ocT[:, k], bank[6], ACT.Copy), t, st["og", 0], st["og", 1], st.get("ocTr"))
                        yield
                    st["ocT"] = t
                    for i in range(TH):
                        bk = 4 + i % 2
                        for k in range(KD):
                            t = do("tensor", lambda e, i=i, k=k, bk=bk: e.matmul(
                                bank[bk][:, 0:D], ocT[:, k, i * P:(i + 1) * P], wo1[:, k], start=k == 0, stop=k == KD - 1),
                                t_oc, free.get(bk), sig=k == KD - 1)
                        free[bk], st["x", TH * c + i] = add_gated(pl, xt, TH * c + i, bank[bk][:, 0:D], gates[:, 2], xadd2, t, st["bias1", c])
                        yield
                    st["ocTr"] = t
                    st["att", c] = True

                def mlp1(c, banks, burst):
                    yield from until(("att", c))
                    z = [*engines_now(), st["split", 1, 0], st["split", 1, 1]]
                    g1, xn2 = at(arena, ZONE_B, [FT, NH]), at(arena, ZONE_B + FT * NH, [TH, D])
                    yield from norm_half(c, 4, *[st["x", TH * c + i] for i in range(TH)], *z, st.get("n2m"), xn2=xn2)
                    st["n2m"] = st["n2", c]
                    t_b = add_bias(c, rows[:, R_B2:R_B2 + D], gates[:, 3], st["t_n"], st["gate3"])
                    for m_ in range(FT):
                        bk = banks[m_ % len(banks)]
                        for k in range(KD):
                            t = do("tensor", lambda e, m_=m_, k=k, bk=bk: e.matmul(
                                bank[bk], w1T[:, k, m_ * P:(m_ + 1) * P], hT2[:, k],
                                start=k == 0, stop=k == KD - 1), *st["hT2"], free.get(bk), sig=k == KD - 1)
                        if burst:
                            t_g = free[bk] = do("scalar", lambda e, m_=m_, bk=bk: e.activation(
                                g1[:, m_], bank[bk], ACT.Identity, bias=cols[:, C_FB1 + m_:C_FB1 + m_ + 1]), t, *z)
                        else:
                            t_g = free[bk] = do("scalar", lambda e, m_=m_, bk=bk: e.activation(
                                g1[:, m_], bank[bk], ACT.Gelu, bias=cols[:, C_FB1 + m_:C_FB1 + m_ + 1]), t, *z)
                        yield
                    if burst:
                        t_g = do("scalar", lambda e: e.activation(g1, g1, ACT.Gelu), t_g)
                        yield
                    for i in range(TH):
                        bk = banks[i % len(banks)]
                        for k in range(FT):
                            t = do("tensor", lambda e, i=i, k=k, bk=bk: e.matmul(
                                bank[bk][:, 0:D], g1[:, k, i * P:(i + 1) * P], w2T[:, k], start=k == 0, stop=k == FT - 1),
                                t_g, free.get(bk), sig=k == FT - 1)
                            if k % 4 == 3:
                                yield
                        free[bk], st["x", TH * c + i] = add_gated(pl, xt, TH * c + i, bank[bk][:, 0:D], gates[:, 3], xadd2, t, t_b, st["gate3"])
                    stored = dma("sync", f"out{c}", lambda e: e.dma_start(
                        out[bass.ds(b2 * 2 + u, 1), c * NH:(c + 1) * NH].rearrange("o (t p) d -> p (o t) d", p=P), xt[:, TH * c:TH * c + TH, :]),
                        st["x", TH * c + TH - 1])
                    if u == 0:
                        load_x(1, c, stored)

                return (chain(begin(), light_start(), light(0), light(1), attention1(0), attention1(1)),
                        chain(heavy(), mlp0(0), project1(0), mlp0(1), project1(1), mlp1(0, [7], True),
                              input_norm(u + 1), mlp1(1, [7, 5, 6] if u == 0 else [7, 0, 1, 2], False)))

            both = [streams(0), streams(1)]
            interleave(chain(both[0][0], both[1][0]), chain(both[0][1], both[1][1]), pace)
            pl.emit(nc)


def chain(*streams):
    for s in streams:
        yield from s


def interleave(first, second, pace):
    done, credit = [False, False], 0.0
    while not all(done):
        credit += pace["first"]
        while credit >= 1.0 and not done[0]:
            done[0] = next(first, "end") == "end"
            credit -= 1.0
        if done[0]:
            credit = 0.0
        if not done[1]:
            done[1] = next(second, "end") == "end"


def copy(pl, on_scalar, dst, src, *waits):
    if on_scalar:
        return pl.do("scalar", lambda e: e.activation(dst, src, ACT.Copy), *waits)
    return pl.do("vector", lambda e: e.tensor_copy(dst, src), *waits)


def affine(pl, on_vector, dst, src, scale, bias, *waits):
    if on_vector:
        return pl.do("vector", lambda e: e.tensor_scalar(dst, src, scale, bias, ALU.mult, ALU.add), *waits)
    return pl.do("scalar", lambda e: e.activation(dst, src, ACT.Identity, scale=scale, bias=bias), *waits)


def add_gated(pl, xt, i, psum, gate, tmp, ready, *x_ready):
    n = pl.count.get(id(tmp[0]), 0)
    pl.count[id(tmp[0])] = n + 1
    buf = tmp[n % len(tmp)]
    t1 = pl.do("vector", lambda e: e.tensor_tensor(buf, psum, gate, ALU.mult), ready, pl.kept.get((id(tmp[0]), n - len(tmp))), *x_ready)
    t2 = pl.do("gpsimd", lambda e: e.tensor_tensor(xt[:, i], xt[:, i], buf, ALU.add), t1, *x_ready)
    pl.kept[id(tmp[0]), n] = t2
    return t1, t2


def pl_last(pl, engine):
    n = pl.count.get(engine, 0)
    return (engine, n) if n else None


def norm_steps(pl, src, dst, small, c0, first, tiles, *ready):
    do = pl.do
    st = small[:, c0:c0 + 6 * tiles].rearrange("p (t s) -> p t s", s=6)
    mv = small[:, c0 + 6 * tiles:c0 + 8 * tiles].rearrange("p (t s) -> p t s", s=2)
    rs = small[:, c0 + 8 * tiles:c0 + 9 * tiles]
    ex = small[:, c0 + 9 * tiles:c0 + 10 * tiles]
    t_e = do("gpsimd", lambda e: e.memset(ex, -0.5), pl_last(pl, "gpsimd"))
    for i in range(tiles):
        do("vector", lambda e, i=i: e.bn_stats(st[:, i], src[:, first + i]), *ready)
        if i % 2:
            yield
    t = pl_last(pl, "vector")
    for i in range(tiles):
        t_a = do("vector", lambda e, i=i: e.bn_aggr(mv[:, i], st[:, i]), t)
    t = do("vector", lambda e: e.tensor_scalar(rs, mv[:, :, 1], 1e-5, None, ALU.add), t_a)
    t = do("gpsimd", lambda e: e.tensor_tensor(rs, rs, ex, ALU.pow), t, t_e)
    yield
    out = []
    for i in range(tiles):
        out.append(do("vector", lambda e, i=i: e.tensor_scalar(
            dst[:, i], src[:, first + i], mv[:, i, 0:1], rs[:, i:i + 1], ALU.subtract, ALU.mult), t))
        if i % 2:
            yield
    return out


def layer_norm(*args):
    steps = norm_steps(*args)
    while True:
        try:
            next(steps)
        except StopIteration as s:
            return s.value


def kernel(**inputs):
    import concourse.bacc as bacc
    from concourse.bass_utils import run_bass_kernel_spmd

    x = {k: np.asarray(v) for k, v in inputs.items()}
    p = lambda n: x["L0_attn_" + n]
    f, q, m = (lambda n: x["L0_ffn_" + n]), (lambda n: x["L1_attn_" + n]), (lambda n: x["L1_ffn_" + n])
    f32 = np.float32
    two = lambda v: v.reshape(2, P).T
    pair = lambda w: w.reshape(MU, INNER // 2, 2).transpose(2, 0, 1).reshape(P, INNER // 2)
    arrays = {
        "x": x["L0_attn_x"],
        "cT": np.stack([x[n].T.reshape(KD, P, B).transpose(1, 0, 2) for n in ("L0_c", "L1_c")], 1),
        "wmod0": x["L0_wmod"], "wmod1": x["L1_wmod"],
        "wqkv": p("light_qkv_w"), "wlo": p("light_out_w"), "whq": p("heavy_q_w"),
        "whk": p("heavy_kv_w")[:, :DH].transpose(2, 0, 1).reshape(D, HD),
        "whv": p("heavy_kv_w")[:, DH:].transpose(2, 0, 1).reshape(D, HD),
        "who": p("heavy_out_w"),
        "nullk": p("heavy_null_kv")[0].reshape(H0 // 2, P).T,
        "null_v": p("heavy_null_kv")[1].reshape(1, H0, DH),
        "win": np.concatenate([f("Win"), f("Win")], 1),
        "wfo": np.concatenate([f("Wout"), f("Wout")], 0),
        "wqk1": np.concatenate([q("Wq").T, q("Wk").T], 1), "wv1": q("Wv").T, "wo1": q("Wo").T,
        "w1": m("w1"), "w2": m("w2"),
        "cols": np.concatenate([two(p("ln_gamma")), two(p("ln_beta")), two(p("heavy_gamma")),
                                np.tile(f("bin_"), 2)[:, None], pair(f("W1")), pair(f("b1")), pair(f("W2")),
                                np.concatenate([f("b2"), np.zeros(MU, f32)])[:, None], m("b1").reshape(FT, P).T], 1),
        "toks": np.concatenate([p("q_route_tok"), p("kv_route_tok")])[None],
        "rows": np.concatenate([p("null_q_token"), f("bout"), q("bo"), m("b2"),
                                q("q_gamma"), q("q_beta"), q("k_gamma"), q("k_beta")])[None],
    }
    i = np.arange(P)
    c = np.arange(2 * P)
    band = (c[None] >= i[:, None]) & (c[None] - i[:, None] <= 2 * WIN)
    first, last = band & (c[None] >= WIN), band & (c[None] < 3 * WIN)
    pos = np.arange(N, dtype=f32)[:, None]
    th = pos * np.exp(-(np.arange(0, HD1, 2, dtype=f32) / f32(HD1)) * f32(math.log(10000.0))).astype(f32)
    sign1 = np.where(np.arange(HD1) < HD1 // 2, -1, 1).astype(f32)
    r1 = np.stack([np.repeat(np.cos(th), 2, 1), np.repeat(np.sin(th), 2, 1) * sign1])
    fr = pos * (f32(1.0) / f32(10000.0) ** (np.arange(0, DH, 2, dtype=f32) / f32(DH))).astype(f32)
    fr = np.concatenate([fr, fr], 1)
    sign0 = np.where(np.arange(DH) < DH // 2, -1, 1).astype(f32)
    arrays |= {
        "ident": np.eye(P, dtype=f32),
        "wmask": np.where(np.stack([first, band, last], 1), 0, NEG).astype(f32),
        "cmask": np.where(i[None] > i[:, None], NEG, 0).astype(f32),
        "rope1": r1.reshape(2, T, P, HD1).transpose(2, 0, 1, 3).astype(f32),
        "rope0": np.concatenate([np.cos(fr), np.sin(fr) * sign0], 1).astype(f32),
        "group": (i[:, None] // T == i[None] // T).astype(f32),
        "lower": ((i[:, None] // T == i[None] // T) & (i[:, None] < i[None])).astype(f32),
        "iota": np.arange(NQ, dtype=f32)[None],
        "tokv": (np.arange(T)[None] * P + i[:, None]).astype(f32),
        "rowoff": (np.arange(4 * B) // 4 * N).astype(f32)[None],
    }
    arrays = {n: np.ascontiguousarray(v) for n, v in arrays.items()}
    nc = bacc.Bacc("TRN2", target_bir_lowering=False, num_devices=1)
    aps = {n: nc.dram_tensor("in_" + n, v.shape, mybir.dt.from_np(v.dtype), kind="ExternalInput").ap() for n, v in arrays.items()}
    out = nc.dram_tensor("y", (B, N, D), F32, kind="ExternalOutput").ap()
    adaln_kernel(nc, aps, out)
    r = run_bass_kernel_spmd(nc, [{"in_" + n: v for n, v in arrays.items()}], core_ids=[0])
    return r.results[0]["y"]
```
